# Optimizing a Trainium2 kernel written in Bass

```python
import numpy as np
import jax
import jax.numpy as jnp

def _softmax(x, axis=-1):
    return jax.nn.softmax(x, axis=axis)

def _gelu(x):
    return jax.nn.gelu(x, approximate=True)

def _silu(x):
    return jax.nn.silu(x)

def _sigmoid(x):
    return jax.nn.sigmoid(x)

def _layernorm(x, axis=-1, eps=1e-05):
    m = jnp.mean(x, axis=axis, keepdims=True)
    v = jnp.var(x, axis=axis, keepdims=True)
    return (x - m) / jnp.sqrt(v + eps)

def _scatter_add(tgt, idx, src, axis=0):
    return tgt.at[idx].add(src)

def _segment_sum(src, seg, n):
    return jax.ops.segment_sum(src, seg, n)
kernel_name = 'mk_flamingo_gated_d4_seqx_r4_7b1bfe'

def setup_inputs(seed: int=0):
    np.random.seed(seed)
    _w = jnp.asarray

    def _rec_inputs():
        import jax
        import jax.numpy as jnp
        _rk = jax.random.key(seed)
        x = -0.0002928 + 1 * jax.random.normal(jax.random.fold_in(_rk, 1), (4, 512, 256), jnp.float32)
        _lenS = 512 - jax.random.randint(jax.random.fold_in(_rk, 7), (4,), 0, max(1, 512 // 4) + 1, jnp.int32)
        _lenS2 = 512 - jax.random.randint(jax.random.fold_in(_rk, 8), (4,), 0, max(1, 512 // 4) + 1, jnp.int32)
        _ctx_1024P = jax.random.normal(jax.random.fold_in(_rk, 11), (4, 16, 256), jnp.float32)
        _ctx_1024c = jax.random.dirichlet(jax.random.fold_in(_rk, 511), 0.3 * jnp.ones((16,), jnp.float32), (4, 512))
        _ctx_1024t = jnp.einsum('bsk,bkd->bsd', _ctx_1024c, _ctx_1024P)
        _ctx_1024t = _ctx_1024t * jax.lax.rsqrt(jnp.mean(jnp.square(_ctx_1024t)) + 1e-12) * 0.953939
        ctx_1024 = -1.39393e-06 + 0.999914 * (_ctx_1024t + 0.3 * jax.random.normal(jax.random.fold_in(_rk, 611), (4, 512, 256), jnp.float32))
        _validS = jnp.arange(512)[None, :] < _lenS[:, None]
        _validS2 = jnp.arange(512)[None, :] < _lenS2[:, None]
        _causal = jnp.tril(jnp.ones((512, 512), dtype=bool))
        mask_BxS2_if1 = jnp.where(jnp.ones((4, 512), dtype=bool), 1, 0).astype(jnp.int32)
        mask_BxS2_bk0 = jnp.logical_not(jnp.broadcast_to(_validS2[:, :], (4, 512)))
        _g = jax.random.normal(jax.random.fold_in(_rk, 9001), (2, 4), jnp.float32)
        _g = jnp.sign(_g) * jnp.maximum(jnp.abs(_g), 1.0) + (_g == 0) * 1.0
        g_xattn = _g[0]
        g_ffn = _g[1]
        return (x, ctx_1024, mask_BxS2_if1, mask_BxS2_bk0, g_xattn, g_ffn)
    x, ctx_1024, mask_BxS2_if1, mask_BxS2_bk0, g_xattn, g_ffn = _rec_inputs()

    def _L0_xattn_setup():
        import jax, jax.numpy as jnp
        import numpy as np
        import math
        B, S, D, H = (2, 512, 256, 16)
        DK = D // H

        def _split_heads(x):
            b, s, d = x.shape
            return x.reshape(b, s, H, DK).transpose(0, 2, 1, 3)
        key = jax.random.key(seed)
        ks = jax.random.split(key, 12)
        scale = 0.02
        return {'q': jax.random.normal(ks[0], (B, S, D), jnp.float32), 'k': jax.random.normal(ks[1], (B, S, D), jnp.float32), 'v': jax.random.normal(ks[2], (B, S, D), jnp.float32), 'mask': jnp.ones((B, S), jnp.int32), 'Wq': jax.random.normal(ks[3], (D, D), jnp.float32) * scale, 'bq': jnp.zeros((D,), jnp.float32), 'Wk': jax.random.normal(ks[4], (D, D), jnp.float32) * scale, 'bk': jnp.zeros((D,), jnp.float32), 'Wv': jax.random.normal(ks[5], (D, D), jnp.float32) * scale, 'bv': jnp.zeros((D,), jnp.float32), 'Wo': jax.random.normal(ks[6], (D, D), jnp.float32) * scale, 'bo': jnp.zeros((D,), jnp.float32)}
    _L0_xattn_all = _L0_xattn_setup()
    _L0_xattn_in = {k: v for k, v in _L0_xattn_all.items() if k in ('Wq', 'bq', 'Wk', 'bk', 'Wv', 'bv', 'Wo', 'bo')}
    del _L0_xattn_all

    def _L0_ffn_setup():
        import jax, jax.numpy as jnp
        import numpy as np
        NUM_EXPERTS = 64
        TOP_K = 8
        HIDDEN = 256
        INTER = 192
        BATCH, SEQ = (1, 256)
        CAPACITY = 64

        def _moe_forward(hidden_states, gate_w, w_gate, w_up, w_down):
            B, S, H = hidden_states.shape
            x = hidden_states.reshape(-1, H)
            T = x.shape[0]
            logits = (x @ gate_w.T).astype(jnp.float32)
            probs = jax.nn.softmax(logits, axis=-1)
            topk_p, topk_i = jax.lax.top_k(probs, TOP_K)
            topk_p = topk_p / jnp.sum(topk_p, axis=-1, keepdims=True)
            flat_e = topk_i.reshape(-1)
            onehot = jax.nn.one_hot(flat_e, NUM_EXPERTS, dtype=jnp.int32)
            pos_all = jnp.cumsum(onehot, axis=0) - 1
            pos = jnp.take_along_axis(pos_all, flat_e[:, None], axis=1)[:, 0]
            x_rep = jnp.repeat(x, TOP_K, axis=0)
            dispatch = jnp.zeros((NUM_EXPERTS, CAPACITY, H), x.dtype)
            dispatch = dispatch.at[flat_e, pos].set(x_rep, mode='drop')
            g = jax.nn.silu(jnp.einsum('ech,eih->eci', dispatch, w_gate))
            u = jnp.einsum('ech,eih->eci', dispatch, w_up)
            y = jnp.einsum('eci,ehi->ech', g * u, w_down)
            valid = pos < CAPACITY
            y_tok = y[flat_e, jnp.minimum(pos, CAPACITY - 1)]
            w = (topk_p.reshape(-1) * valid.astype(topk_p.dtype)).astype(x.dtype)
            out = (y_tok * w[:, None]).reshape(T, TOP_K, H).sum(axis=1)
            return out.reshape(B, S, H)
        key = jax.random.key(seed)
        k1, k2, k3, k4, k5 = jax.random.split(key, 5)
        scale = 0.02
        return {'hidden_states': jax.random.normal(k1, (BATCH, SEQ, HIDDEN), dtype=jnp.float32), 'gate_w': jax.random.normal(k2, (NUM_EXPERTS, HIDDEN), dtype=jnp.float32) * scale, 'w_gate': jax.random.normal(k3, (NUM_EXPERTS, INTER, HIDDEN), dtype=jnp.float32) * scale, 'w_up': jax.random.normal(k4, (NUM_EXPERTS, INTER, HIDDEN), dtype=jnp.float32) * scale, 'w_down': jax.random.normal(k5, (NUM_EXPERTS, HIDDEN, INTER), dtype=jnp.float32) * scale}
    _L0_ffn_all = _L0_ffn_setup()
    _L0_ffn_in = {k: v for k, v in _L0_ffn_all.items() if k in ('gate_w', 'w_gate', 'w_up', 'w_down')}
    del _L0_ffn_all

    def _L1_xattn_setup():
        import jax, jax.numpy as jnp
        import numpy as np
        import math
        EPS = 1e-08
        LN_EPS = 1e-05
        B, S, E, NH = (2, 512, 256, 4)
        DH = E // NH

        def _mlstm_cell(q, k, v, igate_w, igate_b, fgate_w, fgate_b, out_w):
            Bq, Sq, Eq = q.shape
            if_in = jnp.concatenate([q, k, v], axis=-1)
            ig = jnp.einsum('bsf,hf->bsh', if_in, igate_w) + igate_b
            fg = jnp.einsum('bsf,hf->bsh', if_in, fgate_w) + fgate_b
            ig = jnp.transpose(ig, (0, 2, 1))[..., None]
            fg = jnp.transpose(fg, (0, 2, 1))[..., None]
            qh = q.reshape(Bq, Sq, NH, DH).transpose(0, 2, 1, 3)
            kh = k.reshape(Bq, Sq, NH, DH).transpose(0, 2, 1, 3)
            vh = v.reshape(Bq, Sq, NH, DH).transpose(0, 2, 1, 3)
            log_fg = jax.nn.log_sigmoid(fg)
            cs = jnp.cumsum(log_fg, axis=2)
            cs_shift = jnp.concatenate([jnp.zeros_like(cs[:, :, :1]), cs[:, :, :-1]], axis=2)
            logfg_mat = cs - jnp.swapaxes(cs_shift, -2, -1)
            ltr = jnp.tril(jnp.ones((Sq, Sq), dtype=bool))
            logfg_mat = jnp.where(ltr, logfg_mat, -jnp.inf)
            log_D = logfg_mat + jnp.swapaxes(ig, -2, -1)
            max_log_D = jnp.max(log_D, axis=-1, keepdims=True)
            D = jnp.exp(log_D - max_log_D)
            qk = jnp.einsum('bhsd,bhtd->bhst', qh, kh / math.sqrt(DH))
            C = qk * D
            sum_C_abs = jnp.abs(jnp.sum(C, axis=-1, keepdims=True))
            normaliser = jnp.maximum(sum_C_abs, jnp.exp(-max_log_D))
            C_norm = C / (normaliser + EPS)
            h = jnp.einsum('bhst,bhtd->bhsd', C_norm, vh)
            mean = jnp.mean(h, axis=-1, keepdims=True)
            var = jnp.mean((h - mean) ** 2, axis=-1, keepdims=True)
            h_norm = (h - mean) / jnp.sqrt(var + LN_EPS)
            scale = (1.0 + out_w).reshape(1, NH, 1, DH)
            h_norm = h_norm * scale
            return h_norm.transpose(0, 2, 1, 3).reshape(Bq, Sq, Eq)
        key = jax.random.key(seed)
        ks = jax.random.split(key, 7)
        std_g = math.sqrt(2.0 / (5.0 * 3 * E))
        return {'q': jax.random.normal(ks[0], (B, S, E), dtype=jnp.float32), 'k': jax.random.normal(ks[1], (B, S, E), dtype=jnp.float32), 'v': jax.random.normal(ks[2], (B, S, E), dtype=jnp.float32), 'igate_w': jax.random.normal(ks[3], (NH, 3 * E), dtype=jnp.float32) * std_g, 'igate_b': jax.random.normal(ks[4], (NH,), dtype=jnp.float32) * 0.1, 'fgate_w': jax.random.normal(ks[5], (NH, 3 * E), dtype=jnp.float32) * std_g, 'fgate_b': jnp.linspace(3.4, 6.0, NH, dtype=jnp.float32), 'out_w': jnp.zeros((E,), dtype=jnp.float32)}
    _L1_xattn_all = _L1_xattn_setup()
    _L1_xattn_in = {k: v for k, v in _L1_xattn_all.items() if k in ('igate_w', 'igate_b', 'fgate_w', 'fgate_b', 'out_w')}
    del _L1_xattn_all

    def _L1_ffn_setup():
        import jax, jax.numpy as jnp
        import numpy as np
        CAPACITY_FACTOR = 0.5
        key = jax.random.key(seed)
        ks = jax.random.split(key, 5)
        B, S, D, F = (4, 1024, 256, 1024)
        scale_in = 1.0 / np.sqrt(D)
        scale_ff = 1.0 / np.sqrt(F)
        return {'hidden_states': jax.random.normal(ks[0], (B, S, D), dtype=jnp.float32), 'w_router': jax.random.normal(ks[1], (D,), dtype=jnp.float32) * scale_in, 'W1': jax.random.normal(ks[2], (D, F), dtype=jnp.float32) * scale_in, 'b1': jnp.zeros((F,), dtype=jnp.float32), 'W2': jax.random.normal(ks[3], (F, D), dtype=jnp.float32) * scale_ff, 'b2': jnp.zeros((D,), dtype=jnp.float32)}
    _L1_ffn_all = _L1_ffn_setup()
    _L1_ffn_in = {k: v for k, v in _L1_ffn_all.items() if k in ('w_router', 'W1', 'b1', 'W2', 'b2')}
    del _L1_ffn_all

    def _L2_xattn_setup():
        import jax, jax.numpy as jnp
        import numpy as np
        DIM = 256
        CTX_DIM = 256
        HEADS = 16
        DIM_HEAD = 64
        INNER = HEADS * DIM_HEAD
        FF_INNER = 4 * DIM
        EPS = 1e-05

        def layer_norm(x, g, b):
            mu = jnp.mean(x, axis=-1, keepdims=True)
            var = jnp.var(x, axis=-1, keepdims=True)
            return (x - mu) * jax.lax.rsqrt(var + EPS) * g + b
        key = jax.random.key(seed)
        ks = jax.random.split(key, 9)
        b, n, j = (4, 512, 256)
        inp = {'x': jax.random.normal(ks[0], (b, n, DIM), dtype=jnp.float32), 'context': jax.random.normal(ks[1], (b, j, CTX_DIM), dtype=jnp.float32), 'ln_g': jnp.ones((DIM,), jnp.float32), 'ln_b': jnp.zeros((DIM,), jnp.float32), 'cln_g': jnp.ones((CTX_DIM,), jnp.float32), 'cln_b': jnp.zeros((CTX_DIM,), jnp.float32), 'Wq': jax.random.normal(ks[2], (DIM, INNER), dtype=jnp.float32) * DIM ** (-0.5), 'Wkv': jax.random.normal(ks[3], (CTX_DIM, 2 * DIM_HEAD), dtype=jnp.float32) * CTX_DIM ** (-0.5), 'Wo': jax.random.normal(ks[4], (INNER, DIM), dtype=jnp.float32) * INNER ** (-0.5), 'Wff1': jax.random.normal(ks[5], (DIM, 2 * FF_INNER), dtype=jnp.float32) * DIM ** (-0.5), 'Wff2': jax.random.normal(ks[6], (FF_INNER, DIM), dtype=jnp.float32) * FF_INNER ** (-0.5)}
        return inp
    _L2_xattn_all = _L2_xattn_setup()
    _L2_xattn_in = {k: v for k, v in _L2_xattn_all.items() if k in ('ln_g', 'ln_b', 'cln_g', 'cln_b', 'Wq', 'Wkv', 'Wo', 'Wff1', 'Wff2')}
    del _L2_xattn_all

    def _L2_ffn_setup():
        import jax, jax.numpy as jnp
        import numpy as np
        B, S, H = (8, 1024, 256)
        NAV = 128
        E = 8
        F = 2 * H
        key = jax.random.key(seed)
        ks = jax.random.split(key, 12)

        def w(k, shape, fan_in):
            return jax.random.normal(k, shape, dtype=jnp.float32) / np.sqrt(fan_in)
        return {'hidden_states': jax.random.normal(ks[0], (B, S, H), dtype=jnp.float32), 'Wp1': w(ks[1], (H, NAV), H), 'bp1': jnp.zeros((NAV,), jnp.float32), 'Wp2': w(ks[2], (NAV, E), NAV), 'bp2': jnp.zeros((E,), jnp.float32), 'W1': w(ks[3], (E, H, F), H), 'b1': jnp.zeros((E, F), jnp.float32), 'W2': w(ks[4], (E, F, H), F), 'b2': jnp.zeros((E, H), jnp.float32), 'Wo': w(ks[5], (H, H), H), 'bo': jnp.zeros((H,), jnp.float32)}
    _L2_ffn_all = _L2_ffn_setup()
    _L2_ffn_in = {k: v for k, v in _L2_ffn_all.items() if k in ('Wp1', 'bp1', 'Wp2', 'bp2', 'W1', 'b1', 'W2', 'b2', 'Wo', 'bo')}
    del _L2_ffn_all

    def _L3_xattn_setup():
        import jax, jax.numpy as jnp
        import numpy as np
        EPS = 1e-05

        def layer_norm(x, g, b):
            mu = jnp.mean(x, axis=-1, keepdims=True)
            var = jnp.mean((x - mu) ** 2, axis=-1, keepdims=True)
            return (x - mu) * jax.lax.rsqrt(var + EPS) * g + b
        key = jax.random.key(seed)
        ks = jax.random.split(key, 8)
        b, n, l, D = (8, 1024, 64, 256)
        heads, dim_head = (16, 64)
        inner = heads * dim_head
        x = jax.random.normal(ks[0], (b, n, D), dtype=jnp.float32)
        latents = jax.random.normal(ks[1], (b, l, D), dtype=jnp.float32)
        mask = jax.random.randint(ks[2], (b, n), 0, 2) > 0
        Wq = jax.random.normal(ks[3], (D, inner), dtype=jnp.float32) * D ** (-0.5)
        Wkv = jax.random.normal(ks[4], (D, 2 * inner), dtype=jnp.float32) * D ** (-0.5)
        Wout = jax.random.normal(ks[5], (inner, D), dtype=jnp.float32) * inner ** (-0.5)
        g1 = jnp.ones((D,), jnp.float32)
        b1 = jnp.zeros((D,), jnp.float32)
        g2 = jnp.ones((D,), jnp.float32)
        b2 = jnp.zeros((D,), jnp.float32)
        return {'x': x, 'latents': latents, 'mask': mask, 'g1': g1, 'b1': b1, 'g2': g2, 'b2': b2, 'Wq': Wq, 'Wkv': Wkv, 'Wout': Wout}
    _L3_xattn_all = _L3_xattn_setup()
    _L3_xattn_in = {k: v for k, v in _L3_xattn_all.items() if k in ('g1', 'b1', 'g2', 'b2', 'Wq', 'Wkv', 'Wout')}
    del _L3_xattn_all

    def _L3_ffn_setup():
        import jax, jax.numpy as jnp
        import numpy as np
        QMAX = 127.0
        EPS = 1e-08

        def _quantize_per_token(x):
            amax = jnp.clip(jnp.max(jnp.abs(x), axis=-1, keepdims=True), EPS, None)
            scale = amax / QMAX
            x_q = jnp.clip(jnp.round(x / scale), -128, 127)
            return (x_q, scale)

        def _quantize_per_channel(w):
            amax = jnp.clip(jnp.max(jnp.abs(w), axis=-1, keepdims=True), EPS, None)
            scale = amax / QMAX
            w_q = jnp.clip(jnp.round(w / scale), -128, 127)
            return (w_q, scale)
        key = jax.random.key(seed)
        k1, k2, k3 = jax.random.split(key, 3)
        B, S, DIN, DOUT = (8, 1024, 256, 256)
        x = jax.random.normal(k1, (B, S, DIN), dtype=jnp.float32)
        weight = jax.random.normal(k2, (DOUT, DIN), dtype=jnp.float32) * 0.02
        bias = jax.random.normal(k3, (DOUT,), dtype=jnp.float32)
        return {'x': x, 'weight': weight, 'bias': bias}
    _L3_ffn_all = _L3_ffn_setup()
    _L3_ffn_in = {k: v for k, v in _L3_ffn_all.items() if k in ('weight', 'bias')}
    del _L3_ffn_all
    return {'x': x, 'ctx_1024': ctx_1024, 'mask_BxS2_if1': mask_BxS2_if1, 'mask_BxS2_bk0': mask_BxS2_bk0, 'g_xattn': g_xattn, 'g_ffn': g_ffn, 'L0_xattn_Wq': _L0_xattn_in['Wq'], 'L0_xattn_bq': _L0_xattn_in['bq'], 'L0_xattn_Wk': _L0_xattn_in['Wk'], 'L0_xattn_bk': _L0_xattn_in['bk'], 'L0_xattn_Wv': _L0_xattn_in['Wv'], 'L0_xattn_bv': _L0_xattn_in['bv'], 'L0_xattn_Wo': _L0_xattn_in['Wo'], 'L0_xattn_bo': _L0_xattn_in['bo'], 'L0_ffn_gate_w': _L0_ffn_in['gate_w'], 'L0_ffn_w_gate': _L0_ffn_in['w_gate'], 'L0_ffn_w_up': _L0_ffn_in['w_up'], 'L0_ffn_w_down': _L0_ffn_in['w_down'], 'L1_xattn_igate_w': _L1_xattn_in['igate_w'], 'L1_xattn_igate_b': _L1_xattn_in['igate_b'], 'L1_xattn_fgate_w': _L1_xattn_in['fgate_w'], 'L1_xattn_fgate_b': _L1_xattn_in['fgate_b'], 'L1_xattn_out_w': _L1_xattn_in['out_w'], 'L1_ffn_w_router': _L1_ffn_in['w_router'], 'L1_ffn_W1': _L1_ffn_in['W1'], 'L1_ffn_b1': _L1_ffn_in['b1'], 'L1_ffn_W2': _L1_ffn_in['W2'], 'L1_ffn_b2': _L1_ffn_in['b2'], 'L2_xattn_ln_g': _L2_xattn_in['ln_g'], 'L2_xattn_ln_b': _L2_xattn_in['ln_b'], 'L2_xattn_cln_g': _L2_xattn_in['cln_g'], 'L2_xattn_cln_b': _L2_xattn_in['cln_b'], 'L2_xattn_Wq': _L2_xattn_in['Wq'], 'L2_xattn_Wkv': _L2_xattn_in['Wkv'], 'L2_xattn_Wo': _L2_xattn_in['Wo'], 'L2_xattn_Wff1': _L2_xattn_in['Wff1'], 'L2_xattn_Wff2': _L2_xattn_in['Wff2'], 'L2_ffn_Wp1': _L2_ffn_in['Wp1'], 'L2_ffn_bp1': _L2_ffn_in['bp1'], 'L2_ffn_Wp2': _L2_ffn_in['Wp2'], 'L2_ffn_bp2': _L2_ffn_in['bp2'], 'L2_ffn_W1': _L2_ffn_in['W1'], 'L2_ffn_b1': _L2_ffn_in['b1'], 'L2_ffn_W2': _L2_ffn_in['W2'], 'L2_ffn_b2': _L2_ffn_in['b2'], 'L2_ffn_Wo': _L2_ffn_in['Wo'], 'L2_ffn_bo': _L2_ffn_in['bo'], 'L3_xattn_g1': _L3_xattn_in['g1'], 'L3_xattn_b1': _L3_xattn_in['b1'], 'L3_xattn_g2': _L3_xattn_in['g2'], 'L3_xattn_b2': _L3_xattn_in['b2'], 'L3_xattn_Wq': _L3_xattn_in['Wq'], 'L3_xattn_Wkv': _L3_xattn_in['Wkv'], 'L3_xattn_Wout': _L3_xattn_in['Wout'], 'L3_ffn_weight': _L3_ffn_in['weight'], 'L3_ffn_bias': _L3_ffn_in['bias']}

def reference(x, ctx_1024, mask_BxS2_if1, mask_BxS2_bk0, g_xattn, g_ffn, L0_xattn_Wq, L0_xattn_bq, L0_xattn_Wk, L0_xattn_bk, L0_xattn_Wv, L0_xattn_bv, L0_xattn_Wo, L0_xattn_bo, L0_ffn_gate_w, L0_ffn_w_gate, L0_ffn_w_up, L0_ffn_w_down, L1_xattn_igate_w, L1_xattn_igate_b, L1_xattn_fgate_w, L1_xattn_fgate_b, L1_xattn_out_w, L1_ffn_w_router, L1_ffn_W1, L1_ffn_b1, L1_ffn_W2, L1_ffn_b2, L2_xattn_ln_g, L2_xattn_ln_b, L2_xattn_cln_g, L2_xattn_cln_b, L2_xattn_Wq, L2_xattn_Wkv, L2_xattn_Wo, L2_xattn_Wff1, L2_xattn_Wff2, L2_ffn_Wp1, L2_ffn_bp1, L2_ffn_Wp2, L2_ffn_bp2, L2_ffn_W1, L2_ffn_b1, L2_ffn_W2, L2_ffn_b2, L2_ffn_Wo, L2_ffn_bo, L3_xattn_g1, L3_xattn_b1, L3_xattn_g2, L3_xattn_b2, L3_xattn_Wq, L3_xattn_Wkv, L3_xattn_Wout, L3_ffn_weight, L3_ffn_bias):
    import jax
    import jax.numpy as jnp

    def _L0_xattn_ref(q, k, v, mask, Wq, bq, Wk, bk, Wv, bv, Wo, bo):
        import jax, jax.numpy as jnp
        import numpy as np
        import math
        B, S, D, H = (2, 512, 256, 16)
        DK = D // H

        def _split_heads(x):
            b, s, d = x.shape
            return x.reshape(b, s, H, DK).transpose(0, 2, 1, 3)
        Q = _split_heads(q @ Wq.T + bq)
        K = _split_heads(k @ Wk.T + bk)
        V = _split_heads(v @ Wv.T + bv)
        scores = jnp.einsum('bhqd,bhkd->bhqk', Q, K) / math.sqrt(DK)
        m = mask[:, None, None, :]
        scores = jnp.where(m == 0, jnp.float32(-1000000000.0), scores)
        attn = jax.nn.softmax(scores, axis=-1)
        out = jnp.einsum('bhqk,bhkd->bhqd', attn, V)
        out = out.transpose(0, 2, 1, 3).reshape(q.shape[0], q.shape[1], D)
        return out @ Wo.T + bo

    def _L0_ffn_ref(hidden_states, gate_w, w_gate, w_up, w_down):
        import jax, jax.numpy as jnp
        import numpy as np
        NUM_EXPERTS = 64
        TOP_K = 8
        HIDDEN = 256
        INTER = 192
        BATCH, SEQ = (1, 256)
        CAPACITY = 64

        def _moe_forward(hidden_states, gate_w, w_gate, w_up, w_down):
            B, S, H = hidden_states.shape
            x = hidden_states.reshape(-1, H)
            T = x.shape[0]
            logits = (x @ gate_w.T).astype(jnp.float32)
            probs = jax.nn.softmax(logits, axis=-1)
            topk_p, topk_i = jax.lax.top_k(probs, TOP_K)
            topk_p = topk_p / jnp.sum(topk_p, axis=-1, keepdims=True)
            flat_e = topk_i.reshape(-1)
            onehot = jax.nn.one_hot(flat_e, NUM_EXPERTS, dtype=jnp.int32)
            pos_all = jnp.cumsum(onehot, axis=0) - 1
            pos = jnp.take_along_axis(pos_all, flat_e[:, None], axis=1)[:, 0]
            x_rep = jnp.repeat(x, TOP_K, axis=0)
            dispatch = jnp.zeros((NUM_EXPERTS, CAPACITY, H), x.dtype)
            dispatch = dispatch.at[flat_e, pos].set(x_rep, mode='drop')
            g = jax.nn.silu(jnp.einsum('ech,eih->eci', dispatch, w_gate))
            u = jnp.einsum('ech,eih->eci', dispatch, w_up)
            y = jnp.einsum('eci,ehi->ech', g * u, w_down)
            valid = pos < CAPACITY
            y_tok = y[flat_e, jnp.minimum(pos, CAPACITY - 1)]
            w = (topk_p.reshape(-1) * valid.astype(topk_p.dtype)).astype(x.dtype)
            out = (y_tok * w[:, None]).reshape(T, TOP_K, H).sum(axis=1)
            return out.reshape(B, S, H)
        return _moe_forward(hidden_states, gate_w, w_gate, w_up, w_down)

    def _L1_xattn_ref(q, k, v, igate_w, igate_b, fgate_w, fgate_b, out_w):
        import jax, jax.numpy as jnp
        import numpy as np
        import math
        EPS = 1e-08
        LN_EPS = 1e-05
        B, S, E, NH = (2, 512, 256, 4)
        DH = E // NH

        def _mlstm_cell(q, k, v, igate_w, igate_b, fgate_w, fgate_b, out_w):
            Bq, Sq, Eq = q.shape
            if_in = jnp.concatenate([q, k, v], axis=-1)
            ig = jnp.einsum('bsf,hf->bsh', if_in, igate_w) + igate_b
            fg = jnp.einsum('bsf,hf->bsh', if_in, fgate_w) + fgate_b
            ig = jnp.transpose(ig, (0, 2, 1))[..., None]
            fg = jnp.transpose(fg, (0, 2, 1))[..., None]
            qh = q.reshape(Bq, Sq, NH, DH).transpose(0, 2, 1, 3)
            kh = k.reshape(Bq, Sq, NH, DH).transpose(0, 2, 1, 3)
            vh = v.reshape(Bq, Sq, NH, DH).transpose(0, 2, 1, 3)
            log_fg = jax.nn.log_sigmoid(fg)
            cs = jnp.cumsum(log_fg, axis=2)
            cs_shift = jnp.concatenate([jnp.zeros_like(cs[:, :, :1]), cs[:, :, :-1]], axis=2)
            logfg_mat = cs - jnp.swapaxes(cs_shift, -2, -1)
            ltr = jnp.tril(jnp.ones((Sq, Sq), dtype=bool))
            logfg_mat = jnp.where(ltr, logfg_mat, -jnp.inf)
            log_D = logfg_mat + jnp.swapaxes(ig, -2, -1)
            max_log_D = jnp.max(log_D, axis=-1, keepdims=True)
            D = jnp.exp(log_D - max_log_D)
            qk = jnp.einsum('bhsd,bhtd->bhst', qh, kh / math.sqrt(DH))
            C = qk * D
            sum_C_abs = jnp.abs(jnp.sum(C, axis=-1, keepdims=True))
            normaliser = jnp.maximum(sum_C_abs, jnp.exp(-max_log_D))
            C_norm = C / (normaliser + EPS)
            h = jnp.einsum('bhst,bhtd->bhsd', C_norm, vh)
            mean = jnp.mean(h, axis=-1, keepdims=True)
            var = jnp.mean((h - mean) ** 2, axis=-1, keepdims=True)
            h_norm = (h - mean) / jnp.sqrt(var + LN_EPS)
            scale = (1.0 + out_w).reshape(1, NH, 1, DH)
            h_norm = h_norm * scale
            return h_norm.transpose(0, 2, 1, 3).reshape(Bq, Sq, Eq)
        return _mlstm_cell(q, k, v, igate_w, igate_b, fgate_w, fgate_b, out_w)

    def _L1_ffn_ref(hidden_states, w_router, W1, b1, W2, b2):
        import jax, jax.numpy as jnp
        import numpy as np
        CAPACITY_FACTOR = 0.5
        'Mixture-of-Depths block: route top-k tokens through an FFN inner block,\n            scatter back with sigmoid router weights; bypassed tokens pass through.'
        B, S, D = hidden_states.shape
        k = int(S * CAPACITY_FACTOR)
        scores = jnp.einsum('bsd,d->bs', hidden_states, w_router)
        top_scores, top_idx = jax.lax.top_k(scores, k)
        weights = jax.nn.sigmoid(top_scores)
        selected = jnp.take_along_axis(hidden_states, top_idx[:, :, None], axis=1)
        h = jax.nn.gelu(jnp.einsum('bkd,df->bkf', selected, W1) + b1)
        processed = jnp.einsum('bkf,fd->bkd', h, W2) + b2
        update = weights[:, :, None] * processed

        def scatter_one(xb, ib, ub):
            return xb.at[ib].add(ub)
        output = jax.vmap(scatter_one)(hidden_states, top_idx, update)
        return output

    def _L2_xattn_ref(x, context, ln_g, ln_b, cln_g, cln_b, Wq, Wkv, Wo, Wff1, Wff2):
        import jax, jax.numpy as jnp
        import numpy as np
        DIM = 256
        CTX_DIM = 256
        HEADS = 16
        DIM_HEAD = 64
        INNER = HEADS * DIM_HEAD
        FF_INNER = 4 * DIM
        EPS = 1e-05

        def layer_norm(x, g, b):
            mu = jnp.mean(x, axis=-1, keepdims=True)
            var = jnp.var(x, axis=-1, keepdims=True)
            return (x - mu) * jax.lax.rsqrt(var + EPS) * g + b
        scale = DIM_HEAD ** (-0.5)
        xn = layer_norm(x, ln_g, ln_b)
        cn = layer_norm(context, cln_g, cln_b)
        b, n, _ = xn.shape
        q = (xn @ Wq).reshape(b, n, HEADS, DIM_HEAD).transpose(0, 2, 1, 3) * scale
        kv = cn @ Wkv
        k, v = (kv[..., :DIM_HEAD], kv[..., DIM_HEAD:])
        sim = jnp.einsum('bhid,bjd->bhij', q, k)
        attn = jax.nn.softmax(sim, axis=-1)
        out = jnp.einsum('bhij,bjd->bhid', attn, v)
        out = out.transpose(0, 2, 1, 3).reshape(b, n, INNER) @ Wo
        ff = xn @ Wff1
        h, gate = (ff[..., :FF_INNER], ff[..., FF_INNER:])
        out = out + jax.nn.silu(gate) * h @ Wff2
        return out

    def _L2_ffn_ref(hidden_states, Wp1, bp1, Wp2, bp2, W1, b1, W2, b2, Wo, bo):
        import jax, jax.numpy as jnp
        import numpy as np
        B, S, H = (8, 1024, 256)
        NAV = 128
        E = 8
        F = 2 * H
        last = hidden_states[:, -1, :]
        logits = jax.nn.gelu(last @ Wp1 + bp1, approximate=False) @ Wp2 + bp2
        action_probs = jax.nn.softmax(logits, axis=-1)
        sel = jnp.argmax(action_probs, axis=-1)
        w1 = W1[sel]
        w2 = W2[sel]
        h = jax.nn.gelu(jnp.einsum('bsh,bhf->bsf', hidden_states, w1) + b1[sel][:, None, :], approximate=False)
        reasoned = jnp.einsum('bsf,bfh->bsh', h, w2) + b2[sel][:, None, :]
        out = reasoned @ Wo + bo
        return hidden_states + 0.3 * out

    def _L3_xattn_ref(x, latents, mask, g1, b1, g2, b2, Wq, Wkv, Wout):
        import jax, jax.numpy as jnp
        import numpy as np
        EPS = 1e-05

        def layer_norm(x, g, b):
            mu = jnp.mean(x, axis=-1, keepdims=True)
            var = jnp.mean((x - mu) ** 2, axis=-1, keepdims=True)
            return (x - mu) * jax.lax.rsqrt(var + EPS) * g + b
        heads, dim_head = (16, 64)
        b, n, D = x.shape
        l = latents.shape[1]
        xn = layer_norm(x, g1, b1)
        ln_lat = layer_norm(latents, g2, b2)
        q = ln_lat @ Wq
        kv = jnp.concatenate([xn, ln_lat], axis=1) @ Wkv
        k, v = jnp.split(kv, 2, axis=-1)

        def to_heads(t):
            return t.reshape(t.shape[0], t.shape[1], heads, dim_head).transpose(0, 2, 1, 3)
        q, k, v = (to_heads(q), to_heads(k), to_heads(v))
        scale = 1.0 / np.sqrt(np.sqrt(dim_head)).astype(np.float32)
        weight = jnp.einsum('bhld,bhnd->bhln', q * scale, k * scale)
        full_mask = jnp.concatenate([mask, jnp.ones((b, l), dtype=bool)], axis=1)
        neg = -jnp.finfo(weight.dtype).max
        weight = jnp.where(full_mask[:, None, None, :], weight, neg)
        weight = jax.nn.softmax(weight.astype(jnp.float32), axis=-1).astype(q.dtype)
        out = jnp.einsum('bhln,bhnd->bhld', weight, v)
        out = out.transpose(0, 2, 1, 3).reshape(b, l, heads * dim_head)
        return out @ Wout

    def _L3_ffn_ref(x, weight, bias):
        import jax, jax.numpy as jnp
        import numpy as np
        QMAX = 127.0
        EPS = 1e-08

        def _quantize_per_token(x):
            amax = jnp.clip(jnp.max(jnp.abs(x), axis=-1, keepdims=True), EPS, None)
            scale = amax / QMAX
            x_q = jnp.clip(jnp.round(x / scale), -128, 127)
            return (x_q, scale)

        def _quantize_per_channel(w):
            amax = jnp.clip(jnp.max(jnp.abs(w), axis=-1, keepdims=True), EPS, None)
            scale = amax / QMAX
            w_q = jnp.clip(jnp.round(w / scale), -128, 127)
            return (w_q, scale)
        B, S, DIN = x.shape
        w_q, w_scale = _quantize_per_channel(weight.astype(jnp.float32))
        x_flat = x.reshape(-1, DIN).astype(jnp.float32)
        x_q, x_scale = _quantize_per_token(x_flat)
        out = jnp.matmul(x_q, w_q.T) * x_scale * w_scale.T
        out = out.reshape(B, S, -1) + bias
        return out.astype(x.dtype)
    x = x + jnp.tanh(g_xattn[0]) * _L0_xattn_ref(_layernorm(x, axis=-1), ctx_1024, ctx_1024, mask_BxS2_if1, L0_xattn_Wq, L0_xattn_bq, L0_xattn_Wk, L0_xattn_bk, L0_xattn_Wv, L0_xattn_bv, L0_xattn_Wo, L0_xattn_bo)
    x = x + jnp.tanh(g_ffn[0]) * _L0_ffn_ref(_layernorm(x, axis=-1), L0_ffn_gate_w, L0_ffn_w_gate, L0_ffn_w_up, L0_ffn_w_down)
    x = x + jnp.tanh(g_xattn[1]) * _L1_xattn_ref(_layernorm(x, axis=-1), ctx_1024, ctx_1024, L1_xattn_igate_w, L1_xattn_igate_b, L1_xattn_fgate_w, L1_xattn_fgate_b, L1_xattn_out_w)
    x = x + jnp.tanh(g_ffn[1]) * _L1_ffn_ref(_layernorm(x, axis=-1), L1_ffn_w_router, L1_ffn_W1, L1_ffn_b1, L1_ffn_W2, L1_ffn_b2)
    x = x + jnp.tanh(g_xattn[2]) * _L2_xattn_ref(_layernorm(x, axis=-1), ctx_1024, L2_xattn_ln_g, L2_xattn_ln_b, L2_xattn_cln_g, L2_xattn_cln_b, L2_xattn_Wq, L2_xattn_Wkv, L2_xattn_Wo, L2_xattn_Wff1, L2_xattn_Wff2)
    x = x + jnp.tanh(g_ffn[2]) * _L2_ffn_ref(_layernorm(x, axis=-1), L2_ffn_Wp1, L2_ffn_bp1, L2_ffn_Wp2, L2_ffn_bp2, L2_ffn_W1, L2_ffn_b1, L2_ffn_W2, L2_ffn_b2, L2_ffn_Wo, L2_ffn_bo)
    x = x + jnp.tanh(g_xattn[3]) * _L3_xattn_ref(ctx_1024, _layernorm(x, axis=-1), mask_BxS2_bk0, L3_xattn_g1, L3_xattn_b1, L3_xattn_g2, L3_xattn_b2, L3_xattn_Wq, L3_xattn_Wkv, L3_xattn_Wout)
    x = x + jnp.tanh(g_ffn[3]) * _L3_ffn_ref(_layernorm(x, axis=-1), L3_ffn_weight, L3_ffn_bias)
    return x

_drawn_inputs = setup_inputs


def setup_inputs(seed=0):
    import zlib

    import numpy as np

    out = dict(_drawn_inputs(seed))
    spreads = {'L0_xattn_bq': (0.0, 0.8),
     'L0_xattn_bk': (0.0, 2.0),
     'L0_xattn_bv': (0.0, 0.275),
     'L0_xattn_bo': (0.0, 0.1),
     'L1_xattn_out_w': (0.0, 0.1),
     'L1_ffn_b1': (0.0, 0.569),
     'L1_ffn_b2': (0.0, 0.379),
     'L2_xattn_ln_g': (1.0, 0.2),
     'L2_xattn_ln_b': (0.0, 0.274),
     'L2_xattn_cln_g': (1.0, 0.6),
     'L2_xattn_cln_b': (0.0, 0.386),
     'L2_ffn_bp1': (0.0, 0.1),
     'L2_ffn_bp2': (0.0, 0.1),
     'L2_ffn_b1': (0.0, 0.8),
     'L2_ffn_b2': (0.0, 0.536),
     'L2_ffn_bo': (0.0, 0.509),
     'L3_xattn_g1': (1.0, 0.6),
     'L3_xattn_b1': (0.0, 0.8),
     'L3_xattn_g2': (1.0, 0.6),
     'L3_xattn_b2': (0.0, 0.307)}
    factors = {'L0_xattn_Wq': 8.0,
     'L0_xattn_Wk': 8.0,
     'L0_ffn_gate_w': 8.0,
     'L0_ffn_w_gate': 8.0,
     'L0_ffn_w_up': 8.0,
     'L0_ffn_w_down': 8.0,
     'L1_xattn_igate_b': 64.0,
     'g_ffn': 24.096,
     'L1_xattn_fgate_w': 2.972}
    for name, (base, spread) in spreads.items():
        noise = np.random.default_rng([zlib.crc32(name.encode()), seed]).standard_normal(out[name].shape)
        drawn = base * np.exp(spread * noise) if base else spread * noise
        out[name] = jnp.asarray(drawn.astype(out[name].dtype))
    for name, factor in factors.items():
        out[name] = (out[name] * factor).astype(out[name].dtype)
    return out
```

```python
from contextlib import ExitStack, contextmanager

import concourse.bass as bass
import numpy as np
from concourse import mybir

F32 = mybir.dt.float32
BF16 = mybir.dt.bfloat16
I32 = mybir.dt.int32
U32 = mybir.dt.uint32
ALU = mybir.AluOpType
ACT = mybir.ActivationFunctionType
AX = mybir.AxisListType

P = 128
B, S, D = 4, 512, 256
NT = S // P
DC = D // P
TOK = B * S
BANK = 512
LN_EPS = 1e-5

H0, DK0 = 16, 16
HPAD = 32
QUADS = H0 * HPAD // P
E, TOPK, CAP, INTER = 64, 8, 64, 192
PAIRS = E // 2
IH = INTER // 2
SLOTS = E * CAP
H1, DH1 = 4, 64
F1 = 1024
FC1 = F1 // P
KEEP = S // 2
H2, DH2 = 16, 64
INNER = H2 * DH2
HP = H2 // 2
FF2 = 4 * D
FFC = FF2 // P
NAV, E2, FE2 = 128, 8, 512
FEC = FE2 // P
KEYS3 = 2 * S
QMAX = 127.0
ROUND = 12582912.0
RSQRT_BITS, RSQRT_STEPS = 1597463007.0, 3
NEG1E9, FMAX = 1.0e9, float(np.finfo(np.float32).max)

mult, add, subtract = ALU.mult, ALU.add, ALU.subtract


class Chain:

    def __init__(self, eng, sem):
        self.eng, self.sem, self.n = eng, sem, 0

    def __call__(self, ins):
        self.n += 1
        ins.then_inc(self.sem, 1)
        self.eng.wait_ge(self.sem, self.n)


def layernorm(nc, link, src, dst, stats, tiles=NT):
    s6, mv, rstd, var, half = (x[:, 0:tiles] for x in stats)
    for t in range(tiles):
        last = nc.vector.bn_stats(s6[:, t, :], src[:, t, :])
    link(last)
    for t in range(tiles):
        last = nc.vector.bn_aggr(mv[:, t, :], s6[:, t, :])
    link(last)
    link(nc.vector.tensor_scalar(var, mv[:, :, 1], LN_EPS, None, add))
    link(nc.vector.tensor_scalar(rstd.bitcast(I32), var.bitcast(I32), -0.5, RSQRT_BITS, mult, add))
    for _ in range(RSQRT_STEPS):
        link(nc.vector.tensor_tensor(half, var, rstd, mult))
        link(nc.vector.scalar_tensor_tensor(out=half, in0=half, scalar=-0.5, in1=rstd, op0=mult, op1=mult))
        link(nc.vector.scalar_tensor_tensor(out=rstd, in0=half, scalar=1.5, in1=rstd, op0=add, op1=mult))
    for t in range(tiles):
        last = nc.vector.tensor_scalar(dst[:, t, :], src[:, t, :], mv[:, t, 0:1], rstd[:, t:t + 1],
                                       subtract, mult)
    return last


def attention(nc, sem, name, ps, ident, heads, groups, nk, q_of, k_of, v_of, rows, mask, bufs, out,
              prep=None, jobs=None):
    banks = nk // 4
    ring = 4 // banks
    probs, sums, recip, least, pt = bufs
    np_ = len(probs)
    per = NT * heads
    steps = groups * per
    scores_ready = sem(name + "_scores_ready")
    least_ready = sem(name + "_least_ready")
    exp_ready = sem(name + "_exp_ready")
    probs_ready = sem(name + "_probs_ready")
    turned = sem(name + "_turned")
    turned_kept = sem(name + "_turned_kept")
    av_ready = sem(name + "_av_ready")
    av_kept = sem(name + "_av_kept")
    recip_ready = sem(name + "_recip_ready")
    jobs_ready = sem(name + "_jobs_ready")
    jobs_kept = sem(name + "_jobs_kept")

    def where(n):
        g, r = divmod(n, per)
        return g, r // heads, r % heads

    def scores(n):
        return ps[:, (n % ring) * banks:(n % ring + 1) * banks, :].rearrange("p b k -> p (b k)")

    before = {}
    first_jobs = []
    if jobs:
        first_jobs = jobs(0)
        for g in range(1, groups):
            for i, job in enumerate(jobs(g)):
                before.setdefault((g - 1) * per + i, []).append(job)
    count = [0]

    def tensor(pe):
        done = [0]

        def project(job):
            if done[0]:
                pe.wait_ge(jobs_kept, done[0])
            job[0]().then_inc(jobs_ready, 1)
            done[0] += 1

        def score(n):
            g, qt, s = where(n)
            if jobs and n % per == 0:
                pe.wait_ge(jobs_kept, len(first_jobs) * (g + 1))
            if n >= ring:
                pe.wait_ge(exp_ready, n - ring + 1)
            for kb in range(banks):
                last = nc.tensor.matmul(scores(n)[:, kb * BANK:(kb + 1) * BANK], q_of(g, s, qt),
                                        k_of(g, s, kb), start=True, stop=True)
            last.then_inc(scores_ready, 1)

        def turn(n):
            pe.wait_ge(probs_ready, n + 1)
            for kb in range(banks):
                m = n * banks + kb
                if m >= 2:
                    pe.wait_ge(turned_kept, m - 1)
                for c in range(4):
                    kc = kb * 4 + c
                    last = nc.tensor.transpose(ps[:, 4 + m % 2, c * P:(c + 1) * P],
                                               probs[n % np_][:, kc * P:(kc + 1) * P], ident)
                last.then_inc(turned, 1)

        def values(g):
            pe.wait_ge(turned_kept, (g + 1) * per * banks)
            if g:
                pe.wait_ge(av_kept, g)
            for kc in range(nk):
                for s in range(heads):
                    last = nc.tensor.matmul(ps[rows * s:rows * (s + 1), 6, :], v_of(g, s, kc),
                                            pt[:, s, kc, :], start=kc == 0, stop=kc == nk - 1)
            last.then_inc(av_ready, 1)

        if prep:
            prep(pe)
        for job in first_jobs:
            project(job)
        for n in range(ring):
            score(n)
        for n in range(steps):
            if n + ring < steps:
                score(n + ring)
            turn(n)
            for job in before.get(n, []):
                project(job)
            if n % per == 0 and n:
                values(n // per - 1)
        values(groups - 1)

    def vector(v):
        done = [0]

        def keep_job(job):
            v.wait_ge(jobs_ready, done[0] + 1)
            job[1]().then_inc(jobs_kept, 1)
            done[0] += 1

        def find(n):
            v.wait_ge(scores_ready, n + 1)
            x = scores(n)
            if mask is None:
                nc.vector.tensor_reduce(least[:, n % 8:n % 8 + 1], x, AX.X, ALU.min).then_inc(least_ready, 1)
            else:
                nc.vector.tensor_tensor_reduce(out=x, in0=x, in1=mask, scale=1.0, scalar=FMAX, op0=add,
                                               op1=ALU.min, accum_out=least[:, n % 8:n % 8 + 1])\
                    .then_inc(least_ready, 1)

        def divide(n):
            v.wait_ge(exp_ready, n + 1)
            nc.vector.reciprocal(recip[:, n % 8:n % 8 + 1], sums[:, n % 8:n % 8 + 1]).then_inc(recip_ready, 1)
            v.wait_ge(recip_ready, n + 1)
            p = probs[n % np_]
            nc.vector.tensor_scalar(p, p, recip[:, n % 8:n % 8 + 1], None, mult).then_inc(probs_ready, 1)

        def keep_values(g):
            v.wait_ge(av_ready, g + 1)
            nc.vector.tensor_copy(out[:, g, :], ps[:, 6, :]).then_inc(av_kept, 1)

        for job in first_jobs:
            keep_job(job)
        for n in range(steps + 1):
            if n < steps:
                find(n)
            if n:
                divide(n - 1)
            for job in before.get(n - 2, []):
                keep_job(job)
            if n % per == 3 and n > per:
                keep_values(n // per - 1)
        keep_values(groups - 1)

    def scalar(act):
        def exponent(n):
            act.wait_ge(least_ready, n + 1)
            if n >= np_:
                act.wait_ge(turned, (n - np_ + 1) * banks)
            nc.scalar.activation(probs[n % np_], scores(n), ACT.Exp, bias=least[:, n % 8:n % 8 + 1],
                                 scale=-1.0, accum_out=sums[:, n % 8:n % 8 + 1]).then_inc(exp_ready, 1)

        def keep_turned(n):
            g, qt, s = where(n)
            if n % per == 0 and g:
                act.wait_ge(av_ready, g)
            for kb in range(banks):
                m = n * banks + kb
                act.wait_ge(turned, m + 1)
                nc.scalar.activation(pt[:, s, kb * 4:kb * 4 + 4, qt * P:(qt + 1) * P],
                                     ps[:, 4 + m % 2, :].rearrange("p (c q) -> p c q", c=4),
                                     ACT.Copy).then_inc(turned_kept, 1)

        for n in range(steps + 1):
            if n < steps:
                exponent(n)
            if n:
                keep_turned(n - 1)

    return tensor, vector, scalar, av_kept


def program(nc, a, out):
    ctx = ExitStack()
    with ctx:
        every = []

        def sem(name, scope=ctx):
            s = scope.enter_context(nc.semaphore(name))
            every.append(s)
            return s

        def keep(name, shape, dt=F32):
            return ctx.enter_context(nc.sbuf_tensor(name, shape, dt))

        @contextmanager
        def zeroed(since):
            yield
            nums = sorted(s.num for s in every[since:])
            starts = [n for n in nums if n - 1 not in nums]
            ends = [n + 1 for n in nums if n + 1 not in nums]
            for start, end in zip(starts, ends):
                nc.sync.sem_clear(range(start, end))
            nc.all_engine_barrier()

        x1_d = nc.dram_tensor("x1_scratch", [B, P, NT, D], F32, kind="Internal").ap()
        rows_d = nc.dram_tensor("normed_rows", [TOK + P, D], F32, kind="Internal").ap()
        taken_all = nc.dram_tensor("slot_token", [2 * SLOTS, 1], U32, kind="Internal").ap()
        taken_d = taken_all[0:SLOTS, :]
        y_d = nc.dram_tensor("expert_rows", [SLOTS, D], F32, kind="Internal").ap()

        ps = ctx.enter_context(nc.psum_tensor("ps", [P, 8, BANK], F32))
        consts = keep("consts", [P, 4, P])
        gates = keep("gates", [P, 8])
        vec = keep("vec", [P, 5, D])
        slot8 = keep("slot8", [P, B * NT, TOPK], U32)
        weight8 = keep("weight8", [P, B * NT, TOPK])
        taken = keep("taken", [P, PAIRS], U32)
        place8 = keep("place8", [P, NT, TOPK], U32)
        token_i = keep("token_i", [P, NT], U32)
        ident, upper, ones = consts[:, 0, :], consts[:, 1, :], consts[:, 2, :]
        keyrow = consts[:, 3, 0:E]
        bo0, outw1, b21, bo2, bias3 = (vec[:, i, :] for i in range(5))
        xb = keep("xb", [P, NT, D])
        xn = keep("xn", [P, NT, D])
        xnT = keep("xnT", [P, DC, S])
        ctxT = keep("ctxT", [P, DC, S])
        s6 = keep("s6", [P, 16, 6])
        mv = keep("mv", [P, 16, 2])
        stats = (s6, mv, keep("rstd", [P, 16]), keep("var", [P, 16]), keep("half", [P, 16]))
        least = keep("least", [P, 8])
        sums = keep("sums", [P, 8])
        recip = keep("recip", [P, 8])
        tmp = keep("tmp", [P, 2, D])

        consts_in = sem("consts_in")
        scattered = sem("scattered")
        gates_ready = sem("gates_ready")
        fill_ready = sem("fill_ready")
        fill_out = sem("fill_out")

        with nc.sbuf_tensor("zero_rows", [P, D], F32) as zero_rows, \
                nc.sbuf_tensor("no_token", [P, PAIRS], U32) as no_token, nc.Block() as block:
            @block.sync
            def _(sp):
                sp.dma_start(consts[:, :, :], a["consts"]).then_inc(consts_in, 16)
                sp.dma_start(gates[:, :], a["gates"].partition_broadcast(P)).then_inc(consts_in, 16)
                sp.dma_start(vec[:, :, :], a["vec"].partition_broadcast(P)).then_inc(consts_in, 16)
                sp.wait_ge(fill_ready, 2)
                sp.dma_start(rows_d[TOK:TOK + P, :], zero_rows[:, :]).then_inc(fill_out, 16)
                sp.dma_start(taken_d.rearrange("(p n) o -> p (n o)", p=P), no_token[:, :]).then_inc(fill_out, 16)
                sp.wait_ge(fill_out, 32)
                sp.wait_ge(consts_in, 48)

            @block.vector
            def _(v):
                nc.vector.memset(zero_rows[:, :], 0.0).then_inc(fill_ready, 1)
                nc.vector.memset(no_token[:, :], TOK).then_inc(fill_ready, 1)

            @block.scalar
            def _(act):
                act.wait_ge(consts_in, 48)
                nc.scalar.activation(gates[:, :], gates[:, :], ACT.Tanh).then_inc(gates_ready, 1)
                act.wait_ge(gates_ready, 1)

        def scatter():
            for t in range(NT):
                for k in range(TOPK):
                    nc.gpsimd.indirect_dma_start(
                        taken_all[:, :], bass.IndirectOffsetOnAxis(place8[:, t, k:k + 1], 0), token_i[:, t:t + 1], None,
                        bounds_check=2 * SLOTS - 1, oob_is_err=False).then_inc(scattered, 16)

        layer0(nc, a, sem, every, zeroed, locals())
        experts(nc, a, sem, locals())
        layers1to3(nc, a, sem, every, zeroed, locals(), out)


def layer0(nc, a, allocate, every, zeroed, G):
    ps, ident, upper, ones, keyrow = G["ps"], G["ident"], G["upper"], G["ones"], G["keyrow"]
    gates, bo0, slot8, weight8 = G["gates"], G["bo0"], G["slot8"], G["weight8"]
    xb, xn, xnT, ctxT, stats, tmp = G["xb"], G["xn"], G["xnT"], G["ctxT"], G["stats"], G["tmp"]
    least, sums, recip = G["least"], G["sums"], G["recip"]
    x1_d, rows_d = G["x1_d"], G["rows_d"]
    place8, token_i, scattered, scatter = G["place8"], G["token_i"], G["scattered"], G["scatter"]
    with ExitStack() as ctx:
        def keep(name, shape, dt=F32):
            return ctx.enter_context(nc.sbuf_tensor(name, shape, dt))

        def sem(name):
            return allocate(name, ctx)

        wq = keep("wq0", [P, DC, D])
        wk = keep("wk0", [P, DC, D])
        wv = keep("wv0", [P, DC, H0 * HPAD])
        wo = keep("wo0", [P, QUADS, D])
        wgate = keep("wgate0", [P, DC, E])
        bqk = keep("bqk0", [P, 2, DC])
        bv = keep("bv0", [P, H0 * HPAD])
        block16 = keep("block16", [P, P // DK0])
        mask_i = keep("mask_i", [P, S], I32)
        mask_f = keep("mask_f", [P, S])
        mask_add = keep("mask_add", [P, S])
        qT = keep("qT0", [P, DC, S])
        kT = keep("kT0", [P, DC, S])
        kH = keep("kH0", [P, H0, S])
        vh = keep("v0", [P, NT, H0 * HPAD])
        probs = [keep(f"probs0_{i}", [P, S])[:, :] for i in range(6)]
        pt = keep("pt0", [P, 4, NT, S])
        oT = keep("oT0", [P, QUADS, S])
        lg = keep("lg", [P, NT, E])
        rep = keep("rep", [P, NT, E])
        sel = keep("sel", [P, NT, E])
        ex = keep("ex", [P, NT, E])
        valid = keep("valid", [P, NT, E])
        key = keep("key", [P, NT, E])
        before = keep("before", [P, NT + 1, E])
        m8 = keep("m8", [P, NT, TOPK])
        e8 = keep("e8", [P, NT, TOPK])
        k8 = keep("k8", [P, NT, TOPK])
        w8 = keep("w8", [P, NT, TOPK])
        off8 = keep("off8", [P, NT, TOPK])
        negm = keep("negm", [P, NT])
        s8 = keep("s8", [P, NT])
        r8 = keep("r8", [P, NT])
        junk = keep("junk0", [P, NT * TOPK, E])
        token_f = keep("token_f", [P, NT])

        w_in = allocate("w0_in")
        before_zero = allocate("before_zero")
        with nc.Block() as block:
            @block.sync
            def _(sp):
                for dst, n in ((wq, "L0_wq"), (wk, "L0_wk"), (wv, "L0_wv"), (wo, "L0_wo"), (wgate, "L0_gate")):
                    sp.dma_start(dst[:, :, :], a[n]).then_inc(w_in, 16)
                sp.dma_start(bqk[:, :, :], a["L0_bqk"]).then_inc(w_in, 16)
                sp.dma_start(bv[:, :], a["L0_bv"].partition_broadcast(P)).then_inc(w_in, 16)
                sp.dma_start(block16[:, :], a["block16"]).then_inc(w_in, 16)
                sp.dma_start(token_f[:, :], a["token"]).then_inc(w_in, 16)
                sp.dma_start(place8[:, :, :], a["place_none"]).then_inc(w_in, 16)
                sp.wait_ge(w_in, 10 * 16)

            @block.vector
            def _(v):
                nc.vector.memset(before[:, 0, :], 0.0).then_inc(before_zero, 1)
                nc.vector.memset(token_i[:, :], 0).then_inc(before_zero, 1)
                v.wait_ge(before_zero, 2)

        since = len(every)
        x_in, ctxT_in, mask_in = sem("x0_in"), sem("ctxT0_in"), sem("mask0_in")
        order = sem("dve_order0")
        mask_ready = sem("mask0_ready")
        xn_ready = sem("xn0_ready")
        turned = sem("xn0_turned")
        xnT_ready = sem("xnT0_ready")
        prep_ready = sem("prep0_ready")
        prep_kept = sem("prep0_kept")
        out_ready = sem("out0_ready")
        rows_out = sem("rows0_out")
        logits_ready = sem("logits_ready")
        chosen = sem("chosen")
        exps = sem("exps0")
        before_ready = sem("before_ready")
        pos_ready = sem("pos_ready")
        placed = sem("placed")

        NPREP = 2 * DC + NT
        with nc.Fori(0, B) as b, zeroed(since), nc.Block() as block:
            def q_of(g, s, qt):
                return qT[:, (4 * g + s) // 8, qt * P:(qt + 1) * P]

            def k_of(g, s, kb):
                return kH[:, 4 * g + s, :]

            def v_of(g, s, kc):
                h = 4 * g + s
                return vh[:, kc, h * HPAD:(h + 1) * HPAD]

            att = attention(nc, sem, "a0", ps, ident, 4, QUADS, NT, q_of, k_of, v_of, HPAD, mask_add[:, :],
                            (probs, sums, recip, least, pt), oT)

            @block.sync
            def _(sp):
                sp.dma_start(xb[:, :, :], a["x"][b]).then_inc(x_in, 16)
                sp.dma_start(ctxT[:, :, :], a["ctxT"][b]).then_inc(ctxT_in, 16)
                sp.dma_start(mask_i[:, :], a["mask0"][b].partition_broadcast(P)).then_inc(mask_in, 16)
                sp.wait_ge(xn_ready, 2)
                sp.dma_start(x1_d[b], xb[:, :, :]).then_inc(rows_out, 16)
                sp.dma_start(rows_d[0:TOK, :].rearrange("(b t p) d -> b p t d", b=B, t=NT)[b],
                             xn[:, :, :]).then_inc(rows_out, 16)
                sp.wait_ge(rows_out, 32)

            @block.tensor
            def _(pe):
                def turn(k):
                    pe.wait_ge(xn_ready, k + 1)
                    for c in range(DC):
                        for t in range(NT):
                            last = nc.tensor.transpose(ps[:, c, t * P:(t + 1) * P],
                                                       xn[:, t, c * P:(c + 1) * P], ident)
                        last.then_inc(turned, 1)

                def prep(i, dst, pairs):
                    if i >= 4:
                        pe.wait_ge(prep_kept, i - 3)
                    for n, (l, r) in enumerate(pairs):
                        last = nc.tensor.matmul(dst, l, r, start=n == 0, stop=n == len(pairs) - 1)
                    last.then_inc(prep_ready, 1)

                pe.wait_ge(ctxT_in, 16)
                for i in range(DC):
                    prep(i, ps[:, 2 + i % 4, :], [(wk[:, c, i * P:(i + 1) * P], ctxT[:, c, :]) for c in range(DC)])
                for t in range(NT):
                    i = DC + t
                    prep(i, ps[:, 2 + i % 4, :], [(ctxT[:, c, t * P:(t + 1) * P], wv[:, c, :]) for c in range(DC)])
                turn(0)
                for j in range(DC):
                    i = DC + NT + j
                    if j == 0:
                        pe.wait_ge(xnT_ready, DC)
                    prep(i, ps[:, 2 + i % 4, :], [(wq[:, c, j * P:(j + 1) * P], xnT[:, c, :]) for c in range(DC)])
                pe.wait_ge(prep_kept, NPREP + 1)
                att[0](pe)
                pe.wait_ge(att[3], QUADS)
                for t in range(NT):
                    for g in range(QUADS):
                        last = nc.tensor.matmul(ps[:, t, 0:D], oT[:, g, t * P:(t + 1) * P], wo[:, g, :],
                                                start=g == 0, stop=g == QUADS - 1)
                    last.then_inc(out_ready, 1)
                turn(1)
                pe.wait_ge(xnT_ready, 2 * DC)
                for t in range(NT):
                    for c in range(DC):
                        last = nc.tensor.matmul(ps[:, 7, t * E:(t + 1) * E], xnT[:, c, t * P:(t + 1) * P],
                                                wgate[:, c, :], start=c == 0, stop=c == DC - 1)
                last.then_inc(logits_ready, 1)
                pe.wait_ge(before_ready, 1)
                for t in range(NT):
                    nc.tensor.matmul(ps[:, 6, t * E:(t + 1) * E], upper, sel[:, t, :], start=True, stop=False)
                    last = nc.tensor.matmul(ps[:, 6, t * E:(t + 1) * E], ones, before[:, t, :], start=False, stop=True)
                last.then_inc(pos_ready, 1)

            @block.scalar
            def _(act):
                def keep_turned(k):
                    for c in range(DC):
                        act.wait_ge(turned, k * DC + c + 1)
                        nc.scalar.activation(xnT[:, c, :], ps[:, c, :], ACT.Copy).then_inc(xnT_ready, 1)

                keep_turned(0)
                att[2](act)
                keep_turned(1)
                act.wait_ge(chosen, 1)
                for t in range(NT):
                    nc.scalar.activation(ex[:, t, :], lg[:, t, :], ACT.Exp, bias=negm[:, t:t + 1])
                    last = nc.scalar.activation(e8[:, t, :], m8[:, t, :], ACT.Exp, bias=negm[:, t:t + 1],
                                                accum_out=s8[:, t:t + 1])
                last.then_inc(exps, 1)

            @block.vector
            def _(v):
                link = Chain(v, order)
                v.wait_ge(x_in, 16)
                layernorm(nc, link, xb, xn, stats).then_inc(xn_ready, 1)
                v.wait_ge(mask_in, 16)
                link(nc.vector.tensor_scalar(mask_f[:, :], mask_i[:, :], 0.0, None, ALU.not_equal))
                nc.vector.tensor_scalar(mask_add[:, :], mask_f[:, :], -NEG1E9, NEG1E9, mult, add).then_inc(mask_ready, 1)
                for i in range(DC):
                    v.wait_ge(prep_ready, i + 1)
                    nc.vector.scalar_tensor_tensor(out=kT[:, i, :], in0=ps[:, 2 + i % 4, :], scalar=bqk[:, 1, i:i + 1],
                                                   in1=mask_f[:, :], op0=add, op1=mult).then_inc(prep_kept, 1)
                for t in range(NT):
                    i = DC + t
                    v.wait_ge(prep_ready, i + 1)
                    nc.vector.tensor_tensor(vh[:, t, :], ps[:, 2 + i % 4, :], bv[:, :], add).then_inc(prep_kept, 1)
                for j in range(DC):
                    i = DC + NT + j
                    v.wait_ge(prep_ready, i + 1)
                    nc.vector.tensor_scalar(qT[:, j, :], ps[:, 2 + i % 4, :], bqk[:, 0, j:j + 1], -DK0 ** -0.5,
                                            add, mult).then_inc(prep_kept, 1)
                v.wait_ge(prep_kept, NPREP)
                v.wait_ge(mask_ready, 1)
                for h in range(H0):
                    last = nc.vector.tensor_scalar(kH[:, h, :], kT[:, h // 8, :], block16[:, h % 8:h % 8 + 1], None, mult)
                last.then_inc(prep_kept, 1)
                att[1](v)
                for t in range(NT):
                    v.wait_ge(out_ready, t + 1)
                    link(nc.vector.tensor_tensor(tmp[:, t % 2, :], ps[:, t, 0:D], bo0, add))
                    last = nc.vector.scalar_tensor_tensor(out=xb[:, t, :], in0=tmp[:, t % 2, :], scalar=gates[:, 0:1],
                                                          in1=xb[:, t, :], op0=mult, op1=add)
                link(last)
                layernorm(nc, link, xb, xn, stats).then_inc(xn_ready, 1)
                v.wait_ge(logits_ready, 1)
                link(nc.vector.tensor_copy(lg[:, :, :], ps[:, 7, 0:NT * E].rearrange("p (t e) -> p t e", t=NT)))
                for t in range(NT):
                    last = nc.vector.max(m8[:, t, :], lg[:, t, :])
                link(last)
                nc.vector.tensor_scalar(negm[:, :], m8[:, :, 0], -1.0, None, mult).then_inc(chosen, 1)
                for t in range(NT):
                    last = nc.vector.match_replace(rep[:, t, :], m8[:, t, :], lg[:, t, :], -FMAX)
                link(last)
                link(nc.vector.tensor_tensor(sel[:, :, :], rep[:, :, :], lg[:, :, :], ALU.not_equal))
                for t in range(NT):
                    last = nc.vector.tensor_tensor(before[:, t + 1, :], before[:, t, :], sel[:, t, :], add)
                    if t < NT - 1:
                        link(last)
                last.then_inc(before_ready, 1)
                v.wait_ge(exps, 1)
                link(nc.vector.reciprocal(r8[:, :], s8[:, :]))
                for t in range(NT):
                    last = nc.vector.scalar_tensor_tensor(out=ex[:, t, :], in0=ex[:, t, :], scalar=r8[:, t:t + 1],
                                                          in1=sel[:, t, :], op0=mult, op1=mult)
                link(last)
                v.wait_ge(pos_ready, 1)
                pos = ps[:, 6, 0:NT * E].rearrange("p (t e) -> p t e", t=NT)
                nc.vector.scalar_tensor_tensor(out=valid[:, :, :], in0=pos, scalar=float(CAP), in1=sel[:, :, :],
                                               op0=ALU.is_lt, op1=mult)
                for t in range(NT):
                    last = nc.vector.scalar_tensor_tensor(out=key[:, t, :], in0=pos[:, t, :], scalar=float(PAIRS),
                                                          in1=keyrow, op0=mult, op1=add)
                nc.vector.tensor_copy(before[:, 0, :], before[:, NT, :])
                link(last)
                nc.vector.tensor_tensor(ex[:, :, :], ex[:, :, :], valid[:, :, :], mult)
                link(nc.vector.tensor_tensor(key[:, :, :], key[:, :, :], valid[:, :, :], mult))
                for t in range(NT):
                    last = nc.vector.max(k8[:, t, :], key[:, t, :])
                link(last)
                for t in range(NT):
                    for k in range(TOPK):
                        last = nc.vector.scalar_tensor_tensor(out=junk[:, t * TOPK + k, :], in0=key[:, t, :], scalar=k8[:, t, k:k + 1],
                                                              in1=ex[:, t, :], op0=ALU.is_equal, op1=mult,
                                                              accum_out=w8[:, t, k:k + 1])
                link(last)
                nc.vector.tensor_copy(weight8[:, bass.ds(b * NT, NT), :], w8[:, :, :])
                nc.vector.tensor_scalar(slot8[:, bass.ds(b * NT, NT), :], k8[:, :, :], -1.0, 0.0, add, ALU.max)
                link(nc.vector.tensor_scalar(off8[:, :, :], k8[:, :, :], 0.0, float(4 * SLOTS), ALU.is_equal, mult))
                v.wait_ge(scattered, (b + 1) * (NT * TOPK * 16))
                nc.vector.scalar_tensor_tensor(out=place8[:, :, :], in0=k8[:, :, :], scalar=-1.0, in1=off8[:, :, :],
                                               op0=add, op1=add).then_inc(placed, 1)
                nc.vector.tensor_copy(token_i[:, :], token_f[:, :]).then_inc(placed, 1)
                v.wait_ge(placed, 2)
                link(nc.vector.tensor_scalar(token_f[:, :], token_f[:, :], float(S), None, add))

            @block.gpsimd
            def _(pool):
                scatter()


def experts(nc, a, sem, G):
    ps, ident, taken, rows_d, taken_d, y_d = (G[k] for k in ("ps", "ident", "taken", "rows_d", "taken_d", "y_d"))
    scattered, scatter = G["scattered"], G["scatter"]
    RING = 4
    N = PAIRS // RING
    with ExitStack() as ctx:
        def keep(name, shape, dt=F32):
            return [ctx.enter_context(nc.sbuf_tensor(f"{name}_{i}", shape, dt)) for i in range(RING)]

        wgu = keep("wgu", [P, DC, 2, 2 * INTER])
        wd = keep("wd", [IH, 2, 2, D])
        column = keep("column", [P, 1], U32)
        xg = keep("xg", [P, D])
        xgT = keep("xgT", [P, DC, P])
        h = keep("h", [P, INTER])
        hT = keep("hT", [IH, 2, P])
        y = keep("y", [P, D])

        taken_in = sem("taken_in")
        wgu_in, wd_in = ([sem(f"{n}_in_{i}") for i in range(RING)] for n in ("wgu", "wd"))
        column_ready = [sem(f"column_ready_{i}") for i in range(RING)]
        rows_in = [sem(f"xg_in_{i}") for i in range(RING)]
        turned = [sem(f"xg_turned_{i}") for i in range(RING)]
        xgT_ready = [sem(f"xgT_ready_{i}") for i in range(RING)]
        gu_ready = [sem(f"gu_ready_{i}") for i in range(RING)]
        silu_ready = [sem(f"silu_ready_{i}") for i in range(RING)]
        h_ready = [sem(f"h_ready_{i}") for i in range(RING)]
        h_turned = [sem(f"h_turned_{i}") for i in range(RING)]
        hT_ready = [sem(f"hT_ready_{i}") for i in range(RING)]
        y_ready = [sem(f"ye_ready_{i}") for i in range(RING)]
        y_kept = [sem(f"ye_kept_{i}") for i in range(RING)]
        y_out = [sem(f"ye_out_{i}") for i in range(RING)]

        with nc.Block() as block:
            @block.sync
            def _(sp):
                def load(r, i):
                    sp.dma_start(wgu[i][:, :, :, :], a["L0_wgu"][r * RING + i]).then_inc(wgu_in[i], 16)
                    sp.dma_start(wd[i][:, :, :, :], a["L0_wd"][r * RING + i]).then_inc(wd_in[i], 16)

                y_rows = y_d.rearrange("(p r n) h -> r n p h", p=P, r=N)
                for i in range(RING):
                    load(0, i)
                sp.wait_ge(scattered, (B + 1) * NT * TOPK * 16)
                sp.dma_start(taken[:, :], taken_d.rearrange("(p n) o -> p (n o)", p=P)).then_inc(taken_in, 16)
                with sp.Fori(1, N) as r:
                    for i in range(RING):
                        sp.wait_ge(gu_ready[i], r)
                        sp.dma_start(wgu[i][:, :, :, :], a["L0_wgu"][r * RING + i]).then_inc(wgu_in[i], 16)
                        sp.wait_ge(y_ready[i], r)
                        sp.dma_start(wd[i][:, :, :, :], a["L0_wd"][r * RING + i]).then_inc(wd_in[i], 16)
                        sp.wait_ge(y_kept[i], r)
                        sp.dma_start(y_rows[r - 1, i], y[i][:, :]).then_inc(y_out[i], 16)
                for i in range(RING):
                    sp.wait_ge(y_kept[i], N)
                    sp.dma_start(y_rows[N - 1, i], y[i][:, :]).then_inc(y_out[i], 16)
                for i in range(RING):
                    sp.wait_ge(y_out[i], 16 * N)

            @block.gpsimd
            def _(pool):
                scatter()
                pool.wait_ge(taken_in, 16)

                def gather(done, i, at):
                    nc.gpsimd.tensor_copy(column[i][:, :], taken[:, bass.ds(at, 1)]).then_inc(column_ready[i], 1)
                    pool.wait_ge(taken_in, 16)
                    pool.wait_ge(column_ready[i], done)
                    nc.gpsimd.indirect_dma_start(xg[i][:, :], None, rows_d[:, :], bass.IndirectOffsetOnAxis(column[i][:, :], 0),
                                                 bounds_check=TOK + P - 1, oob_is_err=False).then_inc(rows_in[i], 16)

                for i in range(RING):
                    gather(1, i, i)
                with pool.Fori(2, N + 1) as done:
                    for i in range(RING):
                        at = pool.snap((done - 1) * RING + i)
                        pool.wait_ge(turned[i], done - 1)
                        gather(done, i, at)

            @block.tensor
            def _(pe):
                def turn(r, i):
                    pe.wait_ge(rows_in[i], 16 * r + 16)
                    for c in range(DC):
                        last = nc.tensor.transpose(ps[:, i % 2, c * P:(c + 1) * P], xg[i][:, c * P:(c + 1) * P], ident)
                    last.then_inc(turned[i], 1)

                def up(r, i):
                    pe.wait_ge(wgu_in[i], 16 * r + 16)
                    pe.wait_ge(xgT_ready[i], r + 1)
                    for c in range(DC):
                        for e in range(2):
                            last = nc.tensor.matmul(ps[e * CAP:(e + 1) * CAP, 2 + i % 2, 0:2 * INTER],
                                                    xgT[i][:, c, e * CAP:(e + 1) * CAP], wgu[i][:, c, e, :],
                                                    start=c == 0, stop=c == DC - 1)
                    last.then_inc(gu_ready[i], 1)

                def turn_hidden(r, i):
                    pe.wait_ge(h_ready[i], r + 1)
                    for j in range(2):
                        last = nc.tensor.transpose(ps[0:IH, 6 + i % 2, j * P:(j + 1) * P], h[i][:, j * IH:(j + 1) * IH], ident)
                    last.then_inc(h_turned[i], 1)

                def down(r, i, first=False):
                    pe.wait_ge(wd_in[i], 16 * r + 16)
                    pe.wait_ge(hT_ready[i], r + 1)
                    if i >= 2:
                        pe.wait_ge(y_kept[i - 2], r + 1)
                    elif not first:
                        pe.wait_ge(y_kept[i + 2], r)
                    for j in range(2):
                        for e in range(2):
                            last = nc.tensor.matmul(ps[e * CAP:(e + 1) * CAP, 4 + i % 2, 0:D], hT[i][:, j, e * CAP:(e + 1) * CAP],
                                                    wd[i][:, j, e, :], start=j == 0, stop=j == 1)
                    last.then_inc(y_ready[i], 1)

                def step(r, first=False, second=False, final=False):
                    for i in range(RING):
                        if i < RING - 1:
                            turn(r, i + 1)
                        elif not final:
                            turn(r + 1, 0)
                        up(r, i)
                        if i >= 1:
                            turn_hidden(r, i - 1)
                        elif not first:
                            turn_hidden(r - 1, RING - 1)
                        if i >= 2:
                            down(r, i - 2, first)
                        elif not first:
                            down(r - 1, i + RING - 2, second)

                turn(0, 0)
                step(0, first=True)
                step(1, second=True)
                with pe.Fori(2, N - 1) as r:
                    step(r)
                step(N - 1, final=True)
                turn_hidden(N - 1, RING - 1)
                for i in (RING - 2, RING - 1):
                    down(N - 1, i)

            @block.scalar
            def _(act):
                def keep_turned(r, i):
                    act.wait_ge(turned[i], r + 1)
                    nc.scalar.activation(xgT[i][:, :, :], ps[:, i % 2, 0:D].rearrange("p (c s) -> p c s", c=DC),
                                         ACT.Copy).then_inc(xgT_ready[i], 1)

                def keep_hidden(r, i):
                    act.wait_ge(h_turned[i], r + 1)
                    nc.scalar.activation(hT[i][:, :, :], ps[0:IH, 6 + i % 2, 0:2 * P].rearrange("p (j s) -> p j s", j=2),
                                         ACT.Copy).then_inc(hT_ready[i], 1)

                def step(r, first=False, final=False):
                    for i in range(RING):
                        if i < RING - 1:
                            keep_turned(r, i + 1)
                        elif not final:
                            keep_turned(r + 1, 0)
                        act.wait_ge(gu_ready[i], r + 1)
                        nc.scalar.activation(h[i][:, :], ps[:, 2 + i % 2, 0:INTER], ACT.Silu).then_inc(silu_ready[i], 1)
                        if i >= 1:
                            keep_hidden(r, i - 1)
                        elif not first:
                            keep_hidden(r - 1, RING - 1)

                keep_turned(0, 0)
                step(0, first=True)
                with act.Fori(1, N - 1) as r:
                    step(r)
                step(N - 1, final=True)
                keep_hidden(N - 1, RING - 1)

            @block.vector
            def _(v):
                def hidden(r, i):
                    v.wait_ge(silu_ready[i], r + 1)
                    nc.vector.tensor_tensor(h[i][:, :], h[i][:, :], ps[:, 2 + i % 2, INTER:2 * INTER], mult).then_inc(h_ready[i], 1)

                def rows(r, i, first=False):
                    v.wait_ge(y_ready[i], r + 1)
                    if not first:
                        v.wait_ge(y_out[i], 16 * r)
                    nc.vector.tensor_copy(y[i][:, :], ps[:, 4 + i % 2, 0:D]).then_inc(y_kept[i], 1)

                def step(r, first=False, second=False):
                    for i in range(RING):
                        hidden(r, i)
                        if i >= 2:
                            rows(r, i - 2, first)
                        elif not first:
                            rows(r - 1, i + RING - 2, second)

                step(0, first=True)
                step(1, second=True)
                with v.Fori(2, N) as r:
                    step(r)
                for i in (RING - 2, RING - 1):
                    rows(N - 1, i)


def layers1to3(nc, a, sem, every, zeroed, G, out):
    ps, ident, gates, slot8, weight8 = (G[k] for k in ("ps", "ident", "gates", "slot8", "weight8"))
    xb, xn, xnT, ctxT, stats, tmp = (G[k] for k in ("xb", "xn", "xnT", "ctxT", "stats", "tmp"))
    least, sums, recip, x1_d, y_d = (G[k] for k in ("least", "sums", "recip", "x1_d", "y_d"))
    outw1, b21, bo2, bias3, ones = (G[k] for k in ("outw1", "b21", "bo2", "bias3", "ones"))
    with ExitStack() as ctx:
        def keep(name, shape, dt=F32):
            return ctx.enter_context(nc.sbuf_tensor(name, shape, dt))

        gw1 = keep("gw1", [P, 6, 36])
        gb1 = keep("gb1", [36, 1])
        minus1 = keep("minus1", [H1, H1, P])
        wr1 = keep("wr1", [P, DC, P])
        w11 = keep("w11", [P, DC, F1])
        b11 = keep("b11", [P, FC1])
        w21 = keep("w21", [P, FC1, D])
        earlier = keep("earlier", [P, 7 * P])
        ln2 = keep("ln2", [P, 4, DC])
        ln3 = keep("ln3", [P, 4, DC])
        wp1 = keep("wp1", [P, DC, NAV])
        bp1 = keep("bp1", [P, 1])
        wp2 = keep("wp2", [P, E2])
        bp2 = keep("bp2", [1, E2])
        wo2f = keep("wo2f", [P, DC, D])
        wq3 = keep("wq3f", [P, DC, D], BF16)
        scale3 = keep("scale3f", [P, D])
        arena = keep("arena", [P, 41 * 256 + 128])
        ctxb = keep("ctxb", [P, NT, D])
        qT = [keep(f"qT_{i}", [P, S]) for i in range(2)]
        kH = [[keep(f"kH_{i}{s}", [P, KEYS3]) for s in range(2)] for i in range(2)]
        vh = [keep(f"vh_{i}", [P, KEYS3 // P, P]) for i in range(2)]
        work = keep("work", [P, 2 * 8 * S])
        wide = keep("wide", [P, 8, S])
        pbuf = keep("pbuf", [P, 4, KEYS3])
        idx8 = keep("idx8", [P, NT * TOPK], U32)
        w8b = keep("w8b", [P, NT, TOPK])
        small = keep("small", [P, 64])
        we1 = work[:, 0:DC * FE2].rearrange("p (c f) -> p c f", c=DC)
        we2 = work[:, DC * FE2:DC * FE2 + FEC * D].rearrange("p (c f) -> p c f", c=FEC)
        be1 = keep("be1", [P, FEC])
        be2 = keep("be2", [P, DC])

        def cut(start, *shape):
            n = int(np.prod(shape))
            names = "bcd"[:len(shape)]
            v = arena[:, start:start + n]
            return v.rearrange(f"p (b c) -> p b c", b=shape[0]), start + n

        wq2, at = cut(0, DC, INNER)
        wk2, at = cut(at, DC, P)
        wv2, at = cut(at, DC, DH2)
        wo2, at = cut(at, HP, D)
        wff1, at = cut(at, DC, 2 * FF2)
        wff2, at = cut(at, FFC, D)
        assert at <= 41 * 256 + 128
        wqx, at = cut(0, DC, INNER)
        wkx, at = cut(at, DC, INNER)
        wvx, at = cut(at, DC, INNER)
        wox, at = cut(at, HP, D)
        keysT, at = cut(at, DC, KEYS3)
        assert at <= 41 * 256 + 128
        mask_u8 = keep("mask_u8", [P, S], mybir.dt.uint8)
        mask3 = keep("mask3", [P, KEYS3])
        xqT = keep("xqT", [P, DC, S], BF16)
        pick = keep("pick", [1, 8], U32)

        const_in = sem("constB_in")
        prepB = sem("prepB")
        prepB_mm = sem("prepB_mm")
        w3_raw = work[:, 0:2 * D].rearrange("p (c f) -> p c f", c=2)
        w3_q = work[:, 2 * D:4 * D].rearrange("p (c f) -> p c f", c=2)
        w3_d = work[:, 4 * D:5 * D].rearrange("p (c f) -> p c f", c=2)

        def quantise(link, src, dst, tiles, amax, scale, clip):
            link(nc.vector.tensor_reduce(amax, src, AX.X, ALU.max, apply_absolute_value=True))
            link(nc.vector.tensor_scalar(scale, amax, 1e-8, 1.0 / QMAX, ALU.max, mult))
            link(nc.vector.reciprocal(amax, scale))
            for t in range(tiles):
                last = nc.vector.tensor_scalar(clip[:, t, :], src[:, t, :], amax[:, t:t + 1], ROUND, mult, add)
            link(last)
            link(nc.vector.tensor_scalar(clip, clip, ROUND, QMAX, subtract, ALU.min))
            return nc.vector.tensor_scalar(dst, clip, -QMAX - 1, None, ALU.max)

        with nc.Block() as block:
            @block.sync
            def _(sp):
                loads = [(gw1[:, :, :], "L1_gw"), (gb1[:, :], "L1_gb"), (minus1[:, :, :], "minus1"), (wr1[:, :, :], "L1_wr"),
                         (w11[:, :, :], "L1_w1"), (b11[:, :], "L1_b1"), (w21[:, :, :], "L1_w2"), (earlier[:, :], "earlier"),
                         (ln2[:, :, :], "L2_ln"), (ln3[:, :, :], "L3_ln"), (wp1[:, :, :], "L2_wp1"), (bp1[:, :], "L2_bp1"),
                         (wp2[:, :], "L2_wp2"), (bp2[:, :], "L2_bp2"), (wo2f[:, :, :], "L2_wof"), (w3_raw, "L3_w")]
                for dst, n in loads:
                    sp.dma_start(dst, a[n]).then_inc(const_in, 16)
                sp.wait_ge(const_in, 16 * len(loads))

            @block.vector
            def _(v):
                link = Chain(v, prepB)
                for i in range(2):
                    nc.vector.memset(kH[i][0][64:P, :], 0.0)
                    link(nc.vector.memset(kH[i][1][0:64, :], 0.0))
                v.wait_ge(const_in, 16 * 16)
                link(quantise(link, w3_raw, w3_q, 2, small[:, 0:2], small[:, 2:4], w3_q))
                for c in range(2):
                    last = nc.vector.tensor_scalar(w3_d[:, c, :], ident, small[:, 2 + c:3 + c], None, mult)
                link(last)
                v.wait_ge(prepB_mm, 1)
                for c in range(DC):
                    nc.vector.tensor_copy(wq3[:, c, :], ps[:, c, 0:D])
                link(nc.vector.tensor_copy(scale3[:, :], ps[:, 2, 0:D]))

            @block.tensor
            def _(pe):
                pe.wait_ge(prepB, 9)
                for c in range(DC):
                    for o in range(2):
                        nc.tensor.transpose(ps[:, c, o * P:(o + 1) * P], w3_q[:, o, c * P:(c + 1) * P], ident)
                for o in range(2):
                    last = nc.tensor.matmul(ps[:, 2, o * P:(o + 1) * P], ones, w3_d[:, o, :], start=True, stop=True)
                last.then_inc(prepB_mm, 1)

        y_ins = [sem(f"y_in_{t}") for t in range(NT)]
        since = len(every)
        x_in, ctx_in, arena_in, idx_ready = (sem(n + "_B") for n in ("x_in", "ctx_in", "arena_in", "idx_ready"))
        order = sem("dve_orderB")
        xn_ready, turned, xnT_ready = sem("xnB_ready"), sem("xnB_turned"), sem("xnTB_ready")
        summed = sem("y_summed")

        yg = [work[:, i * TOPK * D:(i + 1) * TOPK * D].rearrange("p (k d) -> p k d", k=TOPK) for i in range(2)]

        with nc.Fori(0, B) as b, zeroed(since), nc.Block() as block:
            turns = [0]

            def pe_turn(pe, src, k, extra=None):
                for c in range(DC):
                    for t in range(NT):
                        last = nc.tensor.transpose(ps[:, c, t * P:(t + 1) * P], src[:, t, c * P:(c + 1) * P], ident)
                    last.then_inc(turned, 1)

            qH = work[:, 0:H1 * S].rearrange("p (h s) -> p h s", h=H1)
            cT = [work[:, (H1 + 4 * i) * S:(H1 + 4 * i + 4) * S].rearrange("p (c s) -> p c s", c=NT) for i in range(2)]
            eT = [pbuf[:, i // 2, (i % 2) * S:(i % 2 + 1) * S] for i in range(4)]
            vaug = wide[:, 0:3, :].rearrange("p a b -> p (a b)")[:, 0:NT * H1 * 66].rearrange("p (c h d) -> p c h d", c=NT, h=H1)
            flat = wide[:, :, :].rearrange("p a b -> p (a b)")
            o = NT * H1 * 66
            gsb = flat[0:36, o:o + S]
            f_r = flat[0:H1, o + S:o + 2 * S]
            a_r = flat[0:H1, o + 2 * S:o + 3 * S]
            cs_r = flat[0:H1, o + 3 * S:o + 4 * S + 1]
            G_r = flat[0:H1, o + 4 * S + 2:o + 5 * S + 2]
            stack = pbuf[0:36, 2, 0:S]
            names = ("gates_ready", "gsb_ready", "f_ready", "abs_ready", "softplus", "stack_ready", "stackT_ready", "gT_ready",
                     "en_ready", "gb_ready", "e_ready", "d_ready", "dmask_ready", "qk_ready", "c_ready", "h_ready", "h_kept", "zeros1")
            L1 = {n: sem("L1_" + n) for n in names}
            gT = keep("gT1", [P, NT, 36])
            en = keep("en1", [P, NT, H1])
            hb = pbuf[:, 2, :].rearrange("p (t h d) -> p t h d", t=NT, h=H1)
            hn = pbuf[:, 3, :].rearrange("p (t h d) -> p t h d", t=NT, h=H1)

            def l1_tensor(pe):
                pe.wait_ge(xn_ready, 1)
                pe_turn(pe, xn, 0)
                pe.wait_ge(xnT_ready, 4)
                pe.wait_ge(ctx_in, 32)
                g_terms = [(gw1[:, h // 2, :], qH[:, h, :]) for h in range(H1)] + \
                          [(gw1[:, 2 + c, :], ctxT[:, c % 2, :]) for c in range(4)]
                for n, (l, r) in enumerate(g_terms):
                    last = nc.tensor.matmul(ps[0:36, 2, :], l, r, start=n == 0, stop=n == len(g_terms) - 1)
                last.then_inc(L1["gates_ready"], 1)
                pe.wait_ge(L1["stack_ready"], 1)
                for t in range(NT):
                    last = nc.tensor.transpose(ps[:, 3, t * 36:(t + 1) * 36], stack[:, t * P:(t + 1) * P], ident[0:36, 0:36])
                last.then_inc(L1["stackT_ready"], 1)
                pe.wait_ge(L1["gT_ready"], 1)

                def product(h):
                    pe.wait_ge(L1["c_ready"], NT * (h + 1))
                    if h:
                        pe.wait_ge(L1["h_kept"], h)
                    for st in range(NT):
                        for tc in range(st + 1):
                            last = nc.tensor.matmul(ps[:, 6, st * 65:(st + 1) * 65], cT[h % 2][:, tc, st * P:(st + 1) * P],
                                                    vaug[:, tc, h, 0:65], start=tc == 0, stop=tc == st)
                    last.then_inc(L1["h_ready"], 1)

                for h in range(H1):
                    if h >= 2:
                        pe.wait_ge(L1["e_ready"], NT * (h - 1))
                    nc.tensor.matmul(ps[:, 4 + h % 2, :], minus1[:, h, :], G_r, start=True, stop=True)\
                        .then_inc(L1["gb_ready"], 1)
                    for tc in range(NT):
                        n = h * NT + tc
                        if n >= 4:
                            pe.wait_ge(L1["c_ready"], n - 3)
                        nc.tensor.matmul(ps[:, n % 4, tc * P:S], ctxT[:, h // 2, tc * P:(tc + 1) * P], qH[:, h, tc * P:S],
                                         start=True, stop=True).then_inc(L1["qk_ready"], 1)
                    if h:
                        product(h - 1)
                product(H1 - 1)

            def l1_scalar(act):
                act.wait_ge(L1["zeros1"], 1)
                for c in range(DC):
                    act.wait_ge(turned, c + 1)
                    for s in range(2):
                        r = slice(64 * s, 64 * s + 64)
                        nc.scalar.activation(qH[r, 2 * c + s, :], ps[r, c, :], ACT.Copy).then_inc(xnT_ready, 1)
                act.wait_ge(L1["gsb_ready"], 1)
                nc.scalar.activation(f_r, gsb[32:36, :], ACT.Copy).then_inc(L1["f_ready"], 1)
                act.wait_ge(L1["abs_ready"], 1)
                nc.scalar.activation(a_r, a_r, ACT.Exp, scale=-1.0).then_inc(L1["softplus"], 1)
                act.wait_ge(L1["softplus"], 1)
                nc.scalar.activation(a_r, a_r, ACT.Ln, bias=1.0).then_inc(L1["softplus"], 1)
                act.wait_ge(L1["gT_ready"], 1)
                nc.scalar.activation(en[:, :, :], gT[:, :, 32:36], ACT.Exp, scale=-1.0).then_inc(L1["en_ready"], 1)
                for n in range(H1 * NT):
                    tc = n % NT
                    act.wait_ge(L1["e_ready"], n + 1)
                    nc.scalar.activation(eT[n % 4][:, tc * P:S], eT[n % 4][:, tc * P:S], ACT.Exp).then_inc(L1["d_ready"], 1)

            def l1_pool(pool):
                for n in range(H1 * NT):
                    tc = n % NT
                    pool.wait_ge(L1["d_ready"], n + 1)
                    d = eT[n % 4][:, tc * P:(tc + 1) * P]
                    nc.gpsimd.affine_select(out=d, in_=d, pattern=[[1, P]], compare_op=ALU.is_ge, fill=0.0, base=0,
                                            channel_multiplier=-1).then_inc(L1["dmask_ready"], 1)

            def l1_vector(v, link):
                for h in range(H1):
                    o = 64 * (1 - h % 2)
                    nc.vector.memset(qH[o:o + 64, h, :], 0.0)
                nc.vector.memset(stack[:, :], 0.0)
                nc.vector.memset(cs_r[:, 0:1], 0.0)
                nc.vector.memset(G_r, 1.0)
                nc.vector.memset(vaug[:, :, :, 64:65], 1.0).then_inc(L1["zeros1"], 1)
                v.wait_ge(L1["zeros1"], 1)
                v.wait_ge(ctx_in, 32)
                nc.vector.tensor_copy(vaug[:, :, :, 0:64], ctxb[:, :, :].rearrange("p c (h d) -> p c h d", h=H1))
                v.wait_ge(L1["gates_ready"], 1)
                nc.vector.tensor_scalar(gsb, ps[0:36, 2, :], gb1[:, 0:1], None, add).then_inc(L1["gsb_ready"], 1)
                v.wait_ge(L1["f_ready"], 1)
                nc.vector.scalar_tensor_tensor(out=a_r, in0=f_r, scalar=-1.0, in1=f_r, op0=mult, op1=ALU.max).then_inc(L1["abs_ready"], 1)
                v.wait_ge(L1["softplus"], 2)
                link(nc.vector.scalar_tensor_tensor(out=f_r, in0=f_r, scalar=0.0, in1=a_r,
                                                    op0=ALU.min, op1=subtract))
                link(nc.vector.tensor_tensor_scan(cs_r[:, 1:S + 1], G_r, f_r, 0.0, mult, add))
                link(nc.vector.tensor_tensor(stack[0:H1, :], gsb[0:H1, :], cs_r[:, 0:S], subtract))
                link(nc.vector.tensor_tensor_scan(G_r, stack[0:H1, :], stack[0:H1, :], -FMAX, ALU.max, ALU.max))
                nc.vector.tensor_tensor(stack[32:36, :], cs_r[:, 1:S + 1], G_r, add).then_inc(L1["stack_ready"], 1)
                v.wait_ge(L1["stackT_ready"], 1)
                nc.vector.tensor_copy(gT[:, :, :], ps[:, 3, 0:NT * 36].rearrange("p (t k) -> p t k", t=NT)).then_inc(L1["gT_ready"], 1)
                v.wait_ge(L1["gT_ready"], 1)

                def exponent(n):
                    h, tc = divmod(n, NT)
                    v.wait_ge(L1["gb_ready"], h + 1)
                    if n >= 4:
                        v.wait_ge(L1["c_ready"], n - 3)
                    nc.vector.tensor_scalar(eT[n % 4][:, tc * P:S], ps[:, 4 + h % 2, tc * P:S], gT[:, tc, h:h + 1], 0.0,
                                            add, ALU.min).then_inc(L1["e_ready"], 1)

                def normed(h):
                    o = ps[:, 6, 0:NT * 65].rearrange("p (t d) -> p t d", t=NT)
                    n4 = small[:, 4 * (h % 2):4 * (h % 2) + 4]
                    v.wait_ge(L1["h_ready"], h + 1)
                    v.wait_ge(L1["en_ready"], 1)
                    link(nc.vector.tensor_tensor(n4, o[:, :, 64], en[:, :, h], ALU.max))
                    link(nc.vector.scalar_tensor_tensor(out=n4, in0=o[:, :, 64], scalar=-1.0, in1=n4, op0=mult, op1=ALU.max))
                    link(nc.vector.tensor_scalar(n4, n4, 1e-8, None, add))
                    link(nc.vector.reciprocal(n4, n4))
                    for t in range(NT):
                        last = nc.vector.tensor_scalar(hb[:, t, h, :], o[:, t, 0:64], n4[:, t:t + 1], None, mult)
                    last.then_inc(L1["h_kept"], 1)

                for n in range(2):
                    exponent(n)
                for n in range(H1 * NT):
                    if n + 2 < H1 * NT:
                        exponent(n + 2)
                    h, tc = divmod(n, NT)
                    v.wait_ge(L1["qk_ready"], n + 1)
                    v.wait_ge(L1["dmask_ready"], n + 1)
                    if h >= 2:
                        v.wait_ge(L1["h_ready"], h - 1)
                    nc.vector.scalar_tensor_tensor(out=cT[h % 2][:, tc, tc * P:S], in0=ps[:, n % 4, tc * P:S], scalar=DH1 ** -0.5,
                                                   in1=eT[n % 4][:, tc * P:S], op0=mult, op1=mult).then_inc(L1["c_ready"], 1)
                    if tc == 2 and h:
                        normed(h - 1)
                normed(H1 - 1)
                v.wait_ge(L1["h_kept"], H1)
                link(layernorm(nc, link, hb.rearrange("p t h d -> p (t h) d"), hn.rearrange("p t h d -> p (t h) d"), stats, NT * H1))
                link(nc.vector.tensor_scalar(tmp[:, 1, :], outw1, 1.0, gates[:, 1:2], add, mult))
                hrow = hn.rearrange("p t h d -> p t (h d)")
                for t in range(NT):
                    last = nc.vector.tensor_tensor(hrow[:, t, :], hrow[:, t, :], tmp[:, 1, :], mult)
                link(last)
                link(nc.vector.tensor_tensor(xb[:, :, :], xb[:, :, :], hrow, add))

            F = {n: sem("F1_" + n) for n in ("score_ready", "col_ready", "sig_ready", "hid_ready", "hid_kept", "out_ready", "out_kept")}
            srow, one_row, sjunk = pbuf[:, 2, 0:S], pbuf[:, 2, S:2 * S], pbuf[:, 3, 0:S]
            col, c1, c2, sig = small[:, 0:4], small[:, 4:8], small[:, 8:12], small[:, 12:16]

            def f1_tensor(pe):
                pe.wait_ge(xn_ready, 2)
                pe_turn(pe, xn, 1)
                pe.wait_ge(xnT_ready, 6)
                for c in range(DC):
                    last = nc.tensor.matmul(ps[:, 2, :], wr1[:, c, :], xnT[:, c, :], start=c == 0, stop=c == DC - 1)
                last.then_inc(F["score_ready"], 1)
                for f in range(FC1):
                    if f >= 3:
                        pe.wait_ge(F["hid_kept"], f - 2)
                    for c in range(DC):
                        last = nc.tensor.matmul(ps[:, 3 + f % 3, :], w11[:, c, f * P:(f + 1) * P], xnT[:, c, :],
                                                start=c == 0, stop=c == DC - 1)
                    last.then_inc(F["hid_ready"], 1)
                pe.wait_ge(F["hid_kept"], FC1)
                for t in range(NT):
                    if t >= 2:
                        pe.wait_ge(F["out_kept"], t - 1)
                    for f in range(FC1):
                        last = nc.tensor.matmul(ps[:, 6 + t % 2, 0:D], wide[:, f, t * P:(t + 1) * P], w21[:, f, :],
                                                start=f == 0, stop=f == FC1 - 1)
                    last.then_inc(F["out_ready"], 1)

            def keep_turned(act, k, dst, at_):
                for c in range(DC):
                    act.wait_ge(turned, at_ + c + 1)
                    nc.scalar.activation(dst[:, c, :], ps[:, c, :], ACT.Copy).then_inc(xnT_ready, 1)

            def f1_scalar(act):
                keep_turned(act, 1, xnT, 2)
                act.wait_ge(F["col_ready"], 1)
                nc.scalar.activation(sig, col, ACT.Exp, scale=-1.0).then_inc(F["sig_ready"], 1)
                for f in range(FC1):
                    act.wait_ge(F["hid_ready"], f + 1)
                    nc.scalar.activation(wide[:, f, :], ps[:, 3 + f % 3, :], ACT.Gelu_apprx_tanh, bias=b11[:, f:f + 1])\
                        .then_inc(F["hid_kept"], 1)

            def f1_vector(v, link):
                layernorm(nc, link, xb, xn, stats).then_inc(xn_ready, 1)
                link(nc.vector.memset(one_row, 1.0))
                v.wait_ge(F["score_ready"], 1)
                link(nc.vector.tensor_copy(srow, ps[:, 2, :]))
                for t in range(NT):
                    last = nc.vector.tensor_tensor_reduce(out=sjunk[:, t * P:(t + 1) * P], in0=srow[:, t * P:(t + 1) * P], in1=ident, scale=1.0,
                                                          scalar=0.0, op0=mult, op1=add, accum_out=col[:, t:t + 1])
                last.then_inc(F["col_ready"], 1)
                v.wait_ge(F["col_ready"], 1)
                for t in range(NT):
                    link(nc.vector.scalar_tensor_tensor(out=sjunk, in0=srow, scalar=col[:, t:t + 1], in1=one_row,
                                                        op0=ALU.is_gt, op1=mult, accum_out=c1[:, t:t + 1]))
                    last = nc.vector.scalar_tensor_tensor(out=sjunk, in0=srow, scalar=col[:, t:t + 1],
                                                          in1=earlier[:, 3 * P - t * P:3 * P - t * P + S], op0=ALU.is_equal,
                                                          op1=mult, accum_out=c2[:, t:t + 1])
                    link(last)
                link(nc.vector.tensor_tensor(c1, c1, c2, add))
                v.wait_ge(F["sig_ready"], 1)
                link(nc.vector.tensor_scalar(sig, sig, 1.0, None, add))
                link(nc.vector.reciprocal(sig, sig))
                link(nc.vector.scalar_tensor_tensor(out=sig, in0=c1, scalar=float(KEEP), in1=sig, op0=ALU.is_lt, op1=mult))
                for t in range(NT):
                    v.wait_ge(F["out_ready"], t + 1)
                    o = tmp[:, t % 2, :]
                    nc.vector.tensor_tensor(o, ps[:, 6 + t % 2, 0:D], b21, add).then_inc(F["out_kept"], 1)
                    v.wait_ge(F["out_kept"], t + 1)
                    link(nc.vector.scalar_tensor_tensor(out=o, in0=o, scalar=sig[:, t:t + 1], in1=xn[:, t, :], op0=mult, op1=add))
                    last = nc.vector.scalar_tensor_tensor(out=xb[:, t, :], in0=o, scalar=gates[:, 5:6], in1=xb[:, t, :],
                                                          op0=mult, op1=add)
                link(last)

            A = {n: sem("A2_" + n) for n in ("k_ready", "kv_kept", "gate_ready", "silu_ready", "hT_ready", "out_ready")}
            cnT = wide[:, 0:DC, :]
            hT2 = work[:, 0:FFC * S].rearrange("p (f s) -> p f s", f=FFC)

            def q_job(w, xT, g):
                def product():
                    for c in range(DC):
                        last = nc.tensor.matmul(ps[:, 7, :], w[:, c, g * P:(g + 1) * P], xT[:, c, :], start=c == 0, stop=c == DC - 1)
                    return last

                return product, lambda: nc.vector.tensor_scalar(qT[g % 2][:, :], ps[:, 7, :], -DH2 ** -0.5, None, mult)

            def prep2(pe):
                pe.wait_ge(arena_in, 96)
                pe.wait_ge(xnT_ready, 12)
                for c in range(DC):
                    last = nc.tensor.matmul(ps[:, 2, :], wk2[:, c, :], cnT[:, c, :], start=c == 0, stop=c == DC - 1)
                for t in range(NT):
                    for c in range(DC):
                        last = nc.tensor.matmul(ps[:, 3, t * DH2:(t + 1) * DH2], cnT[:, c, t * P:(t + 1) * P], wv2[:, c, :],
                                                start=c == 0, stop=c == DC - 1)
                last.then_inc(A["k_ready"], 1)
                pe.wait_ge(A["kv_kept"], 1)

            att2 = attention(nc, sem, "a2", ps, ident, 2, HP, NT,
                             lambda g, s, qt: qT[g % 2][:, qt * P:(qt + 1) * P],
                             lambda g, s, kb: kH[0][s][:, 0:S],
                             lambda g, s, kc: vh[0][:, kc, 0:DH2], DH2, None,
                             ([pbuf[:, i // 2, (i % 2) * S:(i % 2 + 1) * S] for i in range(8)], sums, recip, least,
                              work[:, 0:2 * NT * S].rearrange("p (s c q) -> p s c q", s=2, c=NT)), wide,
                             prep=prep2, jobs=lambda g: [q_job(wq2, xnT, g)])

            def l2_tensor(pe):
                pe.wait_ge(xn_ready, 3)
                pe_turn(pe, xn, 2)
                pe.wait_ge(xn_ready, 4)
                pe.wait_ge(xnT_ready, 8)
                pe_turn(pe, ctxb, 3)
                att2[0](pe)
                for f in range(FFC):
                    if f >= 2:
                        pe.wait_ge(A["hT_ready"], f - 1)
                    for c in range(DC):
                        nc.tensor.matmul(ps[:, f % 2, :], wff1[:, c, FF2 + f * P:FF2 + (f + 1) * P], xnT[:, c, :],
                                         start=c == 0, stop=c == DC - 1)
                    for c in range(DC):
                        last = nc.tensor.matmul(ps[:, 2 + f % 2, :], wff1[:, c, f * P:(f + 1) * P], xnT[:, c, :],
                                                start=c == 0, stop=c == DC - 1)
                    last.then_inc(A["gate_ready"], 1)
                pe.wait_ge(att2[3], HP)
                pe.wait_ge(A["hT_ready"], FFC)
                for t in range(NT):
                    for g in range(HP):
                        nc.tensor.matmul(ps[:, 4 + t, 0:D], wide[:, g, t * P:(t + 1) * P], wo2[:, g, :], start=g == 0, stop=False)
                    for f in range(FFC):
                        last = nc.tensor.matmul(ps[:, 4 + t, 0:D], hT2[:, f, t * P:(t + 1) * P], wff2[:, f, :],
                                                start=False, stop=f == FFC - 1)
                    last.then_inc(A["out_ready"], 1)

            def l2_scalar(act):
                for c in range(DC):
                    act.wait_ge(turned, 4 + c + 1)
                    nc.scalar.activation(xnT[:, c, :], ps[:, c, :], ACT.Identity, bias=ln2[:, 1, c:c + 1],
                                         scale=ln2[:, 0, c:c + 1]).then_inc(xnT_ready, 1)
                for c in range(DC):
                    act.wait_ge(turned, 6 + c + 1)
                    nc.scalar.activation(ctxT[:, c, :], ps[:, c, :], ACT.Copy).then_inc(xnT_ready, 1)
                    nc.scalar.activation(cnT[:, c, :], ps[:, c, :], ACT.Identity, bias=ln2[:, 3, c:c + 1],
                                         scale=ln2[:, 2, c:c + 1]).then_inc(xnT_ready, 1)
                att2[2](act)
                for f in range(FFC):
                    act.wait_ge(A["gate_ready"], f + 1)
                    if f >= 2:
                        act.wait_ge(A["hT_ready"], f - 1)
                    nc.scalar.activation(pbuf[:, f % 2, 0:S], ps[:, f % 2, :], ACT.Silu).then_inc(A["silu_ready"], 1)

            def l2_vector(v, link):
                link(layernorm(nc, link, xb, xn, stats))
                layernorm(nc, link, xn, xn, stats).then_inc(xn_ready, 1)
                v.wait_ge(xn_ready, 3)
                layernorm(nc, link, ctxb, ctxb, stats).then_inc(xn_ready, 1)
                v.wait_ge(A["k_ready"], 1)
                for s in range(2):
                    r = slice(64 * s, 64 * s + 64)
                    nc.vector.tensor_copy(kH[0][s][r, 0:S], ps[r, 2, :])
                nc.vector.tensor_copy(vh[0][:, 0:NT, 0:DH2], ps[:, 3, 0:NT * DH2].rearrange("p (t d) -> p t d", t=NT))\
                    .then_inc(A["kv_kept"], 1)
                att2[1](v)
                for f in range(FFC):
                    v.wait_ge(A["silu_ready"], f + 1)
                    nc.vector.tensor_tensor(hT2[:, f, :], pbuf[:, f % 2, 0:S], ps[:, 2 + f % 2, :], mult).then_inc(A["hT_ready"], 1)
                for t in range(NT):
                    v.wait_ge(A["out_ready"], t + 1)
                    last = nc.vector.scalar_tensor_tensor(out=xb[:, t, :], in0=ps[:, 4 + t, 0:D], scalar=gates[:, 2:3],
                                                          in1=xb[:, t, :], op0=mult, op1=add)
                link(last)

            R = {n: sem("R2_" + n) for n in ("z_ready", "z_kept", "logit_ready", "picked", "we_in", "hid_ready", "hid_kept",
                                             "mid_ready", "mid_kept", "out_ready")}
            z, lrow, l8 = small[:, 32:33], small[0:1, 40:48], small[0:1, 48:56]

            def r2_tensor(pe):
                pe.wait_ge(xn_ready, 5)
                pe_turn(pe, xn, 4)
                pe.wait_ge(xnT_ready, 14)
                for c in range(DC):
                    last = nc.tensor.matmul(ps[:, 2, 0:1], wp1[:, c, :], xnT[:, c, S - 1:S], start=c == 0, stop=c == DC - 1)
                last.then_inc(R["z_ready"], 1)
                pe.wait_ge(R["z_kept"], 1)
                nc.tensor.matmul(ps[0:1, 3, 0:E2], z, wp2[:, :], start=True, stop=True).then_inc(R["logit_ready"], 1)
                pe.wait_ge(R["we_in"], 64)
                for f in range(FEC):
                    for c in range(DC):
                        last = nc.tensor.matmul(ps[:, 4 + f, :], we1[:, c, f * P:(f + 1) * P], xnT[:, c, :],
                                                start=c == 0, stop=c == DC - 1)
                    last.then_inc(R["hid_ready"], 1)
                for h in range(DC):
                    for f in range(FEC):
                        if h == 0:
                            pe.wait_ge(R["hid_kept"], f + 1)
                        last = nc.tensor.matmul(ps[:, h, :], we2[:, f, h * P:(h + 1) * P], wide[:, f, :],
                                                start=f == 0, stop=f == FEC - 1)
                    last.then_inc(R["mid_ready"], 1)
                pe.wait_ge(R["mid_kept"], DC)
                for t in range(NT):
                    for h in range(DC):
                        last = nc.tensor.matmul(ps[:, 2 + t, 0:D], wide[:, FEC + h, t * P:(t + 1) * P], wo2f[:, h, :],
                                                start=h == 0, stop=h == DC - 1)
                    last.then_inc(R["out_ready"], 1)

            def r2_scalar(act):
                keep_turned(act, 4, xnT, 8)
                act.wait_ge(R["z_ready"], 1)
                nc.scalar.activation(z, ps[:, 2, 0:1], ACT.Gelu, bias=bp1[:, 0:1]).then_inc(R["z_kept"], 1)
                act.wait_ge(R["we_in"], 64)
                for f in range(FEC):
                    act.wait_ge(R["hid_ready"], f + 1)
                    nc.scalar.activation(wide[:, f, :], ps[:, 4 + f, :], ACT.Gelu, bias=be1[:, f:f + 1]).then_inc(R["hid_kept"], 1)

            def r2_vector(v, link):
                layernorm(nc, link, xb, xn, stats).then_inc(xn_ready, 1)
                v.wait_ge(R["logit_ready"], 1)
                link(nc.vector.tensor_tensor(lrow, ps[0:1, 3, 0:E2], bp2[:, :], add))
                link(nc.vector.max(l8, lrow))
                nc.vector.max_index(pick[:, :], l8, lrow).then_inc(R["picked"], 1)
                v.wait_ge(R["we_in"], 64)
                for h in range(DC):
                    v.wait_ge(R["mid_ready"], h + 1)
                    nc.vector.tensor_scalar(wide[:, FEC + h, :], ps[:, h, :], be2[:, h:h + 1], None, add).then_inc(R["mid_kept"], 1)
                for t in range(NT):
                    v.wait_ge(R["out_ready"], t + 1)
                    o = tmp[:, t % 2, :]
                    link(nc.vector.tensor_tensor(o, ps[:, 2 + t, 0:D], bo2, add))
                    link(nc.vector.scalar_tensor_tensor(out=o, in0=o, scalar=0.3, in1=xn[:, t, :], op0=mult, op1=add))
                    last = nc.vector.scalar_tensor_tensor(out=xb[:, t, :], in0=o, scalar=gates[:, 6:7], in1=xb[:, t, :],
                                                          op0=mult, op1=add)
                link(last)

            M = {n: sem("A3_" + n) for n in ("mask_ready", "out_ready")}
            arena3_in = sem("arena3_in")
            latT = keysT[:, :, S:KEYS3]

            def jobs3(g):
                cols = slice(g * P, (g + 1) * P)

                def keys(kb):
                    def product():
                        for c in range(DC):
                            last = nc.tensor.matmul(ps[:, 7, :], wkx[:, c, cols], keysT[:, c, kb * BANK:(kb + 1) * BANK],
                                                    start=c == 0, stop=c == DC - 1)
                        return last

                    def copy():
                        for s in range(2):
                            r = slice(64 * s, 64 * s + 64)
                            last = nc.vector.tensor_copy(kH[g % 2][s][r, kb * BANK:(kb + 1) * BANK], ps[r, 7, :])
                        return last

                    return product, copy

                def vals(kb):
                    def product():
                        for i in range(4):
                            tok = slice((4 * kb + i) * P, (4 * kb + i + 1) * P)
                            for c in range(DC):
                                last = nc.tensor.matmul(ps[:, 7, i * P:(i + 1) * P], keysT[:, c, tok], wvx[:, c, cols],
                                                        start=c == 0, stop=c == DC - 1)
                        return last

                    return product, lambda: nc.vector.tensor_copy(
                        vh[g % 2][:, 4 * kb:4 * kb + 4, :], ps[:, 7, :].rearrange("p (i d) -> p i d", i=4))

                return [q_job(wqx, latT, g), keys(0), keys(1), vals(0), vals(1)]

            def prep3(pe):
                pe.wait_ge(arena3_in, 64)
                pe.wait_ge(xnT_ready, 18)

            att3 = attention(nc, sem, "a3", ps, ident, 2, HP, KEYS3 // P,
                             lambda g, s, qt: qT[g % 2][:, qt * P:(qt + 1) * P],
                             lambda g, s, kb: kH[g % 2][s][:, kb * BANK:(kb + 1) * BANK],
                             lambda g, s, kc: vh[g % 2][:, kc, s * DH2:(s + 1) * DH2], DH2, mask3[:, :],
                             ([pbuf[:, i, :] for i in range(4)], sums, recip, least,
                              work[:, :].rearrange("p (s c q) -> p s c q", s=2, c=KEYS3 // P)), wide,
                             prep=prep3, jobs=jobs3)

            def l3_tensor(pe):
                pe.wait_ge(xn_ready, 6)
                pe_turn(pe, xn, 5)
                att3[0](pe)
                pe.wait_ge(att3[3], HP)
                for t in range(NT):
                    for g in range(HP):
                        last = nc.tensor.matmul(ps[:, t, 0:D], wide[:, g, t * P:(t + 1) * P], wox[:, g, :], start=g == 0, stop=g == HP - 1)
                    last.then_inc(M["out_ready"], 1)

            def l3_scalar(act):
                for c in range(DC):
                    act.wait_ge(turned, 10 + c + 1)
                    nc.scalar.activation(latT[:, c, :], ps[:, c, :], ACT.Identity, bias=ln3[:, 3, c:c + 1],
                                         scale=ln3[:, 2, c:c + 1]).then_inc(xnT_ready, 1)
                for c in range(DC):
                    nc.scalar.activation(keysT[:, c, 0:S], ctxT[:, c, :], ACT.Identity, bias=ln3[:, 1, c:c + 1],
                                         scale=ln3[:, 0, c:c + 1]).then_inc(xnT_ready, 1)
                att3[2](act)

            def l3_vector(v, link):
                link(layernorm(nc, link, xb, xn, stats))
                layernorm(nc, link, xn, xn, stats).then_inc(xn_ready, 1)
                v.wait_ge(mask_in, 16)
                nc.vector.tensor_scalar(mask3[:, 0:S], mask_u8[:, :], 0.0, FMAX, ALU.is_equal, mult).then_inc(M["mask_ready"], 1)
                nc.vector.memset(mask3[:, S:KEYS3], 0.0).then_inc(M["mask_ready"], 1)
                v.wait_ge(M["mask_ready"], 2)
                att3[1](v)
                for t in range(NT):
                    v.wait_ge(M["out_ready"], t + 1)
                    last = nc.vector.scalar_tensor_tensor(out=xb[:, t, :], in0=ps[:, t, 0:D], scalar=gates[:, 3:4],
                                                          in1=xb[:, t, :], op0=mult, op1=add)
                link(last)

            Q = {n: sem("Q3_" + n) for n in ("out_ready", "x_ready")}
            xq = work[:, 0:NT * D].rearrange("p (t d) -> p t d", t=NT)
            amax, xscale = small[:, 0:4], small[:, 4:8]

            def q3_tensor(pe):
                pe.wait_ge(xn_ready, 7)
                pe_turn(pe, xq, 6)
                pe.wait_ge(xnT_ready, 20)
                for t in range(NT):
                    for c in range(DC):
                        last = nc.tensor.matmul(ps[:, 4 + t, 0:D], xqT[:, c, t * P:(t + 1) * P], wq3[:, c, :],
                                                start=c == 0, stop=c == DC - 1)
                    last.then_inc(Q["out_ready"], 1)

            def q3_vector(v, link):
                link(layernorm(nc, link, xb, xn, stats))
                quantise(link, xn[:, :, :], xq, NT, amax, xscale, xq).then_inc(xn_ready, 1)
                for t in range(NT):
                    v.wait_ge(Q["out_ready"], t + 1)
                    o = tmp[:, t % 2, :]
                    link(nc.vector.scalar_tensor_tensor(out=o, in0=ps[:, 4 + t, 0:D], scalar=xscale[:, t:t + 1], in1=scale3[:, :],
                                                        op0=mult, op1=mult))
                    link(nc.vector.tensor_tensor(o, o, bias3, add))
                    last = nc.vector.scalar_tensor_tensor(out=xb[:, t, :], in0=o, scalar=gates[:, 7:8], in1=xb[:, t, :],
                                                          op0=mult, op1=add)
                last.then_inc(Q["x_ready"], 1)

            mask_in, out_done = sem("mask3_in"), sem("out_done")

            @block.sync
            def _(sp):
                sp.dma_start(xb[:, :, :], x1_d[b]).then_inc(x_in, 16)
                sp.dma_start(ctxb[:, :, :], a["ctx"][b]).then_inc(ctx_in, 16)
                sp.dma_start(ctxT[:, :, :], a["ctxT"][b]).then_inc(ctx_in, 16)
                sp.dma_start(mask_u8[:, :], a["mask3"][b].partition_broadcast(P)).then_inc(mask_in, 16)
                for dst, n in ((wq2, "L2_wq"), (wk2, "L2_wk"), (wv2, "L2_wv"), (wo2, "L2_wo"), (wff1, "L2_wff1"), (wff2, "L2_wff2")):
                    sp.dma_start(dst, a[n]).then_inc(arena_in, 16)
                sp.wait_ge(xn_ready, 5)
                for dst, n in ((wqx, "L3_wq"), (wkx, "L3_wk"), (wvx, "L3_wv"), (wox, "L3_wo")):
                    sp.dma_start(dst, a[n]).then_inc(arena3_in, 16)
                sp.wait_ge(R["picked"], 1)
                e = sp.value_load(pick[0:1, 0:1], min_val=0, max_val=E2 - 1)
                for dst, n in ((we1, "L2_we1"), (we2, "L2_we2"), (be1[:, :], "L2_be1"), (be2[:, :], "L2_be2")):
                    sp.dma_start(dst, a[n][e]).then_inc(R["we_in"], 16)
                sp.wait_ge(Q["x_ready"], 1)
                sp.dma_start(out[b], xb[:, :, :]).then_inc(out_done, 16)
                sp.wait_ge(out_done, 16)

            @block.gpsimd
            def _(pool):
                nc.gpsimd.tensor_copy(idx8[:, :], slot8[:, bass.ds(b * NT, NT), :].rearrange("p t k -> p (t k)")).then_inc(idx_ready, 1)
                pool.wait_ge(idx_ready, 1)
                for t in range(NT):
                    if t >= 2:
                        pool.wait_ge(summed, t - 1)
                    for k in range(TOPK):
                        nc.gpsimd.indirect_dma_start(yg[t % 2][:, k, :], None, y_d[:, :],
                                                     bass.IndirectOffsetOnAxis(idx8[:, t * TOPK + k:t * TOPK + k + 1], 0),
                                                     bounds_check=SLOTS - 1, oob_is_err=False).then_inc(y_ins[t], 16)
                l1_pool(pool)

            @block.vector
            def _(v):
                link = Chain(v, order)
                link(nc.vector.tensor_copy(w8b[:, :, :], weight8[:, bass.ds(b * NT, NT), :]))
                v.wait_ge(x_in, 16)
                for t in range(NT):
                    v.wait_ge(y_ins[t], (b + 1) * (16 * TOPK))
                    o = tmp[:, t % 2, :]
                    link(nc.vector.tensor_scalar(o, yg[t % 2][:, 0, :], w8b[:, t, 0:1], None, mult))
                    for k in range(1, TOPK):
                        last = nc.vector.scalar_tensor_tensor(out=o, in0=yg[t % 2][:, k, :], scalar=w8b[:, t, k:k + 1], in1=o,
                                                              op0=mult, op1=add)
                        if k < TOPK - 1:
                            link(last)
                    last.then_inc(summed, 1)
                    v.wait_ge(summed, t + 1)
                    last = nc.vector.scalar_tensor_tensor(out=xb[:, t, :], in0=o, scalar=gates[:, 4:5], in1=xb[:, t, :],
                                                          op0=mult, op1=add)
                link(last)
                layernorm(nc, link, xb, xn, stats).then_inc(xn_ready, 1)
                l1_vector(v, link)
                f1_vector(v, link)
                l2_vector(v, link)
                r2_vector(v, link)
                l3_vector(v, link)
                q3_vector(v, link)

            @block.tensor
            def _(pe):
                l1_tensor(pe)
                f1_tensor(pe)
                l2_tensor(pe)
                r2_tensor(pe)
                l3_tensor(pe)
                q3_tensor(pe)

            @block.scalar
            def _(act):
                l1_scalar(act)
                f1_scalar(act)
                l2_scalar(act)
                r2_scalar(act)
                l3_scalar(act)
                keep_turned(act, 6, xqT, 12)


def kernel(**inputs):
    import numpy as _np
    import concourse.bacc as _bacc
    from concourse import mybir as _mybir
    from concourse.bass_utils import run_bass_kernel_spmd as _run

    i = {k: _np.asarray(v) for k, v in inputs.items()}

    def rows(w):
        return w.reshape(-1, P, w.shape[1]).transpose(1, 0, 2)

    def cols(v):
        return v.reshape(-1, P).T

    def tiles(x):
        return x.reshape(B, NT, P, D).transpose(0, 2, 1, 3)

    def heads_padded(w):
        z = _np.zeros((H0, HPAD) + w.shape[1:], w.dtype)
        z[:, :DK0] = w.reshape((H0, DK0) + w.shape[1:])
        return z.reshape((H0 * HPAD,) + w.shape[1:])

    consts = _np.zeros((P, 4, P), _np.float32)
    consts[:, 0] = _np.eye(P)
    consts[:, 1] = _np.triu(_np.ones((P, P)), 1)
    consts[:, 2] = 1
    e = _np.arange(E)
    consts[:, 3, :E] = (e % 2) * CAP * PAIRS + e // 2 + 1
    minus1 = _np.zeros((H1, H1, P), _np.float32)
    for h in range(H1):
        minus1[h, h] = -1
    gw1 = _np.zeros((3 * D, 36), _np.float32)
    gw1[:, 0:H1] = i["L1_xattn_igate_w"].T
    gw1[:, 32:36] = i["L1_xattn_fgate_w"].T
    gb1 = _np.zeros((36, 1), _np.float32)
    gb1[0:H1, 0] = i["L1_xattn_igate_b"]
    gb1[32:36, 0] = i["L1_xattn_fgate_b"]
    w_gate, w_up = (i["L0_ffn_" + n].reshape(PAIRS, 2, INTER, DC, P).transpose(0, 4, 3, 1, 2) for n in ("w_gate", "w_up"))
    wkv2, wkv3 = i["L2_xattn_Wkv"], i["L3_xattn_Wkv"]
    arrays = {
        "consts": consts,
        "gates": _np.concatenate([i["g_xattn"], i["g_ffn"]]),
        "vec": _np.stack([i["L0_xattn_bo"], i["L1_xattn_out_w"], i["L1_ffn_b2"], i["L2_ffn_bo"], i["L3_ffn_bias"]]),
        "block16": _np.repeat(_np.eye(P // DK0, dtype=_np.float32), DK0, axis=0),
        "token": _np.arange(S, dtype=_np.float32).reshape(NT, P).T,
        "place_none": SLOTS + _np.arange(SLOTS, dtype=_np.uint32).reshape(P, NT, TOPK),
        "minus1": minus1,
        "earlier": (_np.arange(7 * P)[None] < 3 * P + _np.arange(P)[:, None]).astype(_np.float32),
        "x": tiles(i["x"]),
        "ctx": tiles(i["ctx_1024"]),
        "ctxT": i["ctx_1024"].transpose(0, 2, 1).reshape(B, DC, P, S).transpose(0, 2, 1, 3),
        "mask0": i["mask_BxS2_if1"],
        "mask3": i["mask_BxS2_bk0"],
        "L0_wq": rows(i["L0_xattn_Wq"].T),
        "L0_wk": rows(i["L0_xattn_Wk"].T),
        "L0_wv": rows(heads_padded(i["L0_xattn_Wv"]).T),
        "L0_wo": rows(heads_padded(i["L0_xattn_Wo"].T)),
        "L0_bqk": _np.stack([cols(i["L0_xattn_bq"]), cols(i["L0_xattn_bk"])], axis=1),
        "L0_bv": heads_padded(i["L0_xattn_bv"]),
        "L0_gate": rows(i["L0_ffn_gate_w"].T),
        "L0_wgu": _np.concatenate([w_gate, w_up], axis=4),
        "L0_wd": i["L0_ffn_w_down"].reshape(PAIRS, 2, D, 2, IH).transpose(0, 4, 3, 1, 2),
        "L1_gw": rows(gw1),
        "L1_gb": gb1,
        "L1_wr": _np.repeat(cols(i["L1_ffn_w_router"])[:, :, None], P, axis=2),
        "L1_w1": rows(i["L1_ffn_W1"]),
        "L1_b1": cols(i["L1_ffn_b1"]),
        "L1_w2": rows(i["L1_ffn_W2"]),
        "L2_ln": _np.stack([cols(i["L2_xattn_" + n]) for n in ("ln_g", "ln_b", "cln_g", "cln_b")], axis=1),
        "L2_wq": rows(i["L2_xattn_Wq"]),
        "L2_wk": rows(_np.concatenate([wkv2[:, :DH2], wkv2[:, :DH2]], axis=1)),
        "L2_wv": rows(wkv2[:, DH2:]),
        "L2_wo": rows(i["L2_xattn_Wo"]),
        "L2_wff1": rows(i["L2_xattn_Wff1"]),
        "L2_wff2": rows(i["L2_xattn_Wff2"]),
        "L2_wp1": rows(i["L2_ffn_Wp1"]),
        "L2_bp1": cols(i["L2_ffn_bp1"]),
        "L2_wp2": i["L2_ffn_Wp2"],
        "L2_bp2": i["L2_ffn_bp2"][None],
        "L2_we1": i["L2_ffn_W1"].reshape(E2, DC, P, FE2).transpose(0, 2, 1, 3),
        "L2_be1": i["L2_ffn_b1"].reshape(E2, FEC, P).transpose(0, 2, 1),
        "L2_we2": i["L2_ffn_W2"].reshape(E2, FEC, P, D).transpose(0, 2, 1, 3),
        "L2_be2": i["L2_ffn_b2"].reshape(E2, DC, P).transpose(0, 2, 1),
        "L2_wof": rows(i["L2_ffn_Wo"]),
        "L3_ln": _np.stack([cols(i["L3_xattn_" + n]) for n in ("g1", "b1", "g2", "b2")], axis=1),
        "L3_wq": rows(i["L3_xattn_Wq"]),
        "L3_wk": rows(wkv3[:, :INNER]),
        "L3_wv": rows(wkv3[:, INNER:]),
        "L3_wo": rows(i["L3_xattn_Wout"]),
        "L3_w": i["L3_ffn_weight"].reshape(DC, P, D).transpose(1, 0, 2),
    }
    nc = _bacc.Bacc("TRN2", target_bir_lowering=False, num_devices=1)
    feed, aps = {}, {}
    for name, arr in arrays.items():
        arr = _np.ascontiguousarray(arr)
        feed[f"in_{name}"] = arr
        aps[name] = nc.dram_tensor(f"in_{name}", arr.shape, _mybir.dt.from_np(arr.dtype), kind="ExternalInput").ap()
    out = nc.dram_tensor("out_0", (B, P, NT, D), F32, kind="ExternalOutput").ap()
    program(nc, aps, out)
    r = _run(nc, [feed], core_ids=[0])
    return r.results[0]["out_0"].reshape(B, P, NT, D).transpose(0, 2, 1, 3).reshape(B, S, D)
```

```python
from contextlib import ExitStack, contextmanager

import concourse.bass as bass
import numpy as np
from concourse import mybir

F32 = mybir.dt.float32
BF16 = mybir.dt.bfloat16
I32 = mybir.dt.int32
U32 = mybir.dt.uint32
ALU = mybir.AluOpType
ACT = mybir.ActivationFunctionType
AX = mybir.AxisListType

P = 128
B, S, D = 4, 512, 256
NT = S // P
DC = D // P
TOK = B * S
BANK = 512
LN_EPS = 1e-5

H0, DK0 = 16, 16
HPAD = 32
QUADS = H0 * HPAD // P
E, TOPK, CAP, INTER = 64, 8, 64, 192
PAIRS = E // 2
IH = INTER // 2
SLOTS = E * CAP
H1, DH1 = 4, 64
F1 = 1024
FC1 = F1 // P
KEEP = S // 2
H2, DH2 = 16, 64
INNER = H2 * DH2
HP = H2 // 2
FF2 = 4 * D
FFC = FF2 // P
NAV, E2, FE2 = 128, 8, 512
FEC = FE2 // P
KEYS3 = 2 * S
QMAX = 127.0
ROUND = 12582912.0
RSQRT_BITS, RSQRT_STEPS = 1597463007.0, 3
NEG1E9, FMAX = 1.0e9, float(np.finfo(np.float32).max)

mult, add, subtract = ALU.mult, ALU.add, ALU.subtract


class Chain:

    def __init__(self, eng, sem):
        self.eng, self.sem, self.n = eng, sem, 0

    def __call__(self, ins):
        self.n += 1
        ins.then_inc(self.sem, 1)
        self.eng.wait_ge(self.sem, self.n)


def layernorm_steps(nc, link, src, dst, stats, tiles=NT, twice=False):
    s6, mv, rstd, var, half = (x[:, 0:tiles] for x in stats)
    for t in range(tiles):
        last = nc.vector.bn_stats(s6[:, t, :], src[:, t, :])
        if t == tiles // 2 - 1:
            yield last
    link(last)
    yield last
    for t in range(tiles):
        last = nc.vector.bn_aggr(mv[:, t, :], s6[:, t, :])
    link(last)

    def rsqrt():
        link(nc.vector.tensor_scalar(rstd.bitcast(I32), var.bitcast(I32), -0.5, RSQRT_BITS, mult, add))
        for _ in range(RSQRT_STEPS):
            link(nc.vector.tensor_tensor(half, var, rstd, mult))
            link(nc.vector.scalar_tensor_tensor(out=half, in0=half, scalar=-0.5, in1=rstd, op0=mult, op1=mult))
            link(nc.vector.scalar_tensor_tensor(out=rstd, in0=half, scalar=1.5, in1=rstd, op0=add, op1=mult))
            yield last

    link(nc.vector.tensor_scalar(var, mv[:, :, 1], LN_EPS, None, add))
    yield from rsqrt()
    if twice:
        first = mv[:, :, 1]
        link(nc.vector.tensor_tensor(half, mv[:, :, 1], rstd, mult))
        link(nc.vector.tensor_tensor(var, half, rstd, mult))
        nc.vector.tensor_copy(first, rstd)
        link(nc.vector.tensor_scalar(var, var, LN_EPS, None, add))
        yield last
        yield from rsqrt()
        link(nc.vector.tensor_tensor(rstd, rstd, first, mult))
    for t in range(tiles):
        last = nc.vector.tensor_scalar(dst[:, t, :], src[:, t, :], mv[:, t, 0:1], rstd[:, t:t + 1],
                                       subtract, mult)
        if t == tiles // 2 - 1:
            yield last
    yield last


def layernorm(*args, **kwargs):
    for last in layernorm_steps(*args, **kwargs):
        pass
    return last


def quantise(nc, link, src, tiles, amax, scale):
    link(nc.vector.tensor_reduce(amax, src, AX.X, ALU.max, apply_absolute_value=True))
    yield None
    link(nc.vector.tensor_scalar(scale, amax, 1e-8, 1.0 / QMAX, ALU.max, mult))
    link(nc.vector.reciprocal(amax, scale))
    yield None
    for t in range(tiles):
        last = nc.vector.tensor_scalar(src[:, t, :], src[:, t, :], amax[:, t:t + 1], ROUND, mult, add)
        if t == tiles // 2 - 1:
            yield None
    link(last)
    yield None
    link(nc.vector.tensor_scalar(src, src, ROUND, QMAX, subtract, ALU.min))
    yield None
    yield nc.vector.tensor_scalar(src, src, -QMAX - 1, None, ALU.max)


def attention(nc, sem, name, ps, ident, heads, groups, nk, q_of, k_of, v_of, rows, mask, bufs, out,
              jobs=None):
    banks = nk // 4
    ring = 4 // banks
    probs, sums, recip, least, pt = bufs
    np_ = len(probs)
    per = NT * heads
    steps = groups * per
    scores_ready = sem(name + "_scores_ready")
    least_ready = sem(name + "_least_ready")
    exp_ready = sem(name + "_exp_ready")
    probs_ready = sem(name + "_probs_ready")
    turned = sem(name + "_turned")
    turned_kept = sem(name + "_turned_kept")
    av_ready = sem(name + "_av_ready")
    av_kept = sem(name + "_av_kept")
    recip_ready = sem(name + "_recip_ready")
    jobs_ready = sem(name + "_jobs_ready")
    jobs_kept = sem(name + "_jobs_kept")

    def where(n):
        g, r = divmod(n, per)
        return g, r // heads, r % heads

    def scores(n):
        return ps[:, (n % ring) * banks:(n % ring + 1) * banks, :].rearrange("p b k -> p (b k)")

    each = len(jobs(0)) if jobs else 0

    def plan(background):
        before, need, count = {}, [0], 0
        for n in range(steps):
            g, i = divmod(n, per)
            own = jobs(g + 1)[i:i + 1] if jobs and g + 1 < groups else []
            before[n] = own + background.get(n, [])
            count += sum(job[0] is not None for job in before[n])
            if own and i == each - 1:
                need.append(count - sum(job[0] is not None for job in background.get(n, [])))
        return before, need, count

    def tensor(pe, background={}):
        before, need, _ = plan(background)
        done = [0]

        def project(job):
            if job[0] is None:
                return
            if done[0]:
                pe.wait_ge(jobs_kept, done[0])
            job[0](pe).then_inc(jobs_ready, 1)
            done[0] += 1

        def score(n):
            g, qt, s = where(n)
            if jobs and n % per == 0 and need[g]:
                pe.wait_ge(jobs_kept, need[g])
            if n >= ring:
                pe.wait_ge(exp_ready, n - ring + 1)
            for kb in range(banks):
                last = nc.tensor.matmul(scores(n)[:, kb * BANK:(kb + 1) * BANK], q_of(g, s, qt),
                                        k_of(g, s, kb), start=True, stop=True)
            last.then_inc(scores_ready, 1)

        def turn(n):
            pe.wait_ge(probs_ready, n + 1)
            for kb in range(banks):
                m = n * banks + kb
                if m >= 2:
                    pe.wait_ge(turned_kept, m - 1)
                for c in range(4):
                    kc = kb * 4 + c
                    last = nc.tensor.transpose(ps[:, 4 + m % 2, c * P:(c + 1) * P],
                                               probs[n % np_][:, kc * P:(kc + 1) * P], ident)
                last.then_inc(turned, 1)

        def values(g):
            pe.wait_ge(turned_kept, (g + 1) * per * banks)
            if g:
                pe.wait_ge(av_kept, g)
            for kc in range(nk):
                for s in range(heads):
                    last = nc.tensor.matmul(ps[rows * s:rows * (s + 1), 6, :], v_of(g, s, kc),
                                            pt[:, s, kc, :], start=kc == 0, stop=kc == nk - 1)
            last.then_inc(av_ready, 1)

        for n in range(ring):
            score(n)
        for n in range(steps):
            if n + ring < steps:
                score(n + ring)
            turn(n)
            for job in before[n]:
                project(job)
            if n % per == 0 and n:
                values(n // per - 1)
        values(groups - 1)

    def vector(v, background={}):
        before, _, _ = plan(background)
        done = [0]

        def keep_job(job):
            if job[0] is None:
                job[1](v)
                return
            v.wait_ge(jobs_ready, done[0] + 1)
            job[1](v).then_inc(jobs_kept, 1)
            done[0] += 1

        def find(n):
            v.wait_ge(scores_ready, n + 1)
            x = scores(n)
            if mask is None:
                nc.vector.tensor_reduce(least[:, n % 8:n % 8 + 1], x, AX.X, ALU.min).then_inc(least_ready, 1)
            else:
                nc.vector.tensor_tensor_reduce(out=x, in0=x, in1=mask, scale=1.0, scalar=FMAX, op0=add,
                                               op1=ALU.min, accum_out=least[:, n % 8:n % 8 + 1])\
                    .then_inc(least_ready, 1)

        def divide(n):
            v.wait_ge(exp_ready, n + 1)
            nc.vector.reciprocal(recip[:, n % 8:n % 8 + 1], sums[:, n % 8:n % 8 + 1]).then_inc(recip_ready, 1)
            v.wait_ge(recip_ready, n + 1)
            p = probs[n % np_]
            nc.vector.tensor_scalar(p, p, recip[:, n % 8:n % 8 + 1], None, mult).then_inc(probs_ready, 1)

        def keep_values(g):
            v.wait_ge(av_ready, g + 1)
            nc.vector.tensor_copy(out[:, g, :], ps[:, 6, :]).then_inc(av_kept, 1)

        for n in range(steps + 1):
            if n < steps:
                find(n)
            if n:
                divide(n - 1)
            for job in before[n - 2] if n >= 2 else []:
                keep_job(job)
            if n % per == 3 and n > per:
                keep_values(n // per - 1)
        for job in before[steps - 1]:
            keep_job(job)
        keep_values(groups - 1)

    def scalar(act):
        def exponent(n):
            act.wait_ge(least_ready, n + 1)
            if n >= np_:
                act.wait_ge(turned, (n - np_ + 1) * banks)
            nc.scalar.activation(probs[n % np_], scores(n), ACT.Exp, bias=least[:, n % 8:n % 8 + 1],
                                 scale=-1.0, accum_out=sums[:, n % 8:n % 8 + 1]).then_inc(exp_ready, 1)

        def keep_turned(n):
            g, qt, s = where(n)
            if n % per == 0 and g:
                act.wait_ge(av_ready, g)
            for kb in range(banks):
                m = n * banks + kb
                act.wait_ge(turned, m + 1)
                nc.scalar.activation(pt[:, s, kb * 4:kb * 4 + 4, qt * P:(qt + 1) * P],
                                     ps[:, 4 + m % 2, :].rearrange("p (c q) -> p c q", c=4),
                                     ACT.Copy).then_inc(turned_kept, 1)

        for n in range(steps + 1):
            if n < steps:
                exponent(n)
            if n:
                keep_turned(n - 1)

    return tensor, vector, scalar, av_kept, jobs_kept, plan


def program(nc, a, out):
    ctx = ExitStack()
    with ctx:
        every = []

        def sem(name, scope=ctx):
            s = scope.enter_context(nc.semaphore(name))
            every.append(s)
            return s

        def keep(name, shape, dt=F32):
            return ctx.enter_context(nc.sbuf_tensor(name, shape, dt))

        @contextmanager
        def zeroed(since):
            yield
            nums = sorted(s.num for s in every[since:])
            starts = [n for n in nums if n - 1 not in nums]
            ends = [n + 1 for n in nums if n + 1 not in nums]
            for start, end in zip(starts, ends):
                nc.sync.sem_clear(range(start, end))
            nc.all_engine_barrier()

        x_d = nc.dram_tensor("x_scratch", [B, P, NT, D], F32, kind="Internal").ap()
        rows_d = nc.dram_tensor("normed_rows", [TOK + P, D], F32, kind="Internal").ap()
        taken_all = nc.dram_tensor("slot_token", [2 * SLOTS, 1], U32, kind="Internal").ap()
        taken_d = taken_all[0:SLOTS, :]
        y_d = nc.dram_tensor("expert_rows", [SLOTS, D], F32, kind="Internal").ap()

        ps = ctx.enter_context(nc.psum_tensor("ps", [P, 8, BANK], F32))
        consts = keep("consts", [P, 4, P])
        gates = keep("gates", [P, 8])
        vec = keep("vec", [P, 5, D])
        wq3 = keep("wq3f", [P, DC, D], BF16)
        scale3 = keep("scale3f", [P, D])
        slot8 = keep("slot8", [P, B * NT, TOPK], U32)
        weight8 = keep("weight8", [P, B * NT, TOPK])
        taken = keep("taken", [P, PAIRS], U32)
        place8 = keep("place8", [P, NT, TOPK], U32)
        token_i = keep("token_i", [P, NT], U32)
        ident, upper, ones = consts[:, 0, :], consts[:, 1, :], consts[:, 2, :]
        keyrow = consts[:, 3, 0:E]
        bo0, outw1, b21, bo2, bias3 = (vec[:, i, :] for i in range(5))
        xb = keep("xb", [P, NT, D])
        xn = keep("xn", [P, NT, D])
        xnT = keep("xnT", [P, DC, S])
        ctxT = keep("ctxT", [P, DC, S])
        s6 = keep("s6", [P, 16, 6])
        mv = keep("mv", [P, 16, 2])
        stats = (s6, mv, keep("rstd", [P, 16]), keep("var", [P, 16]), keep("half", [P, 16]))
        least = keep("least", [P, 8])
        sums = keep("sums", [P, 8])
        recip = keep("recip", [P, 8])
        tmp = keep("tmp", [P, 2, D])

        consts_in = sem("consts_in")
        scattered = sem("scattered")
        gates_ready = sem("gates_ready")
        fill_ready = sem("fill_ready")
        fill_out = sem("fill_out")

        with nc.sbuf_tensor("zero_rows", [P, D], F32) as zero_rows, \
                nc.sbuf_tensor("no_token", [P, PAIRS], U32) as no_token, nc.Block() as block:
            @block.sync
            def _(sp):
                sp.dma_start(consts[:, :, :], a["consts"]).then_inc(consts_in, 16)
                sp.dma_start(gates[:, :], a["gates"].partition_broadcast(P)).then_inc(consts_in, 16)
                sp.dma_start(vec[:, :, :], a["vec"].partition_broadcast(P)).then_inc(consts_in, 16)
                sp.wait_ge(fill_ready, 2)
                sp.dma_start(rows_d[TOK:TOK + P, :], zero_rows[:, :]).then_inc(fill_out, 16)
                sp.dma_start(taken_d.rearrange("(p n) o -> p (n o)", p=P), no_token[:, :]).then_inc(fill_out, 16)
                sp.wait_ge(fill_out, 32)
                sp.wait_ge(consts_in, 48)

            @block.vector
            def _(v):
                nc.vector.memset(zero_rows[:, :], 0.0).then_inc(fill_ready, 1)
                nc.vector.memset(no_token[:, :], TOK).then_inc(fill_ready, 1)

            @block.scalar
            def _(act):
                act.wait_ge(consts_in, 48)
                nc.scalar.activation(gates[:, :], gates[:, :], ACT.Tanh).then_inc(gates_ready, 1)
                act.wait_ge(gates_ready, 1)

        def scatter():
            for t in range(NT):
                for k in range(TOPK):
                    nc.gpsimd.indirect_dma_start(
                        taken_all[:, :], bass.IndirectOffsetOnAxis(place8[:, t, k:k + 1], 0), token_i[:, t:t + 1], None,
                        bounds_check=2 * SLOTS - 1, oob_is_err=False).then_inc(scattered, 16)

        layer0(nc, a, sem, every, zeroed, locals())
        with ExitStack() as scope:
            shared1 = layer1_weights(nc, scope)
            experts(nc, a, sem, locals())
            layer1(nc, a, sem, every, zeroed, locals())
        layers2to3(nc, a, sem, every, zeroed, locals(), out)


def layer0(nc, a, allocate, every, zeroed, G):
    ps, ident, upper, ones, keyrow = G["ps"], G["ident"], G["upper"], G["ones"], G["keyrow"]
    gates, bo0, slot8, weight8 = G["gates"], G["bo0"], G["slot8"], G["weight8"]
    xb, xn, xnT, ctxT, stats, tmp = G["xb"], G["xn"], G["xnT"], G["ctxT"], G["stats"], G["tmp"]
    least, sums, recip = G["least"], G["sums"], G["recip"]
    x_d, rows_d = G["x_d"], G["rows_d"]
    place8, token_i, scattered, scatter = G["place8"], G["token_i"], G["scattered"], G["scatter"]
    with ExitStack() as ctx:
        def keep(name, shape, dt=F32):
            return ctx.enter_context(nc.sbuf_tensor(name, shape, dt))

        def sem(name):
            return allocate(name, ctx)

        wq = keep("wq0", [P, DC, D])
        wk = keep("wk0", [P, DC, D])
        wv = keep("wv0", [P, DC, H0 * HPAD])
        wo = keep("wo0", [P, QUADS, D])
        wgate = keep("wgate0", [P, DC, E])
        bqk = keep("bqk0", [P, 2, DC])
        bv = keep("bv0", [P, H0 * HPAD])
        block16 = keep("block16", [P, P // DK0])
        mask_i = keep("mask_i", [P, S], I32)
        mask_f = keep("mask_f", [P, S])
        mask_add = keep("mask_add", [P, S])
        qT = keep("qT0", [P, DC, S])
        kT = keep("kT0", [P, DC, S])
        kH = keep("kH0", [P, H0, S])
        vh = keep("v0", [P, NT, H0 * HPAD])
        probs = [keep(f"probs0_{i}", [P, S])[:, :] for i in range(6)]
        pt = keep("pt0", [P, 4, NT, S])
        oT = keep("oT0", [P, QUADS, S])
        lg = keep("lg", [P, NT, E])
        rep = keep("rep", [P, NT, E])
        sel = keep("sel", [P, NT, E])
        ex = keep("ex", [P, NT, E])
        valid = keep("valid", [P, NT, E])
        key = keep("key", [P, NT, E])
        before = keep("before", [P, NT + 1, E])
        m8 = keep("m8", [P, NT, TOPK])
        e8 = keep("e8", [P, NT, TOPK])
        k8 = keep("k8", [P, NT, TOPK])
        w8 = keep("w8", [P, NT, TOPK])
        off8 = keep("off8", [P, NT, TOPK])
        negm = keep("negm", [P, NT])
        s8 = keep("s8", [P, NT])
        r8 = keep("r8", [P, NT])
        junk = keep("junk0", [P, NT * TOPK, E])
        token_f = keep("token_f", [P, NT])

        w_in = allocate("w0_in")
        before_zero = allocate("before_zero")
        with nc.Block() as block:
            @block.sync
            def _(sp):
                for dst, n in ((wq, "L0_wq"), (wk, "L0_wk"), (wv, "L0_wv"), (wo, "L0_wo"), (wgate, "L0_gate")):
                    sp.dma_start(dst[:, :, :], a[n]).then_inc(w_in, 16)
                sp.dma_start(bqk[:, :, :], a["L0_bqk"]).then_inc(w_in, 16)
                sp.dma_start(bv[:, :], a["L0_bv"].partition_broadcast(P)).then_inc(w_in, 16)
                sp.dma_start(block16[:, :], a["block16"]).then_inc(w_in, 16)
                sp.dma_start(token_f[:, :], a["token"]).then_inc(w_in, 16)
                sp.dma_start(place8[:, :, :], a["place_none"]).then_inc(w_in, 16)
                sp.wait_ge(w_in, 10 * 16)

            @block.vector
            def _(v):
                nc.vector.memset(before[:, 0, :], 0.0).then_inc(before_zero, 1)
                nc.vector.memset(token_i[:, :], 0).then_inc(before_zero, 1)
                v.wait_ge(before_zero, 2)

        since = len(every)
        x_in, ctxT_in, mask_in = sem("x0_in"), sem("ctxT0_in"), sem("mask0_in")
        order = sem("dve_order0")
        mask_ready = sem("mask0_ready")
        xn_ready = sem("xn0_ready")
        turned = sem("xn0_turned")
        xnT_ready = sem("xnT0_ready")
        prep_ready = sem("prep0_ready")
        prep_kept = sem("prep0_kept")
        out_ready = sem("out0_ready")
        rows_out = sem("rows0_out")
        logits_ready = sem("logits_ready")
        chosen = sem("chosen")
        exps = sem("exps0")
        before_ready = sem("before_ready")
        pos_ready = sem("pos_ready")
        placed = sem("placed")

        NPREP = 2 * DC + NT
        with nc.Fori(0, B) as b, zeroed(since), nc.Block() as block:
            def q_of(g, s, qt):
                return qT[:, (4 * g + s) // 8, qt * P:(qt + 1) * P]

            def k_of(g, s, kb):
                return kH[:, 4 * g + s, :]

            def v_of(g, s, kc):
                h = 4 * g + s
                return vh[:, kc, h * HPAD:(h + 1) * HPAD]

            att = attention(nc, sem, "a0", ps, ident, 4, QUADS, NT, q_of, k_of, v_of, HPAD, mask_add[:, :],
                            (probs, sums, recip, least, pt), oT)

            @block.sync
            def _(sp):
                sp.dma_start(xb[:, :, :], a["x"][b]).then_inc(x_in, 16)
                sp.dma_start(ctxT[:, :, :], a["ctxT"][b]).then_inc(ctxT_in, 16)
                sp.dma_start(mask_i[:, :], a["mask0"][b].partition_broadcast(P)).then_inc(mask_in, 16)
                sp.wait_ge(xn_ready, 2)
                sp.dma_start(x_d[b], xb[:, :, :]).then_inc(rows_out, 16)
                sp.dma_start(rows_d[0:TOK, :].rearrange("(b t p) d -> b p t d", b=B, t=NT)[b],
                             xn[:, :, :]).then_inc(rows_out, 16)
                sp.wait_ge(rows_out, 32)

            @block.tensor
            def _(pe):
                def turn(k):
                    pe.wait_ge(xn_ready, k + 1)
                    for c in range(DC):
                        for t in range(NT):
                            last = nc.tensor.transpose(ps[:, c, t * P:(t + 1) * P],
                                                       xn[:, t, c * P:(c + 1) * P], ident)
                        last.then_inc(turned, 1)

                def prep(i, dst, pairs):
                    if i >= 4:
                        pe.wait_ge(prep_kept, i - 3)
                    for n, (l, r) in enumerate(pairs):
                        last = nc.tensor.matmul(dst, l, r, start=n == 0, stop=n == len(pairs) - 1)
                    last.then_inc(prep_ready, 1)

                pe.wait_ge(ctxT_in, 16)
                for i in range(DC):
                    prep(i, ps[:, 2 + i % 4, :], [(wk[:, c, i * P:(i + 1) * P], ctxT[:, c, :]) for c in range(DC)])
                for t in range(NT):
                    i = DC + t
                    prep(i, ps[:, 2 + i % 4, :], [(ctxT[:, c, t * P:(t + 1) * P], wv[:, c, :]) for c in range(DC)])
                turn(0)
                for j in range(DC):
                    i = DC + NT + j
                    if j == 0:
                        pe.wait_ge(xnT_ready, DC)
                    prep(i, ps[:, 2 + i % 4, :], [(wq[:, c, j * P:(j + 1) * P], xnT[:, c, :]) for c in range(DC)])
                pe.wait_ge(prep_kept, NPREP + 1)
                att[0](pe)
                pe.wait_ge(att[3], QUADS)
                for t in range(NT):
                    for g in range(QUADS):
                        last = nc.tensor.matmul(ps[:, t, 0:D], oT[:, g, t * P:(t + 1) * P], wo[:, g, :],
                                                start=g == 0, stop=g == QUADS - 1)
                    last.then_inc(out_ready, 1)
                turn(1)
                pe.wait_ge(xnT_ready, 2 * DC)
                for t in range(NT):
                    for c in range(DC):
                        last = nc.tensor.matmul(ps[:, 7, t * E:(t + 1) * E], xnT[:, c, t * P:(t + 1) * P],
                                                wgate[:, c, :], start=c == 0, stop=c == DC - 1)
                last.then_inc(logits_ready, 1)
                pe.wait_ge(before_ready, 1)
                for t in range(NT):
                    nc.tensor.matmul(ps[:, 6, t * E:(t + 1) * E], upper, sel[:, t, :], start=True, stop=False)
                    last = nc.tensor.matmul(ps[:, 6, t * E:(t + 1) * E], ones, before[:, t, :], start=False, stop=True)
                last.then_inc(pos_ready, 1)

            @block.scalar
            def _(act):
                def keep_turned(k):
                    for c in range(DC):
                        act.wait_ge(turned, k * DC + c + 1)
                        nc.scalar.activation(xnT[:, c, :], ps[:, c, :], ACT.Copy).then_inc(xnT_ready, 1)

                keep_turned(0)
                att[2](act)
                keep_turned(1)
                act.wait_ge(chosen, 1)
                for t in range(NT):
                    nc.scalar.activation(ex[:, t, :], lg[:, t, :], ACT.Exp, bias=negm[:, t:t + 1])
                    last = nc.scalar.activation(e8[:, t, :], m8[:, t, :], ACT.Exp, bias=negm[:, t:t + 1],
                                                accum_out=s8[:, t:t + 1])
                last.then_inc(exps, 1)

            @block.vector
            def _(v):
                link = Chain(v, order)
                v.wait_ge(x_in, 16)
                layernorm(nc, link, xb, xn, stats).then_inc(xn_ready, 1)
                v.wait_ge(mask_in, 16)
                link(nc.vector.tensor_scalar(mask_f[:, :], mask_i[:, :], 0.0, None, ALU.not_equal))
                nc.vector.tensor_scalar(mask_add[:, :], mask_f[:, :], -NEG1E9, NEG1E9, mult, add).then_inc(mask_ready, 1)
                for i in range(DC):
                    v.wait_ge(prep_ready, i + 1)
                    nc.vector.scalar_tensor_tensor(out=kT[:, i, :], in0=ps[:, 2 + i % 4, :], scalar=bqk[:, 1, i:i + 1],
                                                   in1=mask_f[:, :], op0=add, op1=mult).then_inc(prep_kept, 1)
                for t in range(NT):
                    i = DC + t
                    v.wait_ge(prep_ready, i + 1)
                    nc.vector.tensor_tensor(vh[:, t, :], ps[:, 2 + i % 4, :], bv[:, :], add).then_inc(prep_kept, 1)
                for j in range(DC):
                    i = DC + NT + j
                    v.wait_ge(prep_ready, i + 1)
                    nc.vector.tensor_scalar(qT[:, j, :], ps[:, 2 + i % 4, :], bqk[:, 0, j:j + 1], -DK0 ** -0.5,
                                            add, mult).then_inc(prep_kept, 1)
                v.wait_ge(prep_kept, NPREP)
                v.wait_ge(mask_ready, 1)
                for h in range(H0):
                    last = nc.vector.tensor_scalar(kH[:, h, :], kT[:, h // 8, :], block16[:, h % 8:h % 8 + 1], None, mult)
                last.then_inc(prep_kept, 1)
                att[1](v)
                for t in range(NT):
                    v.wait_ge(out_ready, t + 1)
                    link(nc.vector.tensor_tensor(tmp[:, t % 2, :], ps[:, t, 0:D], bo0, add))
                    last = nc.vector.scalar_tensor_tensor(out=xb[:, t, :], in0=tmp[:, t % 2, :], scalar=gates[:, 0:1],
                                                          in1=xb[:, t, :], op0=mult, op1=add)
                link(last)
                layernorm(nc, link, xb, xn, stats).then_inc(xn_ready, 1)
                v.wait_ge(logits_ready, 1)
                link(nc.vector.tensor_copy(lg[:, :, :], ps[:, 7, 0:NT * E].rearrange("p (t e) -> p t e", t=NT)))
                for t in range(NT):
                    last = nc.vector.max(m8[:, t, :], lg[:, t, :])
                link(last)
                nc.vector.tensor_scalar(negm[:, :], m8[:, :, 0], -1.0, None, mult).then_inc(chosen, 1)
                for t in range(NT):
                    last = nc.vector.match_replace(rep[:, t, :], m8[:, t, :], lg[:, t, :], -FMAX)
                link(last)
                link(nc.vector.tensor_tensor(sel[:, :, :], rep[:, :, :], lg[:, :, :], ALU.not_equal))
                for t in range(NT):
                    last = nc.vector.tensor_tensor(before[:, t + 1, :], before[:, t, :], sel[:, t, :], add)
                    if t < NT - 1:
                        link(last)
                last.then_inc(before_ready, 1)
                v.wait_ge(exps, 1)
                link(nc.vector.reciprocal(r8[:, :], s8[:, :]))
                for t in range(NT):
                    last = nc.vector.scalar_tensor_tensor(out=ex[:, t, :], in0=ex[:, t, :], scalar=r8[:, t:t + 1],
                                                          in1=sel[:, t, :], op0=mult, op1=mult)
                link(last)
                v.wait_ge(pos_ready, 1)
                pos = ps[:, 6, 0:NT * E].rearrange("p (t e) -> p t e", t=NT)
                nc.vector.scalar_tensor_tensor(out=valid[:, :, :], in0=pos, scalar=float(CAP), in1=sel[:, :, :],
                                               op0=ALU.is_lt, op1=mult)
                for t in range(NT):
                    last = nc.vector.scalar_tensor_tensor(out=key[:, t, :], in0=pos[:, t, :], scalar=float(PAIRS),
                                                          in1=keyrow, op0=mult, op1=add)
                nc.vector.tensor_copy(before[:, 0, :], before[:, NT, :])
                link(last)
                nc.vector.tensor_tensor(ex[:, :, :], ex[:, :, :], valid[:, :, :], mult)
                link(nc.vector.tensor_tensor(key[:, :, :], key[:, :, :], valid[:, :, :], mult))
                for t in range(NT):
                    last = nc.vector.max(k8[:, t, :], key[:, t, :])
                link(last)
                for t in range(NT):
                    for k in range(TOPK):
                        last = nc.vector.scalar_tensor_tensor(out=junk[:, t * TOPK + k, :], in0=key[:, t, :], scalar=k8[:, t, k:k + 1],
                                                              in1=ex[:, t, :], op0=ALU.is_equal, op1=mult,
                                                              accum_out=w8[:, t, k:k + 1])
                link(last)
                nc.vector.tensor_copy(weight8[:, bass.ds(b * NT, NT), :], w8[:, :, :])
                nc.vector.tensor_scalar(slot8[:, bass.ds(b * NT, NT), :], k8[:, :, :], -1.0, 0.0, add, ALU.max)
                link(nc.vector.tensor_scalar(off8[:, :, :], k8[:, :, :], 0.0, float(4 * SLOTS), ALU.is_equal, mult))
                v.wait_ge(scattered, (b + 1) * (NT * TOPK * 16))
                nc.vector.scalar_tensor_tensor(out=place8[:, :, :], in0=k8[:, :, :], scalar=-1.0, in1=off8[:, :, :],
                                               op0=add, op1=add).then_inc(placed, 1)
                nc.vector.tensor_copy(token_i[:, :], token_f[:, :]).then_inc(placed, 1)
                v.wait_ge(placed, 2)
                link(nc.vector.tensor_scalar(token_f[:, :], token_f[:, :], float(S), None, add))

            @block.gpsimd
            def _(pool):
                scatter()


def experts(nc, a, sem, G):
    ps, ident, taken, rows_d, taken_d, y_d = (G[k] for k in ("ps", "ident", "taken", "rows_d", "taken_d", "y_d"))
    ones, wq3, scale3, shared1 = (G[k] for k in ("ones", "wq3", "scale3", "shared1"))
    scattered, scatter = G["scattered"], G["scatter"]
    RING = 4
    N = PAIRS // RING
    with ExitStack() as ctx:
        def keep(name, shape, dt=F32):
            return [ctx.enter_context(nc.sbuf_tensor(f"{name}_{i}", shape, dt)) for i in range(RING)]

        wgu = keep("wgu", [P, DC, 2, 2 * INTER])
        wd = keep("wd", [IH, 2, 2, D])
        column = keep("column", [P, 1], U32)
        xg = keep("xg", [P, D])
        xgT = keep("xgT", [P, DC, P])
        h = keep("h", [P, INTER])
        hT = keep("hT", [IH, 2, P])
        y = keep("y", [P, D])

        w3 = ctx.enter_context(nc.sbuf_tensor("w3", [P, 2, D], F32))
        w3_d = ctx.enter_context(nc.sbuf_tensor("w3_d", [P, 2, P], F32))
        w3_s = ctx.enter_context(nc.sbuf_tensor("w3_s", [P, 4], F32))
        shared_in = sem("shared_in")
        w3_order, w3_ready, w3_turned, w3_kept = (sem(n) for n in ("w3_order", "w3_ready", "w3_turned", "w3_kept"))
        taken_in = sem("taken_in")
        wgu_in, wd_in = ([sem(f"{n}_in_{i}") for i in range(RING)] for n in ("wgu", "wd"))
        column_ready = [sem(f"column_ready_{i}") for i in range(RING)]
        rows_in = [sem(f"xg_in_{i}") for i in range(RING)]
        turned = [sem(f"xg_turned_{i}") for i in range(RING)]
        xgT_ready = [sem(f"xgT_ready_{i}") for i in range(RING)]
        gu_ready = [sem(f"gu_ready_{i}") for i in range(RING)]
        silu_ready = [sem(f"silu_ready_{i}") for i in range(RING)]
        h_ready = [sem(f"h_ready_{i}") for i in range(RING)]
        h_turned = [sem(f"h_turned_{i}") for i in range(RING)]
        hT_ready = [sem(f"hT_ready_{i}") for i in range(RING)]
        y_ready = [sem(f"ye_ready_{i}") for i in range(RING)]
        y_kept = [sem(f"ye_kept_{i}") for i in range(RING)]
        y_out = [sem(f"ye_out_{i}") for i in range(RING)]

        with nc.Block() as block:
            @block.sync
            def _(sp):
                def load(r, i):
                    sp.dma_start(wgu[i][:, :, :, :], a["L0_wgu"][r * RING + i]).then_inc(wgu_in[i], 16)
                    sp.dma_start(wd[i][:, :, :, :], a["L0_wd"][r * RING + i]).then_inc(wd_in[i], 16)

                y_rows = y_d.rearrange("(p r n) h -> r n p h", p=P, r=N)
                sp.dma_start(w3[:, :, :], a["L3_w"]).then_inc(shared_in, 16)
                for i in range(RING):
                    load(0, i)
                for dst, n in shared1:
                    whole = tuple(slice(None) for _ in dst.shape)
                    sp.dma_start(dst[whole], a[n]).then_inc(shared_in, 16)
                sp.wait_ge(scattered, (B + 1) * NT * TOPK * 16)
                sp.dma_start(taken[:, :], taken_d.rearrange("(p n) o -> p (n o)", p=P)).then_inc(taken_in, 16)
                with sp.Fori(1, N) as r:
                    for i in range(RING):
                        sp.wait_ge(gu_ready[i], r)
                        sp.dma_start(wgu[i][:, :, :, :], a["L0_wgu"][r * RING + i]).then_inc(wgu_in[i], 16)
                        sp.wait_ge(y_ready[i], r)
                        sp.dma_start(wd[i][:, :, :, :], a["L0_wd"][r * RING + i]).then_inc(wd_in[i], 16)
                        sp.wait_ge(y_kept[i], r)
                        sp.dma_start(y_rows[r - 1, i], y[i][:, :]).then_inc(y_out[i], 16)
                for i in range(RING):
                    sp.wait_ge(y_kept[i], N)
                    sp.dma_start(y_rows[N - 1, i], y[i][:, :]).then_inc(y_out[i], 16)
                sp.wait_ge(shared_in, 16 * (1 + len(shared1)))
                for i in range(RING):
                    sp.wait_ge(y_out[i], 16 * N)

            @block.gpsimd
            def _(pool):
                scatter()
                pool.wait_ge(taken_in, 16)

                def gather(done, i, at):
                    nc.gpsimd.tensor_copy(column[i][:, :], taken[:, bass.ds(at, 1)]).then_inc(column_ready[i], 1)
                    pool.wait_ge(taken_in, 16)
                    pool.wait_ge(column_ready[i], done)
                    nc.gpsimd.indirect_dma_start(xg[i][:, :], None, rows_d[:, :], bass.IndirectOffsetOnAxis(column[i][:, :], 0),
                                                 bounds_check=TOK + P - 1, oob_is_err=False).then_inc(rows_in[i], 16)

                for i in range(RING):
                    gather(1, i, i)
                with pool.Fori(2, N + 1) as done:
                    for i in range(RING):
                        at = pool.snap((done - 1) * RING + i)
                        pool.wait_ge(turned[i], done - 1)
                        gather(done, i, at)

            @block.tensor
            def _(pe):
                def turn(r, i):
                    pe.wait_ge(rows_in[i], 16 * r + 16)
                    for c in range(DC):
                        last = nc.tensor.transpose(ps[:, i % 2, c * P:(c + 1) * P], xg[i][:, c * P:(c + 1) * P], ident)
                    last.then_inc(turned[i], 1)

                def up(r, i):
                    pe.wait_ge(wgu_in[i], 16 * r + 16)
                    pe.wait_ge(xgT_ready[i], r + 1)
                    for c in range(DC):
                        for e in range(2):
                            last = nc.tensor.matmul(ps[e * CAP:(e + 1) * CAP, 2 + i % 2, 0:2 * INTER],
                                                    xgT[i][:, c, e * CAP:(e + 1) * CAP], wgu[i][:, c, e, :],
                                                    start=c == 0, stop=c == DC - 1)
                    last.then_inc(gu_ready[i], 1)

                def turn_hidden(r, i):
                    pe.wait_ge(h_ready[i], r + 1)
                    for j in range(2):
                        last = nc.tensor.transpose(ps[0:IH, 6 + i % 2, j * P:(j + 1) * P], h[i][:, j * IH:(j + 1) * IH], ident)
                    last.then_inc(h_turned[i], 1)

                def down(r, i, first=False):
                    pe.wait_ge(wd_in[i], 16 * r + 16)
                    pe.wait_ge(hT_ready[i], r + 1)
                    if i >= 2:
                        pe.wait_ge(y_kept[i - 2], r + 1)
                    elif not first:
                        pe.wait_ge(y_kept[i + 2], r)
                    for j in range(2):
                        for e in range(2):
                            last = nc.tensor.matmul(ps[e * CAP:(e + 1) * CAP, 4 + i % 2, 0:D], hT[i][:, j, e * CAP:(e + 1) * CAP],
                                                    wd[i][:, j, e, :], start=j == 0, stop=j == 1)
                    last.then_inc(y_ready[i], 1)

                def step(r, first=False, second=False, final=False):
                    for i in range(RING):
                        if i < RING - 1:
                            turn(r, i + 1)
                        elif not final:
                            turn(r + 1, 0)
                        up(r, i)
                        if i >= 1:
                            turn_hidden(r, i - 1)
                        elif not first:
                            turn_hidden(r - 1, RING - 1)
                        if i >= 2:
                            down(r, i - 2, first)
                        elif not first:
                            down(r - 1, i + RING - 2, second)

                pe.wait_ge(w3_ready, 1)
                for c in range(DC):
                    for o in range(2):
                        nc.tensor.transpose(ps[:, 6, c * D + o * P:c * D + (o + 1) * P], w3[:, o, c * P:(c + 1) * P], ident)
                for o in range(2):
                    last = nc.tensor.matmul(ps[:, 7, o * P:(o + 1) * P], ones, w3_d[:, o, :], start=True, stop=True)
                last.then_inc(w3_turned, 1)
                pe.wait_ge(w3_kept, 2)
                turn(0, 0)
                step(0, first=True)
                step(1, second=True)
                with pe.Fori(2, N - 1) as r:
                    step(r)
                step(N - 1, final=True)
                turn_hidden(N - 1, RING - 1)
                for i in (RING - 2, RING - 1):
                    down(N - 1, i)

            @block.scalar
            def _(act):
                def keep_turned(r, i):
                    act.wait_ge(turned[i], r + 1)
                    nc.scalar.activation(xgT[i][:, :, :], ps[:, i % 2, 0:D].rearrange("p (c s) -> p c s", c=DC),
                                         ACT.Copy).then_inc(xgT_ready[i], 1)

                def keep_hidden(r, i):
                    act.wait_ge(h_turned[i], r + 1)
                    nc.scalar.activation(hT[i][:, :, :], ps[0:IH, 6 + i % 2, 0:2 * P].rearrange("p (j s) -> p j s", j=2),
                                         ACT.Copy).then_inc(hT_ready[i], 1)

                def step(r, first=False, final=False):
                    for i in range(RING):
                        if i < RING - 1:
                            keep_turned(r, i + 1)
                        elif not final:
                            keep_turned(r + 1, 0)
                        act.wait_ge(gu_ready[i], r + 1)
                        nc.scalar.activation(h[i][:, :], ps[:, 2 + i % 2, 0:INTER], ACT.Silu).then_inc(silu_ready[i], 1)
                        if i >= 1:
                            keep_hidden(r, i - 1)
                        elif not first:
                            keep_hidden(r - 1, RING - 1)

                keep_turned(0, 0)
                step(0, first=True)
                with act.Fori(1, N - 1) as r:
                    step(r)
                step(N - 1, final=True)
                keep_hidden(N - 1, RING - 1)

            @block.vector
            def _(v):
                def hidden(r, i):
                    v.wait_ge(silu_ready[i], r + 1)
                    nc.vector.tensor_tensor(h[i][:, :], h[i][:, :], ps[:, 2 + i % 2, INTER:2 * INTER], mult).then_inc(h_ready[i], 1)

                def rows(r, i, first=False):
                    v.wait_ge(y_ready[i], r + 1)
                    if not first:
                        v.wait_ge(y_out[i], 16 * r)
                    nc.vector.tensor_copy(y[i][:, :], ps[:, 4 + i % 2, 0:D]).then_inc(y_kept[i], 1)

                def step(r, first=False, second=False):
                    for i in range(RING):
                        hidden(r, i)
                        if i >= 2:
                            rows(r, i - 2, first)
                        elif not first:
                            rows(r - 1, i + RING - 2, second)

                link = Chain(v, w3_order)
                v.wait_ge(shared_in, 16 * (1 + len(shared1)))
                for last in quantise(nc, link, w3[:, :, :], 2, w3_s[:, 0:2], w3_s[:, 2:4]):
                    pass
                link(last)
                for o in range(2):
                    last = nc.vector.tensor_scalar(w3_d[:, o, :], ident, w3_s[:, 2 + o:3 + o], None, mult)
                last.then_inc(w3_ready, 1)
                v.wait_ge(w3_turned, 1)
                nc.vector.tensor_copy(wq3[:, :, :], ps[:, 6, :].rearrange("p (c o) -> p c o", c=DC)).then_inc(w3_kept, 1)
                nc.vector.tensor_copy(scale3[:, :], ps[:, 7, 0:D]).then_inc(w3_kept, 1)

                step(0, first=True)
                step(1, second=True)
                with v.Fori(2, N) as r:
                    step(r)
                for i in (RING - 2, RING - 1):
                    rows(N - 1, i)


def layer1_weights(nc, scope):
    def keep(name, shape):
        return scope.enter_context(nc.sbuf_tensor(name, shape, F32))

    return [(keep("gw1", [P, 6, 36]), "L1_gw"),
            (keep("gb1", [36, 1]), "L1_gb"),
            (keep("minus1", [H1, H1, P]), "minus1"),
            (keep("wr1", [P, DC, P]), "L1_wr"),
            (keep("w11", [P, DC, F1]), "L1_w1"),
            (keep("b11", [P, FC1]), "L1_b1"),
            (keep("w21", [P, FC1, D]), "L1_w2"),
            (keep("earlier", [P, 7 * P]), "earlier")]


def side_by_side(*parts):
    parts = list(parts)
    while parts:
        parts = [p for p in parts if next(p, None)]


def layer1(nc, a, allocate, every, zeroed, G):
    ps, ident, gates, slot8, weight8 = (G[k] for k in ("ps", "ident", "gates", "slot8", "weight8"))
    x_d, y_d, outw1, b21 = (G[k] for k in ("x_d", "y_d", "outw1", "b21"))
    PAIR = 2
    with ExitStack() as ctx:
        def sem(name):
            return allocate(name, ctx)

        def keep(name, shape, dt=F32):
            return ctx.enter_context(nc.sbuf_tensor(name, shape, dt))

        def both(name, shape, dt=F32):
            return [keep(f"{name}_{u}", shape, dt) for u in range(PAIR)]

        def sems(name):
            return [sem(f"{name}_{u}") for u in range(PAIR)]

        gw1, gb1, minus1, wr1, w11, b11, w21, earlier = (t for t, _ in G["shared1"])
        xbs = [G["xb"], keep("xb_1", [P, NT, D])]
        xns = [G["xn"], keep("xn_1", [P, NT, D])]
        xnTs = [G["xnT"], keep("xnT_1", [P, DC, S])]
        ctxTs = [G["ctxT"], keep("ctxT_1", [P, DC, S])]
        tmps = [G["tmp"], keep("tmp_1", [P, 2, D])]
        statss = [G["stats"], tuple(keep(f"{n}_1", shape) for n, shape in (
            ("s6", [P, 16, 6]), ("mv", [P, 16, 2]), ("rstd", [P, 16]), ("var", [P, 16]), ("half", [P, 16])))]
        ctxbs = both("ctxb1", [P, NT, D])
        idx8s, w8s = both("idx8", [P, NT * TOPK], U32), both("w8b", [P, NT, TOPK])
        qHs = both("qH1", [P, H1, S])
        works = both("work1", [P, 8 * S])
        eTs = both("eT1", [P, 4, S])
        vaugs = both("vaug1", [P, NT, H1, 66])
        rowss = both("rows1", [36, 4 * S + 4])
        stacks = both("stack1", [36, S])
        gTs, ens = both("gT1", [P, NT, 36]), both("en1", [P, NT, H1])
        hbs, hns = both("hb1", [P, NT, H1, DH1]), both("hn1", [P, NT, H1, DH1])
        smalls = both("small1", [P, 32])

        y_in = [[allocate(f"y_in_{u}{i}") for i in range(2)] for u in range(PAIR)]
        since = len(every)
        names = ("x_in", "ctx_in", "idx_ready", "order", "summed", "xn_ready", "turned", "xnT_ready",
                 "gates_ready", "gsb_ready", "f_ready", "abs_ready", "softplus", "stack_ready", "stackT_ready", "gT_ready",
                 "en_ready", "gb_ready", "d_ready", "dmask_ready", "qk_ready", "c_ready", "h_ready", "n_ready", "h_kept", "zeros",
                 "score_ready", "col_ready", "sig_ready", "hid_ready", "hid_kept", "out_ready", "out_kept", "x_ready", "x_out")
        Ls = [{n: sem(f"B{u}_{n}") for n in names} for u in range(PAIR)]

        with nc.Fori(0, B // PAIR) as pair, zeroed(since), nc.Block() as block:
            @block.sync
            def _(sp):
                for u in range(PAIR):
                    b, L = pair * PAIR + u, Ls[u]
                    sp.dma_start(xbs[u][:, :, :], x_d[b]).then_inc(L["x_in"], 16)
                    sp.dma_start(ctxbs[u][:, :, :], a["ctx"][b]).then_inc(L["ctx_in"], 16)
                    sp.dma_start(ctxTs[u][:, :, :], a["ctxT"][b]).then_inc(L["ctx_in"], 16)
                for u in range(PAIR):
                    sp.wait_ge(Ls[u]["x_ready"], 1)
                    sp.dma_start(x_d[pair * PAIR + u], xbs[u][:, :, :]).then_inc(Ls[u]["x_out"], 16)
                for u in range(PAIR):
                    sp.wait_ge(Ls[u]["x_out"], 16)

            @block.gpsimd
            def _(pool):
                for u in range(PAIR):
                    tiles = bass.ds((pair * PAIR + u) * NT, NT)
                    nc.gpsimd.tensor_copy(idx8s[u][:, :], slot8[:, tiles, :].rearrange("p t k -> p (t k)"))\
                        .then_inc(Ls[u]["idx_ready"], 1)
                for u in range(PAIR):
                    pool.wait_ge(Ls[u]["idx_ready"], 1)
                for t in range(NT):
                    for u in range(PAIR):
                        yg = works[u][:, t % 2 * TOPK * D:(t % 2 + 1) * TOPK * D].rearrange("p (k d) -> p k d", k=TOPK)
                        if t >= 2:
                            pool.wait_ge(Ls[u]["summed"], t - 1)
                        for k in range(TOPK):
                            nc.gpsimd.indirect_dma_start(yg[:, k, :], None, y_d[:, :],
                                                         bass.IndirectOffsetOnAxis(idx8s[u][:, t * TOPK + k:t * TOPK + k + 1], 0),
                                                         bounds_check=SLOTS - 1, oob_is_err=False).then_inc(y_in[u][t % 2], 16)
                for n in range(H1 * NT):
                    for u in range(PAIR):
                        pool.wait_ge(Ls[u]["d_ready"], n + 1)
                        d = eTs[u][:, n % 4, n % NT * P:(n % NT + 1) * P]
                        nc.gpsimd.affine_select(out=d, in_=d, pattern=[[1, P]], compare_op=ALU.is_ge, fill=0.0, base=0,
                                                channel_multiplier=-1).then_inc(Ls[u]["dmask_ready"], 1)

            @block.tensor
            def _(pe):
                def part(u):
                    L, xn, xnT, ctxT, qH, eT, vaug = Ls[u], xns[u], xnTs[u], ctxTs[u], qHs[u], eTs[u], vaugs[u]
                    bank = [ps[:, 4 * u + i, :] for i in range(4)]
                    cT = works[u][:, :].rearrange("p (i c s) -> p i c s", i=2, c=NT)
                    wide = works[u][:, :].rearrange("p (f s) -> p f s", f=FC1)
                    G_r = rowss[u][0:H1, 3 * S + 2:4 * S + 2]

                    def turn(k):
                        pe.wait_ge(L["xn_ready"], k + 1)
                        for c in range(DC):
                            for t in range(NT):
                                last = nc.tensor.transpose(bank[c][:, t * P:(t + 1) * P], xn[:, t, c * P:(c + 1) * P], ident)
                            last.then_inc(L["turned"], 1)

                    turn(0)
                    yield True
                    pe.wait_ge(L["xnT_ready"], 4)
                    pe.wait_ge(L["ctx_in"], 32)
                    g_terms = [(gw1[:, h // 2, :], qH[:, h, :]) for h in range(H1)] + \
                              [(gw1[:, 2 + c, :], ctxT[:, c % 2, :]) for c in range(4)]
                    for n, (l, r) in enumerate(g_terms):
                        last = nc.tensor.matmul(bank[2][0:36, :], l, r, start=n == 0, stop=n == len(g_terms) - 1)
                    last.then_inc(L["gates_ready"], 1)
                    yield True
                    pe.wait_ge(L["stack_ready"], 1)
                    for t in range(NT):
                        last = nc.tensor.transpose(bank[3][:, t * 36:(t + 1) * 36], stacks[u][:, t * P:(t + 1) * P], ident[0:36, 0:36])
                    last.then_inc(L["stackT_ready"], 1)
                    yield True
                    pe.wait_ge(L["gT_ready"], 1)

                    def product(h):
                        pe.wait_ge(L["c_ready"], NT * (h + 1))
                        if h:
                            pe.wait_ge(L["h_kept"], h)
                        for st in range(NT):
                            for tc in range(st + 1):
                                last = nc.tensor.matmul(bank[2][:, st * 65:(st + 1) * 65], cT[:, h % 2, tc, st * P:(st + 1) * P],
                                                        vaug[:, tc, h, 0:65], start=tc == 0, stop=tc == st)
                        last.then_inc(L["h_ready"], 1)

                    for h in range(H1):
                        if h:
                            pe.wait_ge(L["d_ready"], NT * h)
                        nc.tensor.matmul(bank[3], minus1[:, h, :], G_r, start=True, stop=True).then_inc(L["gb_ready"], 1)
                        for tc in range(NT):
                            n = h * NT + tc
                            if n >= 2:
                                pe.wait_ge(L["c_ready"], n - 1)
                            nc.tensor.matmul(bank[n % 2][:, tc * P:S], ctxT[:, h // 2, tc * P:(tc + 1) * P], qH[:, h, tc * P:S],
                                             start=True, stop=True).then_inc(L["qk_ready"], 1)
                            yield True
                        if h:
                            product(h - 1)
                            yield True
                    product(H1 - 1)
                    yield True

                    turn(1)
                    yield True
                    pe.wait_ge(L["h_kept"], H1)
                    pe.wait_ge(L["xnT_ready"], 6)
                    for c in range(DC):
                        last = nc.tensor.matmul(bank[2], wr1[:, c, :], xnT[:, c, :], start=c == 0, stop=c == DC - 1)
                    last.then_inc(L["score_ready"], 1)
                    yield True
                    for f in range(FC1):
                        if f >= 2:
                            pe.wait_ge(L["hid_kept"], f - 1)
                        for c in range(DC):
                            last = nc.tensor.matmul(bank[f % 2], w11[:, c, f * P:(f + 1) * P], xnT[:, c, :],
                                                    start=c == 0, stop=c == DC - 1)
                        last.then_inc(L["hid_ready"], 1)
                        yield True
                    pe.wait_ge(L["hid_kept"], FC1)
                    pe.wait_ge(L["col_ready"], 1)
                    for t in range(NT):
                        if t >= 2:
                            pe.wait_ge(L["out_kept"], t - 1)
                        for f in range(FC1):
                            last = nc.tensor.matmul(bank[2 + t % 2][:, 0:D], wide[:, f, t * P:(t + 1) * P], w21[:, f, :],
                                                    start=f == 0, stop=f == FC1 - 1)
                        last.then_inc(L["out_ready"], 1)
                        yield True

                side_by_side(part(0), part(1))

            @block.scalar
            def _(act):
                def part(u):
                    L, xnT, qH, eT, hb = Ls[u], xnTs[u], qHs[u], eTs[u], hbs[u]
                    bank = [ps[:, 4 * u + i, :] for i in range(4)]
                    wide = works[u][:, :].rearrange("p (f s) -> p f s", f=FC1)
                    gsb, f_r, a_r = rowss[u][0:36, 0:S], rowss[u][0:H1, S:2 * S], rowss[u][0:H1, 2 * S:3 * S]
                    gT = gTs[u]
                    act.wait_ge(L["zeros"], 1)
                    for c in range(DC):
                        act.wait_ge(L["turned"], c + 1)
                        for s in range(2):
                            r = slice(64 * s, 64 * s + 64)
                            nc.scalar.activation(qH[r, 2 * c + s, :], bank[c][r, :], ACT.Copy).then_inc(L["xnT_ready"], 1)
                    yield True
                    act.wait_ge(L["gsb_ready"], 1)
                    nc.scalar.activation(f_r, gsb[32:36, :], ACT.Copy).then_inc(L["f_ready"], 1)
                    yield True
                    act.wait_ge(L["abs_ready"], 1)
                    nc.scalar.activation(a_r, a_r, ACT.Exp, scale=-1.0).then_inc(L["softplus"], 1)
                    yield True
                    act.wait_ge(L["softplus"], 1)
                    nc.scalar.activation(a_r, a_r, ACT.Ln, bias=1.0).then_inc(L["softplus"], 1)
                    yield True
                    act.wait_ge(L["gT_ready"], 1)
                    nc.scalar.activation(ens[u][:, :, :], gT[:, :, 32:36], ACT.Exp, scale=-1.0).then_inc(L["en_ready"], 1)

                    def keep_head(h):
                        act.wait_ge(L["n_ready"], h + 1)
                        n4 = smalls[u][:, 4 * (h % 2):4 * (h % 2) + 4]
                        for t in range(NT):
                            last = nc.scalar.activation(hb[:, t, h, :], bank[2][:, t * 65:t * 65 + 64], ACT.Copy, scale=n4[:, t:t + 1])
                        last.then_inc(L["h_kept"], 1)

                    for n in range(H1 * NT):
                        h, tc = divmod(n, NT)
                        act.wait_ge(L["gb_ready"], h + 1)
                        if n >= 4:
                            act.wait_ge(L["c_ready"], n - 3)
                        nc.scalar.activation(eT[:, n % 4, tc * P:S], bank[3][:, tc * P:S], ACT.Exp, bias=gT[:, tc, h:h + 1])\
                            .then_inc(L["d_ready"], 1)
                        if h and tc == 2:
                            keep_head(h - 1)
                        yield True
                    keep_head(H1 - 1)
                    yield True
                    for c in range(DC):
                        act.wait_ge(L["turned"], DC + c + 1)
                        nc.scalar.activation(xnT[:, c, :], bank[c], ACT.Copy).then_inc(L["xnT_ready"], 1)
                    yield True
                    act.wait_ge(L["col_ready"], 1)
                    nc.scalar.activation(smalls[u][:, 20:24], smalls[u][:, 8:12], ACT.Exp, scale=-1.0).then_inc(L["sig_ready"], 1)
                    yield True
                    for f in range(FC1):
                        act.wait_ge(L["hid_ready"], f + 1)
                        nc.scalar.activation(wide[:, f, :], bank[f % 2], ACT.Gelu_apprx_tanh, bias=b11[:, f:f + 1])\
                            .then_inc(L["hid_kept"], 1)
                        yield True

                side_by_side(part(0), part(1))

            @block.vector
            def _(v):
                def part(u):
                    L, xb, xn, tmp, stats = Ls[u], xbs[u], xns[u], tmps[u], statss[u]
                    qH, eT, vaug, hb, hn, en, gT, small = qHs[u], eTs[u], vaugs[u], hbs[u], hns[u], ens[u], gTs[u], smalls[u]
                    bank = [ps[:, 4 * u + i, :] for i in range(4)]
                    cT = works[u][:, :].rearrange("p (i c s) -> p i c s", i=2, c=NT)
                    rows, stack = rowss[u], stacks[u]
                    gsb, f_r, a_r = rows[0:36, 0:S], rows[0:H1, S:2 * S], rows[0:H1, 2 * S:3 * S]
                    G_r = rows[0:H1, 3 * S + 2:4 * S + 2]
                    cs_r = eT[0:H1, 0:2, :].rearrange("p a b -> p (a b)")[:, 0:S + 1]
                    link = Chain(v, L["order"])

                    for h in range(H1):
                        o = 64 * (1 - h % 2)
                        nc.vector.memset(qH[o:o + 64, h, :], 0.0)
                    nc.vector.memset(stack[:, :], 0.0)
                    nc.vector.memset(cs_r[:, 0:1], 0.0)
                    nc.vector.memset(G_r, 1.0)
                    nc.vector.memset(vaug[:, :, :, 64:65], 1.0).then_inc(L["zeros"], 1)
                    v.wait_ge(L["zeros"], 1)
                    v.wait_ge(L["ctx_in"], 32)
                    nc.vector.tensor_copy(vaug[:, :, :, 0:64], ctxbs[u][:, :, :].rearrange("p c (h d) -> p c h d", h=H1))
                    link(nc.vector.tensor_copy(w8s[u][:, :, :], weight8[:, bass.ds((pair * PAIR + u) * NT, NT), :]))
                    v.wait_ge(L["x_in"], 16)
                    for t in range(NT):
                        yg = works[u][:, t % 2 * TOPK * D:(t % 2 + 1) * TOPK * D].rearrange("p (k d) -> p k d", k=TOPK)
                        v.wait_ge(y_in[u][t % 2], pair * (NT // 2 * 16 * TOPK) + (t // 2 + 1) * 16 * TOPK)
                        o = tmp[:, t % 2, :]
                        link(nc.vector.tensor_scalar(o, yg[:, 0, :], w8s[u][:, t, 0:1], None, mult))
                        for k in range(1, TOPK):
                            last = nc.vector.scalar_tensor_tensor(out=o, in0=yg[:, k, :], scalar=w8s[u][:, t, k:k + 1], in1=o,
                                                                  op0=mult, op1=add)
                            if k < TOPK - 1:
                                link(last)
                        last.then_inc(L["summed"], 1)
                        v.wait_ge(L["summed"], t + 1)
                        last = nc.vector.scalar_tensor_tensor(out=xb[:, t, :], in0=o, scalar=gates[:, 4:5], in1=xb[:, t, :],
                                                              op0=mult, op1=add)
                        if t == NT - 1:
                            link(last)
                        yield True
                    layernorm(nc, link, xb, xn, stats).then_inc(L["xn_ready"], 1)
                    yield True

                    v.wait_ge(L["gates_ready"], 1)
                    nc.vector.tensor_scalar(gsb, bank[2][0:36, :], gb1[:, 0:1], None, add).then_inc(L["gsb_ready"], 1)
                    yield True
                    v.wait_ge(L["f_ready"], 1)
                    nc.vector.scalar_tensor_tensor(out=a_r, in0=f_r, scalar=-1.0, in1=f_r, op0=mult, op1=ALU.max).then_inc(L["abs_ready"], 1)
                    yield True
                    v.wait_ge(L["softplus"], 2)
                    link(nc.vector.scalar_tensor_tensor(out=f_r, in0=f_r, scalar=0.0, in1=a_r,
                                                        op0=ALU.min, op1=subtract))
                    link(nc.vector.tensor_tensor_scan(cs_r[:, 1:S + 1], G_r, f_r, 0.0, mult, add))
                    link(nc.vector.tensor_tensor(stack[0:H1, :], gsb[0:H1, :], cs_r[:, 0:S], subtract))
                    link(nc.vector.tensor_tensor_scan(G_r, stack[0:H1, :], stack[0:H1, :], -FMAX, ALU.max, ALU.max))
                    nc.vector.tensor_tensor(stack[32:36, :], cs_r[:, 1:S + 1], G_r, add).then_inc(L["stack_ready"], 1)
                    yield True
                    v.wait_ge(L["stackT_ready"], 1)
                    nc.vector.tensor_copy(gT[:, :, :], bank[3][:, 0:NT * 36].rearrange("p (t k) -> p t k", t=NT)).then_inc(L["gT_ready"], 1)
                    yield True

                    def normaliser(h):
                        o = bank[2][:, 0:NT * 65].rearrange("p (t d) -> p t d", t=NT)
                        n4 = small[:, 4 * (h % 2):4 * (h % 2) + 4]
                        v.wait_ge(L["h_ready"], h + 1)
                        v.wait_ge(L["en_ready"], 1)
                        link(nc.vector.tensor_tensor(n4, o[:, :, 64], en[:, :, h], ALU.max))
                        link(nc.vector.scalar_tensor_tensor(out=n4, in0=o[:, :, 64], scalar=-1.0, in1=n4, op0=mult, op1=ALU.max))
                        link(nc.vector.tensor_scalar(n4, n4, 1e-8, None, add))
                        nc.vector.reciprocal(n4, n4).then_inc(L["n_ready"], 1)

                    for n in range(H1 * NT):
                        h, tc = divmod(n, NT)
                        v.wait_ge(L["qk_ready"], n + 1)
                        v.wait_ge(L["dmask_ready"], n + 1)
                        if h >= 2:
                            v.wait_ge(L["h_ready"], h - 1)
                        nc.vector.scalar_tensor_tensor(out=cT[:, h % 2, tc, tc * P:S], in0=bank[n % 2][:, tc * P:S], scalar=DH1 ** -0.5,
                                                       in1=eT[:, n % 4, tc * P:S], op0=mult, op1=mult).then_inc(L["c_ready"], 1)
                        if tc == 2 and h:
                            normaliser(h - 1)
                        yield True
                    normaliser(H1 - 1)
                    yield True
                    v.wait_ge(L["h_kept"], H1)
                    link(layernorm(nc, link, hb.rearrange("p t h d -> p (t h) d"), hn.rearrange("p t h d -> p (t h) d"), stats, NT * H1))
                    link(nc.vector.tensor_scalar(tmp[:, 1, :], outw1, 1.0, gates[:, 1:2], add, mult))
                    hrow = hn.rearrange("p t h d -> p t (h d)")
                    for t in range(NT):
                        last = nc.vector.tensor_tensor(hrow[:, t, :], hrow[:, t, :], tmp[:, 1, :], mult)
                    link(last)
                    link(nc.vector.tensor_tensor(xb[:, :, :], xb[:, :, :], hrow, add))
                    layernorm(nc, link, xb, xn, stats).then_inc(L["xn_ready"], 1)
                    yield True

                    srow, one_row, sjunk = eT[:, 0, :], eT[:, 1, :], eT[:, 2, :]
                    col, c1, c2, sig = small[:, 8:12], small[:, 12:16], small[:, 16:20], small[:, 20:24]
                    link(nc.vector.memset(one_row, 1.0))
                    v.wait_ge(L["score_ready"], 1)
                    link(nc.vector.tensor_copy(srow, bank[2]))
                    for t in range(NT):
                        last = nc.vector.tensor_tensor_reduce(out=sjunk[:, t * P:(t + 1) * P], in0=srow[:, t * P:(t + 1) * P], in1=ident, scale=1.0,
                                                              scalar=0.0, op0=mult, op1=add, accum_out=col[:, t:t + 1])
                    last.then_inc(L["col_ready"], 1)
                    v.wait_ge(L["col_ready"], 1)
                    yield True
                    for t in range(NT):
                        link(nc.vector.scalar_tensor_tensor(out=sjunk, in0=srow, scalar=col[:, t:t + 1], in1=one_row,
                                                            op0=ALU.is_gt, op1=mult, accum_out=c1[:, t:t + 1]))
                        last = nc.vector.scalar_tensor_tensor(out=sjunk, in0=srow, scalar=col[:, t:t + 1],
                                                              in1=earlier[:, 3 * P - t * P:3 * P - t * P + S], op0=ALU.is_equal,
                                                              op1=mult, accum_out=c2[:, t:t + 1])
                        link(last)
                        yield True
                    link(nc.vector.tensor_tensor(c1, c1, c2, add))
                    v.wait_ge(L["sig_ready"], 1)
                    link(nc.vector.tensor_scalar(sig, sig, 1.0, None, add))
                    link(nc.vector.reciprocal(sig, sig))
                    link(nc.vector.scalar_tensor_tensor(out=sig, in0=c1, scalar=float(KEEP), in1=sig, op0=ALU.is_lt, op1=mult))
                    yield True
                    for t in range(NT):
                        v.wait_ge(L["out_ready"], t + 1)
                        o = tmp[:, t % 2, :]
                        nc.vector.tensor_tensor(o, bank[2 + t % 2][:, 0:D], b21, add).then_inc(L["out_kept"], 1)
                        v.wait_ge(L["out_kept"], t + 1)
                        link(nc.vector.scalar_tensor_tensor(out=o, in0=o, scalar=sig[:, t:t + 1], in1=xn[:, t, :], op0=mult, op1=add))
                        last = nc.vector.scalar_tensor_tensor(out=xb[:, t, :], in0=o, scalar=gates[:, 5:6], in1=xb[:, t, :],
                                                              op0=mult, op1=add)
                        yield True
                    last.then_inc(L["x_ready"], 1)

                side_by_side(part(0), part(1))


def layers2to3(nc, a, sem, every, zeroed, G, out):
    ps, ident, gates = (G[k] for k in ("ps", "ident", "gates"))
    xb, xn, xnT, ctxT, stats, tmp = (G[k] for k in ("xb", "xn", "xnT", "ctxT", "stats", "tmp"))
    least, sums, recip, x_d = (G[k] for k in ("least", "sums", "recip", "x_d"))
    bo2, bias3, wq3, scale3 = (G[k] for k in ("bo2", "bias3", "wq3", "scale3"))
    with ExitStack() as ctx:
        def keep(name, shape, dt=F32):
            return ctx.enter_context(nc.sbuf_tensor(name, shape, dt))

        ln2 = keep("ln2", [P, 4, DC])
        ln3 = keep("ln3", [P, 4, DC])
        wp1 = keep("wp1", [P, DC, NAV])
        bp1 = keep("bp1", [P, 1])
        wp2 = keep("wp2", [P, E2])
        bp2 = keep("bp2", [1, E2])
        wo2f = keep("wo2f", [P, DC, D])
        arena = keep("arena", [P, 40 * 256])
        wq2 = keep("wq2", [P, DC, INNER])
        wk2 = keep("wk2", [P, DC, P])
        wv2 = keep("wv2", [P, DC, DH2])
        xb2 = keep("xb2", [P, NT, D])
        xnT2 = keep("xnT2", [P, DC, S])
        cnT = keep("cnT", [P, DC, S])
        ctxb = keep("ctxb", [P, NT, D])
        qT = [keep(f"qT_{i}", [P, S]) for i in range(2)]
        kH = [[keep(f"kH_{i}{s}", [P, KEYS3]) for s in range(2)] for i in range(2)]
        vh = [keep(f"vh_{i}", [P, KEYS3 // P, P]) for i in range(2)]
        work = keep("work", [P, 2 * 8 * S])
        wide = keep("wide", [P, 8, S])
        pbuf = keep("pbuf", [P, 4, KEYS3])
        small = keep("small", [P, 64])
        we1 = work[:, 0:DC * FE2].rearrange("p (c f) -> p c f", c=DC)
        we2 = work[:, DC * FE2:DC * FE2 + FEC * D].rearrange("p (c f) -> p c f", c=FEC)
        be1 = keep("be1", [P, FEC])
        be2 = keep("be2", [P, DC])

        def cut(start, *shape):
            n = int(np.prod(shape))
            names = "bcd"[:len(shape)]
            v = arena[:, start:start + n]
            return v.rearrange(f"p (b c) -> p b c", b=shape[0]), start + n

        wo2, at = cut(0, HP, D)
        wff1, at = cut(at, DC, 2 * FF2)
        wff2, at = cut(at, FFC, D)
        assert at <= 40 * 256
        wqx, at = cut(0, DC, INNER)
        wkx, at = cut(at, DC, INNER)
        wvx, at = cut(at, DC, INNER)
        wox, at = cut(at, HP, D)
        keysT, at = cut(at, DC, KEYS3)
        assert at <= 40 * 256
        mask_u8 = keep("mask_u8", [P, S], mybir.dt.uint8)
        mask3 = keep("mask3", [P, KEYS3])
        xqT = keep("xqT", [P, DC, S], BF16)
        pick = keep("pick", [1, 8], U32)

        since = len(every)
        x_in, ctx_in, mask_in, arena_in, arena3_in, out_done = (
            sem(n + "_C") for n in ("x_in", "ctx_in", "mask_in", "arena_in", "arena3_in", "out_done"))
        order = sem("dve_orderC")
        const_in = sem("constC_in")
        loads = [(ln2[:, :, :], "L2_ln"), (wk2[:, :, :], "L2_wk"), (wv2[:, :, :], "L2_wv"), (wq2[:, :, :], "L2_wq"),
                 (ln3[:, :, :], "L3_ln"), (wp1[:, :, :], "L2_wp1"), (bp1[:, :], "L2_bp1"),
                 (wp2[:, :], "L2_wp2"), (bp2[:, :], "L2_bp2"), (wo2f[:, :, :], "L2_wof")]
        link = Chain(nc.vector, order)

        def pe_turn(src, turned):
            for c in range(DC):
                for t in range(NT):
                    last = nc.tensor.transpose(ps[:, c, t * P:(t + 1) * P], src[:, t, c * P:(c + 1) * P], ident)
                last.then_inc(turned, 1)

        def turn_job(src, c, ready, keep_it):
            def product(pe):
                pe.wait_ge(ready, 1)
                for t in range(NT):
                    last = nc.tensor.transpose(ps[:, 7, t * P:(t + 1) * P], src[:, t, c * P:(c + 1) * P], ident)
                return last

            return product, keep_it

        def on_vector(gen, slots, ready):
            def one(v):
                next(gen)

            def rest(v):
                for last in gen:
                    pass
                last.then_inc(ready, 1)

            return [(None, one)] * (slots - 1) + [(None, rest)]

        N2 = {n: sem("N2_" + n) for n in ("xn_ready", "cn_ready", "ready", "kept")}

        def q_job(w, xT, g):
            def product(pe):
                for c in range(DC):
                    last = nc.tensor.matmul(ps[:, 7, :], w[:, c, g * P:(g + 1) * P], xT[:, c, :], start=c == 0, stop=c == DC - 1)
                return last

            return product, lambda v: nc.vector.tensor_scalar(qT[g % 2][:, :], ps[:, 7, :], -DH2 ** -0.5, None, mult)

        def k_job():
            def product(pe):
                for c in range(DC):
                    last = nc.tensor.matmul(ps[:, 7, :], wk2[:, c, :], cnT[:, c, :], start=c == 0, stop=c == DC - 1)
                return last

            def copy(v):
                for s in range(2):
                    r = slice(64 * s, 64 * s + 64)
                    last = nc.vector.tensor_copy(kH[0][s][r, 0:S], ps[r, 7, :])
                return last

            return product, copy

        def v_job():
            def product(pe):
                for t in range(NT):
                    for c in range(DC):
                        last = nc.tensor.matmul(ps[:, 7, t * DH2:(t + 1) * DH2], cnT[:, c, t * P:(t + 1) * P], wv2[:, c, :],
                                                start=c == 0, stop=c == DC - 1)
                return last

            return product, lambda v: nc.vector.tensor_copy(
                vh[0][:, 0:NT, 0:DH2], ps[:, 7, 0:NT * DH2].rearrange("p (t d) -> p t d", t=NT))

        def norm_jobs():
            def begin(v):
                v.wait_ge(x_in, 16)
                v.wait_ge(ctx_in, 16)

            def keep_x(c):
                return lambda v: nc.vector.tensor_scalar(xnT2[:, c, :], ps[:, 7, :], ln2[:, 0, c:c + 1], ln2[:, 1, c:c + 1], mult, add)

            def keep_ctx(c):
                def run(v):
                    nc.vector.tensor_copy(ctxT[:, c, :], ps[:, 7, :])
                    return nc.vector.tensor_scalar(cnT[:, c, :], ps[:, 7, :], ln2[:, 2, c:c + 1], ln2[:, 3, c:c + 1], mult, add)
                return run

            return [(None, begin)] + \
                on_vector(layernorm_steps(nc, link, xb2, xn, stats, twice=True), 11, N2["xn_ready"]) + \
                on_vector(layernorm_steps(nc, link, ctxb, ctxb, stats), 7, N2["cn_ready"]) + \
                [turn_job(xn, c, N2["xn_ready"], keep_x(c)) for c in range(DC)] + \
                [turn_job(ctxb, c, N2["cn_ready"], keep_ctx(c)) for c in range(DC)] + \
                [q_job(wq2, xnT2, 0), k_job(), v_job()]

        def run_jobs(jobs, ready, kept):
            def tensor(pe):
                for n, job in enumerate(j for j in jobs if j[0] is not None):
                    if n:
                        pe.wait_ge(kept, n)
                    job[0](pe).then_inc(ready, 1)

            def vector(v):
                n = 0
                for product, copy in jobs:
                    if product is None:
                        copy(v)
                    else:
                        n += 1
                        v.wait_ge(ready, n)
                        copy(v).then_inc(kept, 1)

            return tensor, vector

        A = {n: sem("A2_" + n) for n in ("gate_ready", "silu_ready", "hT_ready", "out_ready")}
        hT2 = work[:, 0:FFC * S].rearrange("p (f s) -> p f s", f=FFC)

        att2 = attention(nc, sem, "a2", ps, ident, 2, HP, NT,
                         lambda g, s, qt: qT[g % 2][:, qt * P:(qt + 1) * P],
                         lambda g, s, kb: kH[0][s][:, 0:S],
                         lambda g, s, kc: vh[0][:, kc, 0:DH2], DH2, None,
                         ([pbuf[:, i // 2, (i % 2) * S:(i % 2 + 1) * S] for i in range(8)], sums, recip, least,
                          work[:, 0:2 * NT * S].rearrange("p (s c q) -> p s c q", s=2, c=NT)), wide,
                         jobs=lambda g: [q_job(wq2, xnT2, g)])

        R = {n: sem("R2_" + n) for n in ("xn_ready", "turned", "xnT_ready", "z_ready", "z_kept", "logit_ready", "picked", "we_in", "hid_ready", "hid_kept",
                                         "mid_ready", "mid_kept", "out_ready")}
        z, lrow, l8 = small[:, 32:33], small[0:1, 40:48], small[0:1, 48:56]
        LAST_FIRST = [NT - 1] + list(range(NT - 1))

        def r2_turn(n, tiles):
            nc.tensor.wait_ge(R["xn_ready"], n)
            for c in range(DC):
                for t in tiles:
                    last = nc.tensor.transpose(ps[:, c, t * P:(t + 1) * P], xn[:, t, c * P:(c + 1) * P], ident)
                last.then_inc(R["turned"], 1)

        def l2_tensor(pe, background={}):
            att2[0](pe, background)
            pe.wait_ge(arena_in, 48)
            for f in range(FFC):
                if f >= 2:
                    pe.wait_ge(A["hT_ready"], f - 1)
                for c in range(DC):
                    nc.tensor.matmul(ps[:, f % 2, :], wff1[:, c, FF2 + f * P:FF2 + (f + 1) * P], xnT2[:, c, :],
                                     start=c == 0, stop=c == DC - 1)
                for c in range(DC):
                    last = nc.tensor.matmul(ps[:, 2 + f % 2, :], wff1[:, c, f * P:(f + 1) * P], xnT2[:, c, :],
                                            start=c == 0, stop=c == DC - 1)
                last.then_inc(A["gate_ready"], 1)
            pe.wait_ge(att2[3], HP)
            pe.wait_ge(A["hT_ready"], FFC)
            for t in LAST_FIRST:
                for g in range(HP):
                    nc.tensor.matmul(ps[:, 4 + t, 0:D], wide[:, g, t * P:(t + 1) * P], wo2[:, g, :], start=g == 0, stop=False)
                for f in range(FFC):
                    last = nc.tensor.matmul(ps[:, 4 + t, 0:D], hT2[:, f, t * P:(t + 1) * P], wff2[:, f, :],
                                            start=False, stop=f == FFC - 1)
                last.then_inc(A["out_ready"], 1)
                if t == 0:
                    r2_turn(1, [NT - 1])
                if t == 1:
                    pe.wait_ge(R["xnT_ready"], DC)
                    for c in range(DC):
                        last = nc.tensor.matmul(ps[:, 2, 0:1], wp1[:, c, :], xnT[:, c, S - 1:S], start=c == 0, stop=c == DC - 1)
                    last.then_inc(R["z_ready"], 1)
            pe.wait_ge(R["z_kept"], 1)
            nc.tensor.matmul(ps[0:1, 3, 0:E2], z, wp2[:, :], start=True, stop=True).then_inc(R["logit_ready"], 1)

        def l2_scalar(act):
            att2[2](act)
            for f in range(FFC):
                act.wait_ge(A["gate_ready"], f + 1)
                if f >= 2:
                    act.wait_ge(A["hT_ready"], f - 1)
                nc.scalar.activation(pbuf[:, f % 2, 0:S], ps[:, f % 2, :], ACT.Silu).then_inc(A["silu_ready"], 1)

        def l2_vector(v, background={}):
            att2[1](v, background)
            for f in range(FFC):
                v.wait_ge(A["silu_ready"], f + 1)
                nc.vector.tensor_tensor(hT2[:, f, :], pbuf[:, f % 2, 0:S], ps[:, 2 + f % 2, :], mult).then_inc(A["hT_ready"], 1)
            if background:
                v.wait_ge(out_done, 16)
            for n, t in enumerate(LAST_FIRST):
                v.wait_ge(A["out_ready"], n + 1)
                link(nc.vector.scalar_tensor_tensor(out=xb[:, t, :], in0=ps[:, 4 + t, 0:D], scalar=gates[:, 2:3],
                                                    in1=xb2[:, t, :], op0=mult, op1=add))
                if n == 0:
                    layernorm(nc, link, xb[:, NT - 1:NT, :], xn[:, NT - 1:NT, :], stats, 1).then_inc(R["xn_ready"], 1)
            v.wait_ge(R["logit_ready"], 1)
            link(nc.vector.tensor_tensor(lrow, ps[0:1, 3, 0:E2], bp2[:, :], add))
            link(nc.vector.max(l8, lrow))
            nc.vector.max_index(pick[:, :], l8, lrow).then_inc(R["picked"], 1)

        def r2_tensor(pe):
            r2_turn(2, range(NT - 1))
            pe.wait_ge(R["xnT_ready"], 2 * DC)
            pe.wait_ge(R["we_in"], 64)
            for f in range(FEC):
                for c in range(DC):
                    last = nc.tensor.matmul(ps[:, 4 + f, :], we1[:, c, f * P:(f + 1) * P], xnT[:, c, :],
                                            start=c == 0, stop=c == DC - 1)
                last.then_inc(R["hid_ready"], 1)
            for h in range(DC):
                for f in range(FEC):
                    if h == 0:
                        pe.wait_ge(R["hid_kept"], f + 1)
                    last = nc.tensor.matmul(ps[:, h, :], we2[:, f, h * P:(h + 1) * P], wide[:, f, :],
                                            start=f == 0, stop=f == FEC - 1)
                last.then_inc(R["mid_ready"], 1)
            pe.wait_ge(R["mid_kept"], DC)
            for t in range(NT):
                for h in range(DC):
                    last = nc.tensor.matmul(ps[:, 2 + t, 0:D], wide[:, FEC + h, t * P:(t + 1) * P], wo2f[:, h, :],
                                            start=h == 0, stop=h == DC - 1)
                last.then_inc(R["out_ready"], 1)

        def r2_scalar(act):
            def keep_turned(n, columns):
                for c in range(DC):
                    act.wait_ge(R["turned"], n * DC + c + 1)
                    nc.scalar.activation(xnT[:, c, columns], ps[:, c, columns], ACT.Copy).then_inc(R["xnT_ready"], 1)

            keep_turned(0, slice(S - P, S))
            act.wait_ge(R["z_ready"], 1)
            nc.scalar.activation(z, ps[:, 2, 0:1], ACT.Gelu, bias=bp1[:, 0:1]).then_inc(R["z_kept"], 1)
            keep_turned(1, slice(0, S - P))
            act.wait_ge(R["we_in"], 64)
            for f in range(FEC):
                act.wait_ge(R["hid_ready"], f + 1)
                nc.scalar.activation(wide[:, f, :], ps[:, 4 + f, :], ACT.Gelu, bias=be1[:, f:f + 1]).then_inc(R["hid_kept"], 1)

        def r2_vector(v):
            layernorm(nc, link, xb[:, 0:NT - 1, :], xn[:, 0:NT - 1, :], stats, NT - 1).then_inc(R["xn_ready"], 1)
            v.wait_ge(R["we_in"], 64)
            for h in range(DC):
                v.wait_ge(R["mid_ready"], h + 1)
                nc.vector.tensor_scalar(wide[:, FEC + h, :], ps[:, h, :], be2[:, h:h + 1], None, add).then_inc(R["mid_kept"], 1)
            for t in range(NT):
                v.wait_ge(R["out_ready"], t + 1)
                o = tmp[:, t % 2, :]
                link(nc.vector.tensor_tensor(o, ps[:, 2 + t, 0:D], bo2, add))
                link(nc.vector.scalar_tensor_tensor(out=o, in0=o, scalar=0.3, in1=xn[:, t, :], op0=mult, op1=add))
                last = nc.vector.scalar_tensor_tensor(out=xb[:, t, :], in0=o, scalar=gates[:, 6:7], in1=xb[:, t, :],
                                                      op0=mult, op1=add)
            link(last)

        M = {n: sem("A3_" + n) for n in ("mask_ready", "xn_ready", "turned", "keys_ready", "first_ready", "first_kept", "out_ready", "x_ready")}
        latT = keysT[:, :, S:KEYS3]

        def q_product(g, bank):
            for c in range(DC):
                last = nc.tensor.matmul(ps[:, bank, :], wqx[:, c, g * P:(g + 1) * P], latT[:, c, :], start=c == 0, stop=c == DC - 1)
            return last

        def key_product(g, kb, bank):
            for c in range(DC):
                last = nc.tensor.matmul(ps[:, bank, :], wkx[:, c, g * P:(g + 1) * P], keysT[:, c, kb * BANK:(kb + 1) * BANK],
                                        start=c == 0, stop=c == DC - 1)
            return last

        def value_product(g, kb, bank):
            for i in range(4):
                tok = slice((4 * kb + i) * P, (4 * kb + i + 1) * P)
                for c in range(DC):
                    last = nc.tensor.matmul(ps[:, bank, i * P:(i + 1) * P], keysT[:, c, tok], wvx[:, c, g * P:(g + 1) * P],
                                            start=c == 0, stop=c == DC - 1)
            return last

        def by_token(bank):
            return ps[:, bank, :].rearrange("p (i d) -> p i d", i=4)

        def jobs3(g):
            def keys(kb):
                def copy(v):
                    for s in range(2):
                        r = slice(64 * s, 64 * s + 64)
                        last = nc.vector.tensor_copy(kH[g % 2][s][r, kb * BANK:(kb + 1) * BANK], ps[r, 7, :])
                    return last

                return lambda pe: key_product(g, kb, 7), copy

            def vals(kb):
                return (lambda pe: value_product(g, kb, 7),
                        lambda v: nc.vector.tensor_copy(vh[g % 2][:, 4 * kb:4 * kb + 4, :], by_token(7)))

            return [q_job(wqx, latT, g), keys(0), keys(1), vals(0), vals(1)]

        firsts = [(2, lambda bank: key_product(0, 0, bank), "keys", 0), (3, lambda bank: value_product(0, 0, bank), "values", 0),
                  (4, lambda bank: q_product(0, bank), "queries", 0), (5, lambda bank: key_product(0, 1, bank), "keys", 1),
                  (6, lambda bank: value_product(0, 1, bank), "values", 1)]

        def keep_first(bank, product, kind, kb):
            if kind == "keys":
                for s in range(2):
                    r = slice(64 * s, 64 * s + 64)
                    last = nc.scalar.activation(kH[0][s][r, kb * BANK:(kb + 1) * BANK], ps[r, bank, :], ACT.Copy)
                return last
            if kind == "values":
                return nc.scalar.activation(vh[0][:, 4 * kb:4 * kb + 4, :], by_token(bank), ACT.Copy)
            return nc.scalar.activation(qT[0][:, :], ps[:, bank, :], ACT.Copy, scale=-DH2 ** -0.5)

        att3 = attention(nc, sem, "a3", ps, ident, 2, HP, KEYS3 // P,
                         lambda g, s, qt: qT[g % 2][:, qt * P:(qt + 1) * P],
                         lambda g, s, kb: kH[g % 2][s][:, kb * BANK:(kb + 1) * BANK],
                         lambda g, s, kc: vh[g % 2][:, kc, s * DH2:(s + 1) * DH2], DH2, mask3[:, :],
                         ([pbuf[:, i, :] for i in range(4)], sums, recip, least,
                          work[:, :].rearrange("p (s c q) -> p s c q", s=2, c=KEYS3 // P)), wide,
                         jobs=jobs3)

        def l3_tensor(pe, background={}):
            def project(first):
                first[1](first[0]).then_inc(M["first_ready"], 1)

            pe.wait_ge(M["keys_ready"], DC)
            for first in firsts[:2]:
                project(first)
            pe.wait_ge(M["xn_ready"], 1)
            pe_turn(xn, M["turned"])
            pe.wait_ge(M["keys_ready"], 2 * DC)
            for first in firsts[2:]:
                project(first)
            pe.wait_ge(M["first_kept"], len(firsts))
            att3[0](pe, background)
            pe.wait_ge(att3[3], HP)
            for t in range(NT):
                for g in range(HP):
                    last = nc.tensor.matmul(ps[:, t, 0:D], wide[:, g, t * P:(t + 1) * P], wox[:, g, :], start=g == 0, stop=g == HP - 1)
                last.then_inc(M["out_ready"], 1)

        def l3_scalar(act):
            for c in range(DC):
                nc.scalar.activation(keysT[:, c, 0:S], ctxT[:, c, :], ACT.Identity, bias=ln3[:, 1, c:c + 1],
                                     scale=ln3[:, 0, c:c + 1]).then_inc(M["keys_ready"], 1)
            for n, first in enumerate(firsts):
                if n == 2:
                    for c in range(DC):
                        act.wait_ge(M["turned"], c + 1)
                        nc.scalar.activation(latT[:, c, :], ps[:, c, :], ACT.Identity, bias=ln3[:, 3, c:c + 1],
                                             scale=ln3[:, 2, c:c + 1]).then_inc(M["keys_ready"], 1)
                act.wait_ge(M["first_ready"], n + 1)
                keep_first(*first).then_inc(M["first_kept"], 1)
            att3[2](act)

        def l3_vector(v, background={}):
            layernorm(nc, link, xb, xn, stats, twice=True).then_inc(M["xn_ready"], 1)
            nc.vector.tensor_scalar(mask3[:, 0:S], mask_u8[:, :], 0.0, FMAX, ALU.is_equal, mult).then_inc(M["mask_ready"], 1)
            nc.vector.memset(mask3[:, S:KEYS3], 0.0).then_inc(M["mask_ready"], 1)
            v.wait_ge(M["mask_ready"], 2)
            v.wait_ge(M["turned"], DC)
            att3[1](v, background)
            for t in range(NT):
                v.wait_ge(M["out_ready"], t + 1)
                last = nc.vector.scalar_tensor_tensor(out=xb[:, t, :], in0=ps[:, t, 0:D], scalar=gates[:, 3:4],
                                                      in1=xb[:, t, :], op0=mult, op1=add)
            last.then_inc(M["x_ready"], 1)
            v.wait_ge(M["x_ready"], 1)

        Q = {n: sem("Q3_" + n) for n in ("xn_ready", "xq_ready", "x_ready", "ready", "kept")}
        amax, xscale = small[:, 0:4], small[:, 4:8]

        def quantise_rows():
            nc.vector.wait_ge(Q["xn_ready"], 1)
            yield from quantise(nc, link, xn[:, :, :], NT, amax, xscale)

        def linear_jobs():
            def keep_x(c):
                return lambda v: nc.vector.tensor_copy(xqT[:, c, :], ps[:, 7, :])

            def linear(half):
                def product(pe):
                    for t in (2 * half, 2 * half + 1):
                        for c in range(DC):
                            last = nc.tensor.matmul(ps[:, 7, t % 2 * D:(t % 2 + 1) * D], xqT[:, c, t * P:(t + 1) * P], wq3[:, c, :],
                                                    start=c == 0, stop=c == DC - 1)
                    return last

                def scaled(v):
                    for t in (2 * half, 2 * half + 1):
                        last = nc.vector.scalar_tensor_tensor(out=tmp[:, t % 2, :], in0=ps[:, 7, t % 2 * D:(t % 2 + 1) * D],
                                                              scalar=xscale[:, t:t + 1], in1=scale3[:, :], op0=mult, op1=mult)
                        if t % 2 == 0:
                            link(last)
                    return last

                def residual(v):
                    for t in (2 * half, 2 * half + 1):
                        link(nc.vector.tensor_tensor(tmp[:, t % 2, :], tmp[:, t % 2, :], bias3, add))
                    for t in (2 * half, 2 * half + 1):
                        last = nc.vector.scalar_tensor_tensor(out=xb[:, t, :], in0=tmp[:, t % 2, :], scalar=gates[:, 7:8],
                                                              in1=xb[:, t, :], op0=mult, op1=add)
                    last.then_inc(Q["x_ready"], 1)
                    v.wait_ge(Q["x_ready"], half + 1)

                return [(product, scaled), (None, residual)]

            return on_vector(layernorm_steps(nc, link, xb, xn, stats), 7, Q["xn_ready"]) + \
                on_vector(quantise_rows(), 6, Q["xq_ready"]) + \
                [turn_job(xn, c, Q["xq_ready"], keep_x(c)) for c in range(DC)] + linear(0) + linear(1)

        def load_l2(sp):
            for dst, n in ((wo2, "L2_wo"), (wff1, "L2_wff1"), (wff2, "L2_wff2")):
                sp.dma_start(dst, a[n]).then_inc(arena_in, 16)

        def load_next(sp, b):
            sp.dma_start(xb2[:, :, :], x_d[b]).then_inc(x_in, 16)
            sp.dma_start(ctxb[:, :, :], a["ctx"][b]).then_inc(ctx_in, 16)

        def load_l3(sp, b):
            sp.wait_ge(R["picked"], 1)
            e = sp.value_load(pick[0:1, 0:1], min_val=0, max_val=E2 - 1)
            for dst, n in ((we1, "L2_we1"), (be1[:, :], "L2_be1"), (we2, "L2_we2"), (be2[:, :], "L2_be2")):
                sp.dma_start(dst, a[n][e]).then_inc(R["we_in"], 16)
            sp.dma_start(mask_u8[:, :], a["mask3"][b].partition_broadcast(P)).then_inc(mask_in, 16)
            for dst, n in ((wqx, "L3_wq"), (wkx, "L3_wk"), (wvx, "L3_wv"), (wox, "L3_wo")):
                sp.dma_start(dst, a[n]).then_inc(arena3_in, 16)
            sp.wait_ge(mask_in, 16)
            sp.wait_ge(arena3_in, 64)

        def store(sp, b):
            sp.wait_ge(Q["x_ready"], 2)
            sp.dma_start(out[b], xb[:, :, :]).then_inc(out_done, 16)
            sp.wait_ge(out_done, 16)

        link.n = 0
        norms = norm_jobs()
        alone = run_jobs(norms, N2["ready"], N2["kept"])
        with zeroed(since), nc.Block() as block:
            @block.sync
            def _(sp):
                load_next(sp, 0)
                for dst, n in loads:
                    sp.dma_start(dst, a[n]).then_inc(const_in, 16)
                load_l2(sp)
                load_l3(sp, 0)

            @block.tensor
            def _(pe):
                alone[0](pe)
                pe.wait_ge(N2["kept"], 2 * DC + 3)
                l2_tensor(pe)
                r2_tensor(pe)

            @block.scalar
            def _(act):
                l2_scalar(act)
                r2_scalar(act)

            @block.vector
            def _(v):
                for i in range(2):
                    nc.vector.memset(kH[i][0][64:P, :], 0.0)
                    link(nc.vector.memset(kH[i][1][0:64, :], 0.0))
                v.wait_ge(const_in, 16 * len(loads))
                alone[1](v)
                l2_vector(v)
                r2_vector(v)

        link.n = 0
        norm_steps = [n for n in range(0, 7 * 8) if n % 8 >= 5][-19:] + [56, 57, 58, 59, 60, 61, 62]
        linear_steps = [n for n in range(1, 24) if n % 8][:13] + [20, 22, 27, 29, 34, 36]

        def spread(steps, jobs):
            assert len(steps) == len(jobs)
            at = {}
            for n, job in zip(steps, jobs):
                at.setdefault(n, []).append(job)
            return at

        norms = spread(norm_steps, norm_jobs())
        linear = spread(linear_steps, linear_jobs())
        with nc.Fori(0, B - 1) as b, zeroed(since), nc.Block() as block:
            @block.sync
            def _(sp):
                load_next(sp, b + 1)
                sp.wait_ge(M["out_ready"], NT)
                load_l2(sp)
                store(sp, b)
                load_l3(sp, b + 1)

            @block.tensor
            def _(pe):
                l3_tensor(pe, norms)
                pe.wait_ge(att3[4], att3[5](norms)[2])
                pe.wait_ge(M["x_ready"], 1)
                l2_tensor(pe, linear)
                r2_tensor(pe)

            @block.scalar
            def _(act):
                l3_scalar(act)
                l2_scalar(act)
                r2_scalar(act)

            @block.vector
            def _(v):
                l3_vector(v, norms)
                l2_vector(v, linear)
                r2_vector(v)

        link.n = 0
        rest = run_jobs(linear_jobs(), Q["ready"], Q["kept"])
        with nc.Block() as block:
            @block.sync
            def _(sp):
                store(sp, B - 1)

            @block.tensor
            def _(pe):
                l3_tensor(pe)
                rest[0](pe)

            @block.scalar
            def _(act):
                l3_scalar(act)

            @block.vector
            def _(v):
                l3_vector(v)
                rest[1](v)


def kernel(**inputs):
    import numpy as _np
    import concourse.bacc as _bacc
    from concourse import mybir as _mybir
    from concourse.bass_utils import run_bass_kernel_spmd as _run

    i = {k: _np.asarray(v) for k, v in inputs.items()}

    def rows(w):
        return w.reshape(-1, P, w.shape[1]).transpose(1, 0, 2)

    def cols(v):
        return v.reshape(-1, P).T

    def tiles(x):
        return x.reshape(B, NT, P, D).transpose(0, 2, 1, 3)

    def heads_padded(w):
        z = _np.zeros((H0, HPAD) + w.shape[1:], w.dtype)
        z[:, :DK0] = w.reshape((H0, DK0) + w.shape[1:])
        return z.reshape((H0 * HPAD,) + w.shape[1:])

    consts = _np.zeros((P, 4, P), _np.float32)
    consts[:, 0] = _np.eye(P)
    consts[:, 1] = _np.triu(_np.ones((P, P)), 1)
    consts[:, 2] = 1
    e = _np.arange(E)
    consts[:, 3, :E] = (e % 2) * CAP * PAIRS + e // 2 + 1
    minus1 = _np.zeros((H1, H1, P), _np.float32)
    for h in range(H1):
        minus1[h, h] = -1
    gw1 = _np.zeros((3 * D, 36), _np.float32)
    gw1[:, 0:H1] = i["L1_xattn_igate_w"].T
    gw1[:, 32:36] = i["L1_xattn_fgate_w"].T
    gb1 = _np.zeros((36, 1), _np.float32)
    gb1[0:H1, 0] = i["L1_xattn_igate_b"]
    gb1[32:36, 0] = i["L1_xattn_fgate_b"]
    w_gate, w_up = (i["L0_ffn_" + n].reshape(PAIRS, 2, INTER, DC, P).transpose(0, 4, 3, 1, 2) for n in ("w_gate", "w_up"))
    wkv2, wkv3 = i["L2_xattn_Wkv"], i["L3_xattn_Wkv"]
    arrays = {
        "consts": consts,
        "gates": _np.concatenate([i["g_xattn"], i["g_ffn"]]),
        "vec": _np.stack([i["L0_xattn_bo"], i["L1_xattn_out_w"], i["L1_ffn_b2"], i["L2_ffn_bo"], i["L3_ffn_bias"]]),
        "block16": _np.repeat(_np.eye(P // DK0, dtype=_np.float32), DK0, axis=0),
        "token": _np.arange(S, dtype=_np.float32).reshape(NT, P).T,
        "place_none": SLOTS + _np.arange(SLOTS, dtype=_np.uint32).reshape(P, NT, TOPK),
        "minus1": minus1,
        "earlier": (_np.arange(7 * P)[None] < 3 * P + _np.arange(P)[:, None]).astype(_np.float32),
        "x": tiles(i["x"]),
        "ctx": tiles(i["ctx_1024"]),
        "ctxT": i["ctx_1024"].transpose(0, 2, 1).reshape(B, DC, P, S).transpose(0, 2, 1, 3),
        "mask0": i["mask_BxS2_if1"],
        "mask3": i["mask_BxS2_bk0"],
        "L0_wq": rows(i["L0_xattn_Wq"].T),
        "L0_wk": rows(i["L0_xattn_Wk"].T),
        "L0_wv": rows(heads_padded(i["L0_xattn_Wv"]).T),
        "L0_wo": rows(heads_padded(i["L0_xattn_Wo"].T)),
        "L0_bqk": _np.stack([cols(i["L0_xattn_bq"]), cols(i["L0_xattn_bk"])], axis=1),
        "L0_bv": heads_padded(i["L0_xattn_bv"]),
        "L0_gate": rows(i["L0_ffn_gate_w"].T),
        "L0_wgu": _np.concatenate([w_gate, w_up], axis=4),
        "L0_wd": i["L0_ffn_w_down"].reshape(PAIRS, 2, D, 2, IH).transpose(0, 4, 3, 1, 2),
        "L1_gw": rows(gw1),
        "L1_gb": gb1,
        "L1_wr": _np.repeat(cols(i["L1_ffn_w_router"])[:, :, None], P, axis=2),
        "L1_w1": rows(i["L1_ffn_W1"]),
        "L1_b1": cols(i["L1_ffn_b1"]),
        "L1_w2": rows(i["L1_ffn_W2"]),
        "L2_ln": _np.stack([cols(i["L2_xattn_" + n]) for n in ("ln_g", "ln_b", "cln_g", "cln_b")], axis=1),
        "L2_wq": rows(i["L2_xattn_Wq"]),
        "L2_wk": rows(_np.concatenate([wkv2[:, :DH2], wkv2[:, :DH2]], axis=1)),
        "L2_wv": rows(wkv2[:, DH2:]),
        "L2_wo": rows(i["L2_xattn_Wo"]),
        "L2_wff1": rows(i["L2_xattn_Wff1"]),
        "L2_wff2": rows(i["L2_xattn_Wff2"]),
        "L2_wp1": rows(i["L2_ffn_Wp1"]),
        "L2_bp1": cols(i["L2_ffn_bp1"]),
        "L2_wp2": i["L2_ffn_Wp2"],
        "L2_bp2": i["L2_ffn_bp2"][None],
        "L2_we1": i["L2_ffn_W1"].reshape(E2, DC, P, FE2).transpose(0, 2, 1, 3),
        "L2_be1": i["L2_ffn_b1"].reshape(E2, FEC, P).transpose(0, 2, 1),
        "L2_we2": i["L2_ffn_W2"].reshape(E2, FEC, P, D).transpose(0, 2, 1, 3),
        "L2_be2": i["L2_ffn_b2"].reshape(E2, DC, P).transpose(0, 2, 1),
        "L2_wof": rows(i["L2_ffn_Wo"]),
        "L3_ln": _np.stack([cols(i["L3_xattn_" + n]) for n in ("g1", "b1", "g2", "b2")], axis=1),
        "L3_wq": rows(i["L3_xattn_Wq"]),
        "L3_wk": rows(wkv3[:, :INNER]),
        "L3_wv": rows(wkv3[:, INNER:]),
        "L3_wo": rows(i["L3_xattn_Wout"]),
        "L3_w": i["L3_ffn_weight"].reshape(DC, P, D).transpose(1, 0, 2),
    }
    nc = _bacc.Bacc("TRN2", target_bir_lowering=False, num_devices=1)
    feed, aps = {}, {}
    for name, arr in arrays.items():
        arr = _np.ascontiguousarray(arr)
        feed[f"in_{name}"] = arr
        aps[name] = nc.dram_tensor(f"in_{name}", arr.shape, _mybir.dt.from_np(arr.dtype), kind="ExternalInput").ap()
    out = nc.dram_tensor("out_0", (B, P, NT, D), F32, kind="ExternalOutput").ap()
    program(nc, aps, out)
    r = _run(nc, [feed], core_ids=[0])
    return r.results[0]["out_0"].reshape(B, P, NT, D).transpose(0, 2, 1, 3).reshape(B, S, D)
```

```python
from contextlib import ExitStack, contextmanager

import concourse.bass as bass
import numpy as np
from concourse import mybir

F32 = mybir.dt.float32
BF16 = mybir.dt.bfloat16
I32 = mybir.dt.int32
U32 = mybir.dt.uint32
ALU = mybir.AluOpType
ACT = mybir.ActivationFunctionType
AX = mybir.AxisListType

P = 128
B, S, D = 4, 512, 256
NT = S // P
DC = D // P
TOK = B * S
BANK = 512
LN_EPS = 1e-5

H0, DK0 = 16, 16
HPAD = 32
QUADS = H0 * HPAD // P
E, TOPK, CAP, INTER = 64, 8, 64, 192
PAIRS = E // 2
IH = INTER // 2
SLOTS = E * CAP
H1, DH1 = 4, 64
F1 = 1024
FC1 = F1 // P
KEEP = S // 2
H2, DH2 = 16, 64
INNER = H2 * DH2
HP = H2 // 2
FF2 = 4 * D
FFC = FF2 // P
NAV, E2, FE2 = 128, 8, 512
FEC = FE2 // P
KEYS3 = 2 * S
QMAX = 127.0
ROUND = 12582912.0
RSQRT_BITS, RSQRT_STEPS = 1597463007.0, 3
NEG1E9, FMAX = 1.0e9, float(np.finfo(np.float32).max)

mult, add, subtract = ALU.mult, ALU.add, ALU.subtract


class Chain:

    def __init__(self, eng, sem):
        self.eng, self.sem, self.n = eng, sem, 0

    def __call__(self, ins):
        self.n += 1
        ins.then_inc(self.sem, 1)
        self.eng.wait_ge(self.sem, self.n)


def layernorm_steps(nc, link, src, dst, stats, tiles=NT, twice=False):
    s6, mv, rstd, var, half = (x[:, 0:tiles] for x in stats)
    for t in range(tiles):
        last = nc.vector.bn_stats(s6[:, t, :], src[:, t, :])
        if t == tiles // 2 - 1:
            yield last
    link(last)
    yield last
    for t in range(tiles):
        last = nc.vector.bn_aggr(mv[:, t, :], s6[:, t, :])
    link(last)

    def rsqrt():
        link(nc.vector.tensor_scalar(rstd.bitcast(I32), var.bitcast(I32), -0.5, RSQRT_BITS, mult, add))
        for _ in range(RSQRT_STEPS):
            link(nc.vector.tensor_tensor(half, var, rstd, mult))
            link(nc.vector.scalar_tensor_tensor(out=half, in0=half, scalar=-0.5, in1=rstd, op0=mult, op1=mult))
            link(nc.vector.scalar_tensor_tensor(out=rstd, in0=half, scalar=1.5, in1=rstd, op0=add, op1=mult))
            yield last

    link(nc.vector.tensor_scalar(var, mv[:, :, 1], LN_EPS, None, add))
    yield from rsqrt()
    if twice:
        first = mv[:, :, 1]
        link(nc.vector.tensor_tensor(half, mv[:, :, 1], rstd, mult))
        link(nc.vector.tensor_tensor(var, half, rstd, mult))
        nc.vector.tensor_copy(first, rstd)
        link(nc.vector.tensor_scalar(var, var, LN_EPS, None, add))
        yield last
        yield from rsqrt()
        link(nc.vector.tensor_tensor(rstd, rstd, first, mult))
    if tiles > NT:
        link(nc.vector.tensor_tensor(dst, src, mv[:, :, 0:1].broadcast_to(list(src.shape)), subtract))
        yield nc.vector.tensor_tensor(dst, dst, rstd.unsqueeze(2).broadcast_to(list(src.shape)), mult)
        return
    for t in range(tiles):
        last = nc.vector.tensor_scalar(dst[:, t, :], src[:, t, :], mv[:, t, 0:1], rstd[:, t:t + 1],
                                       subtract, mult)
        if t == tiles // 2 - 1:
            yield last
    yield last


def layernorm(*args, **kwargs):
    for last in layernorm_steps(*args, **kwargs):
        pass
    return last


def quantise(nc, link, src, tiles, amax, scale):
    link(nc.vector.tensor_reduce(amax, src, AX.X, ALU.max, apply_absolute_value=True))
    yield None
    link(nc.vector.tensor_scalar(scale, amax, 1e-8, 1.0 / QMAX, ALU.max, mult))
    link(nc.vector.reciprocal(amax, scale))
    yield None
    for t in range(tiles):
        last = nc.vector.tensor_scalar(src[:, t, :], src[:, t, :], amax[:, t:t + 1], ROUND, mult, add)
        if t == tiles // 2 - 1:
            yield None
    link(last)
    yield None
    link(nc.vector.tensor_scalar(src, src, ROUND, QMAX, subtract, ALU.min))
    yield None
    yield nc.vector.tensor_scalar(src, src, -QMAX - 1, None, ALU.max)


def attention(nc, sem, name, ps, ident, heads, groups, nk, q_of, k_of, v_of, rows, mask, bufs, out,
              jobs=None):
    banks = nk // 4
    ring = 4 // banks
    behind = ring // 2
    probs, sums, recip, least, pts = bufs
    np_ = len(probs)
    per = NT * heads
    steps = groups * per
    scores_ready = sem(name + "_scores_ready")
    least_ready = sem(name + "_least_ready")
    exp_ready = sem(name + "_exp_ready")
    probs_ready = sem(name + "_probs_ready")
    turned = sem(name + "_turned")
    turned_kept = sem(name + "_turned_kept")
    av_ready = sem(name + "_av_ready")
    av_kept = sem(name + "_av_kept")
    recip_ready = sem(name + "_recip_ready")
    jobs_ready = sem(name + "_jobs_ready")
    jobs_kept = sem(name + "_jobs_kept")

    def where(n):
        g, r = divmod(n, per)
        return g, r // heads, r % heads

    def scores(n):
        return ps[:, (n % ring) * banks:(n % ring + 1) * banks, :].rearrange("p b k -> p (b k)")

    each = len(jobs(0)) if jobs else 0

    def plan(background):
        before, need, count = {}, [0], 0
        for n in range(steps):
            g, i = divmod(n, per)
            own = jobs(g + 1)[i:i + 1] if jobs and g + 1 < groups else []
            before[n] = own + background.get(n, [])
            count += sum(job[0] is not None for job in before[n])
            if own and i == each - 1:
                need.append(count - sum(job[0] is not None for job in background.get(n, [])))
        return before, need, count

    def tensor(pe, background={}):
        before, need, _ = plan(background)
        done = [0]

        def project(job):
            if job[0] is None:
                return
            if done[0]:
                pe.wait_ge(jobs_kept, done[0])
            job[0](pe).then_inc(jobs_ready, 1)
            done[0] += 1

        def score(n):
            g, qt, s = where(n)
            if jobs and n % per == 0 and need[g]:
                pe.wait_ge(jobs_kept, need[g])
            if n >= ring:
                pe.wait_ge(exp_ready, n - ring + 1)
            for kb in range(banks):
                last = nc.tensor.matmul(scores(n)[:, kb * BANK:(kb + 1) * BANK], q_of(g, s, qt),
                                        k_of(g, s, kb), start=True, stop=True)
            last.then_inc(scores_ready, 1)

        def turn(n):
            pe.wait_ge(probs_ready, n + 1)
            for kb in range(banks):
                m = n * banks + kb
                if m >= 2:
                    pe.wait_ge(turned_kept, m - 1)
                for c in range(4):
                    kc = kb * 4 + c
                    last = nc.tensor.transpose(ps[:, 4 + m % 2, c * P:(c + 1) * P],
                                               probs[n % np_][:, kc * P:(kc + 1) * P], ident)
                last.then_inc(turned, 1)

        def values(g):
            pe.wait_ge(turned_kept, (g + 1) * per * banks)
            if g:
                pe.wait_ge(av_kept, g)
            for kc in range(nk):
                for s in range(heads):
                    last = nc.tensor.matmul(ps[rows * s:rows * (s + 1), 6, :], v_of(g, s, kc),
                                            pts[g % len(pts)][:, s, kc, :], start=kc == 0, stop=kc == nk - 1)
            last.then_inc(av_ready, 1)

        for n in range(ring):
            score(n)
        for n in range(steps):
            if n + ring < steps:
                score(n + ring)
            turn(n)
            for job in before[n]:
                project(job)
            if n % per == 0 and n:
                values(n // per - 1)
        values(groups - 1)

    def vector(v, background={}):
        before, _, _ = plan(background)
        done = [0]

        def keep_job(job):
            if job[0] is None:
                job[1](v)
                return
            v.wait_ge(jobs_ready, done[0] + 1)
            job[1](v).then_inc(jobs_kept, 1)
            done[0] += 1

        def find(n):
            v.wait_ge(scores_ready, n + 1)
            x = scores(n)
            if mask is None:
                nc.vector.tensor_reduce(least[:, n % 8:n % 8 + 1], x, AX.X, ALU.min).then_inc(least_ready, 1)
            else:
                nc.vector.tensor_tensor_reduce(out=x, in0=x, in1=mask, scale=1.0, scalar=FMAX, op0=add,
                                               op1=ALU.min, accum_out=least[:, n % 8:n % 8 + 1])\
                    .then_inc(least_ready, 1)

        def invert(n):
            v.wait_ge(exp_ready, n + 1)
            nc.vector.reciprocal(recip[:, n % 8:n % 8 + 1], sums[:, n % 8:n % 8 + 1]).then_inc(recip_ready, 1)

        def divide(n):
            v.wait_ge(recip_ready, n + 1)
            p = probs[n % np_]
            nc.vector.tensor_scalar(p, p, recip[:, n % 8:n % 8 + 1], None, mult).then_inc(probs_ready, 1)

        def keep_values(g):
            v.wait_ge(av_ready, g + 1)
            nc.vector.tensor_copy(out[:, g, :], ps[:, 6, :]).then_inc(av_kept, 1)

        for n in range(steps + behind):
            if behind > 1 and n >= behind:
                invert(n - behind)
            if n < steps:
                find(n)
            if behind == 1 and n:
                invert(n - 1)
            if n >= behind:
                divide(n - behind)
            for job in before[n - behind - 1] if n > behind else []:
                keep_job(job)
            if n % per == 2 + behind and n > per:
                keep_values(n // per - 1)
        for job in before[steps - 1]:
            keep_job(job)
        keep_values(groups - 1)

    def scalar(act, background={}):
        def exponent(n):
            act.wait_ge(least_ready, n + 1)
            if n >= np_:
                act.wait_ge(turned, (n - np_ + 1) * banks)
            nc.scalar.activation(probs[n % np_], scores(n), ACT.Exp, bias=least[:, n % 8:n % 8 + 1],
                                 scale=-1.0, accum_out=sums[:, n % 8:n % 8 + 1]).then_inc(exp_ready, 1)

        def keep_turned(n):
            g, qt, s = where(n)
            if n % per == 0 and g >= len(pts):
                act.wait_ge(av_ready, g - len(pts) + 1)
            for kb in range(banks):
                m = n * banks + kb
                act.wait_ge(turned, m + 1)
                nc.scalar.activation(pts[g % len(pts)][:, s, kb * 4:kb * 4 + 4, qt * P:(qt + 1) * P],
                                     ps[:, 4 + m % 2, :].rearrange("p (c q) -> p c q", c=4),
                                     ACT.Copy).then_inc(turned_kept, 1)

        for n in range(steps + behind):
            if n < steps:
                exponent(n)
            if n >= behind:
                keep_turned(n - behind)
            if n in background:
                background[n](act)

    return tensor, vector, scalar, av_kept, jobs_kept, plan


def turn_job(nc, ps, ident, src, c, ready, keep_it):
    def product(pe):
        pe.wait_ge(ready, 1)
        for t in range(NT):
            last = nc.tensor.transpose(ps[:, 7, t * P:(t + 1) * P], src[:, t, c * P:(c + 1) * P], ident)
        return last

    return product, keep_it


def on_vector(gen, slots, ready):
    def one(v):
        next(gen)

    def rest(v):
        for last in gen:
            pass
        last.then_inc(ready, 1)

    return [(None, one)] * (slots - 1) + [(None, rest)]


def run_jobs(jobs, ready, kept):
    def tensor(pe):
        for n, job in enumerate(j for j in jobs if j[0] is not None):
            if n:
                pe.wait_ge(kept, n)
            job[0](pe).then_inc(ready, 1)

    def vector(v):
        n = 0
        for product, copy in jobs:
            if product is None:
                copy(v)
            else:
                n += 1
                v.wait_ge(ready, n)
                copy(v).then_inc(kept, 1)

    return tensor, vector


def spread(steps, jobs):
    assert len(steps) == len(jobs)
    at = {}
    for n, job in zip(steps, jobs):
        at.setdefault(n, []).append(job)
    return at


def program(nc, a, out):
    ctx = ExitStack()
    with ctx:
        every = []

        def sem(name, scope=ctx):
            s = scope.enter_context(nc.semaphore(name))
            every.append(s)
            return s

        def keep(name, shape, dt=F32):
            return ctx.enter_context(nc.sbuf_tensor(name, shape, dt))

        @contextmanager
        def zeroed(since):
            yield
            nums = sorted(s.num for s in every[since:])
            starts = [n for n in nums if n - 1 not in nums]
            ends = [n + 1 for n in nums if n + 1 not in nums]
            for start, end in zip(starts, ends):
                nc.sync.sem_clear(range(start, end))
            nc.all_engine_barrier()

        x_d = nc.dram_tensor("x_scratch", [B, P, NT, D], F32, kind="Internal").ap()
        rows_d = nc.dram_tensor("normed_rows", [TOK + P, D], F32, kind="Internal").ap()
        taken_d = nc.dram_tensor("slot_token", [SLOTS, 1], U32, kind="Internal").ap()
        y_d = nc.dram_tensor("expert_rows", [SLOTS, D], F32, kind="Internal").ap()

        ps = ctx.enter_context(nc.psum_tensor("ps", [P, 8, BANK], F32))
        consts = keep("consts", [P, 4, P])
        gates = keep("gates", [P, 8])
        vec = keep("vec", [P, 5, D])
        wq3 = keep("wq3f", [P, DC, D], BF16)
        scale3 = keep("scale3f", [P, D])
        slot8 = keep("slot8", [P, (B + 2) * NT, TOPK], U32)
        weight8 = keep("weight8", [P, (B + 2) * NT, TOPK])
        taken = keep("taken", [P, PAIRS], U32)
        place8 = keep("place8", [P, NT, TOPK], U32)
        token_i = keep("token_i", [P, NT], U32)
        ident, upper, ones = consts[:, 0, :], consts[:, 1, :], consts[:, 2, :]
        keyrow = consts[:, 3, 0:E]
        bo0, outw1, b21, bo2, bias3 = (vec[:, i, :] for i in range(5))
        xb = keep("xb", [P, NT, D])
        xn = keep("xn", [P, NT, D])
        xnT = keep("xnT", [P, DC, S])
        ctxT = keep("ctxT", [P, DC, S])
        s6 = keep("s6", [P, 16, 6])
        mv = keep("mv", [P, 16, 2])
        stats = (s6, mv, keep("rstd", [P, 16]), keep("var", [P, 16]), keep("half", [P, 16]))
        least = keep("least", [P, 8])
        sums = keep("sums", [P, 8])
        recip = keep("recip", [P, 8])
        tmp = keep("tmp", [P, 2, D])

        consts_in = sem("consts_in")
        scattered = sem("scattered")
        gates_ready = sem("gates_ready")
        fill_ready = sem("fill_ready")
        fill_out = sem("fill_out")

        with nc.sbuf_tensor("zero_rows", [P, D], F32) as zero_rows, \
                nc.sbuf_tensor("no_token", [P, PAIRS], U32) as no_token, nc.Block() as block:
            @block.sync
            def _(sp):
                sp.dma_start(consts[:, :, :], a["consts"]).then_inc(consts_in, 16)
                sp.dma_start(gates[:, :], a["gates"].partition_broadcast(P)).then_inc(consts_in, 16)
                sp.dma_start(vec[:, :, :], a["vec"].partition_broadcast(P)).then_inc(consts_in, 16)
                sp.wait_ge(fill_ready, 4)
                sp.dma_start(rows_d[TOK:TOK + P, :], zero_rows[:, :]).then_inc(fill_out, 16)
                sp.dma_start(taken_d.rearrange("(p n) o -> p (n o)", p=P), no_token[:, :]).then_inc(fill_out, 16)
                sp.wait_ge(fill_out, 32)
                sp.wait_ge(consts_in, 48)

            @block.vector
            def _(v):
                nc.vector.memset(zero_rows[:, :], 0.0).then_inc(fill_ready, 1)
                nc.vector.memset(no_token[:, :], TOK).then_inc(fill_ready, 1)
                nc.vector.memset(slot8[:, B * NT:, :], 0).then_inc(fill_ready, 1)
                nc.vector.memset(weight8[:, B * NT:, :], 0.0).then_inc(fill_ready, 1)

            @block.scalar
            def _(act):
                act.wait_ge(consts_in, 48)
                nc.scalar.activation(gates[:, :], gates[:, :], ACT.Tanh).then_inc(gates_ready, 1)
                act.wait_ge(gates_ready, 1)

        def scatter():
            for t in range(NT):
                for k in range(TOPK):
                    nc.gpsimd.indirect_dma_start(
                        taken_d[:, :], bass.IndirectOffsetOnAxis(place8[:, t, k:k + 1], 0), token_i[:, t:t + 1], None,
                        bounds_check=SLOTS - 1, oob_is_err=False).then_inc(scattered, 16)

        layer0(nc, a, sem, every, zeroed, locals())
        with ExitStack() as scope:
            shared1 = layer1_weights(nc, scope)
            experts(nc, a, sem, locals())
            layer1(nc, a, sem, every, zeroed, locals())
        layers2to3(nc, a, sem, every, zeroed, locals(), out)


def layer0(nc, a, allocate, every, zeroed, G):
    ps, ident, upper, ones, keyrow = G["ps"], G["ident"], G["upper"], G["ones"], G["keyrow"]
    gates, bo0, slot8, weight8 = G["gates"], G["bo0"], G["slot8"], G["weight8"]
    xb, xn, xnT, ctxT, stats, tmp = G["xb"], G["xn"], G["xnT"], G["ctxT"], G["stats"], G["tmp"]
    least, sums, recip = G["least"], G["sums"], G["recip"]
    x_d, rows_d = G["x_d"], G["rows_d"]
    place8, token_i, scattered, scatter = G["place8"], G["token_i"], G["scattered"], G["scatter"]
    with ExitStack() as ctx:
        def keep(name, shape, dt=F32):
            return ctx.enter_context(nc.sbuf_tensor(name, shape, dt))

        def sem(name):
            return allocate(name, ctx)

        wq = keep("wq0", [P, DC, D])
        wk = keep("wk0", [P, DC, D])
        wv = keep("wv0", [P, DC, H0 * HPAD])
        wo = keep("wo0", [P, QUADS, D])
        wgate = keep("wgate0", [P, DC, E])
        bqk = keep("bqk0", [P, 2, DC])
        bv = keep("bv0", [P, H0 * HPAD])
        block16 = keep("block16", [P, P // DK0])
        mask_i = keep("mask_i", [P, S], I32)
        mask_f = keep("mask_f", [P, S])
        mask_add = keep("mask_add", [P, S])
        qT = keep("qT0", [P, DC, S])
        kT = keep("kT0", [P, DC, S])
        kH = keep("kH0", [P, H0, S])
        vh = keep("v0", [P, NT, H0 * HPAD])
        probs = [keep(f"probs0_{i}", [P, S])[:, :] for i in range(6)]
        pt = [keep(f"pt0_{i}", [P, 4, NT, S]) for i in range(2)]
        oT = keep("oT0", [P, QUADS, S])
        x1 = keep("x1", [P, NT, D])
        x1n = keep("x1n", [P, NT, D])
        x1nT = keep("x1nT", [P, DC, S])
        lg = keep("lg", [P, NT, E])
        rep = keep("rep", [P, NT, E])
        sel = keep("sel", [P, NT, E])
        ex = keep("ex", [P, NT, E])
        valid = keep("valid", [P, NT, E])
        key = keep("key", [P, NT, E])
        before = keep("before", [P, NT + 1, E])
        m8 = keep("m8", [P, NT, TOPK])
        e8 = keep("e8", [P, NT, TOPK])
        k8 = keep("k8", [P, NT, TOPK])
        w8 = keep("w8", [P, NT, TOPK])
        off8 = keep("off8", [P, NT, TOPK])
        negm = keep("negm", [P, NT])
        s8 = keep("s8", [P, NT])
        r8 = keep("r8", [P, NT])
        junk = [buf[:, i, :].rearrange("p (k e) -> p k e", e=E) for buf in (kT, xnT) for i in range(DC)]
        token_f = keep("token_f", [P, NT])

        w_in = allocate("w0_in")
        before_zero = allocate("before_zero")
        with nc.Block() as block:
            @block.sync
            def _(sp):
                for dst, n in ((wq, "L0_wq"), (wk, "L0_wk"), (wv, "L0_wv"), (wo, "L0_wo"), (wgate, "L0_gate")):
                    sp.dma_start(dst[:, :, :], a[n]).then_inc(w_in, 16)
                sp.dma_start(bqk[:, :, :], a["L0_bqk"]).then_inc(w_in, 16)
                sp.dma_start(bv[:, :], a["L0_bv"].partition_broadcast(P)).then_inc(w_in, 16)
                sp.dma_start(block16[:, :], a["block16"]).then_inc(w_in, 16)
                sp.dma_start(token_f[:, :], a["token"]).then_inc(w_in, 16)
                sp.wait_ge(w_in, 9 * 16)

            @block.vector
            def _(v):
                nc.vector.memset(before[:, 0, :], 0.0).then_inc(before_zero, 1)
                v.wait_ge(before_zero, 1)

        since = len(every)
        x_in, ctxT_in, mask_in = sem("x0_in"), sem("ctxT0_in"), sem("mask0_in")
        order = sem("dve_order0")
        mask_ready = sem("mask0_ready")
        xn_ready = sem("xn0_ready")
        turned = sem("xn0_turned")
        xnT_ready = sem("xnT0_ready")
        prep_ready = sem("prep0_ready")
        prep_kept = sem("prep0_kept")
        out_ready = sem("out0_ready")
        x1n_ready = sem("x1n_ready")
        rows_out = sem("rows0_out")
        chosen = sem("chosen")
        exps = sem("exps0")
        before_ready = sem("before_ready")
        placed = sem("placed")
        x1_ready = sem("x1_ready")
        route_ready, route_kept = sem("route_ready"), sem("route_kept")
        link = Chain(nc.vector, order)

        NPREP = 2 * DC + NT
        def q_of(g, s, qt):
            return qT[:, (4 * g + s) // 8, qt * P:(qt + 1) * P]

        def k_of(g, s, kb):
            return kH[:, 4 * g + s, :]

        def v_of(g, s, kc):
            h = 4 * g + s
            return vh[:, kc, h * HPAD:(h + 1) * HPAD]

        att = attention(nc, sem, "a0", ps, ident, 4, QUADS, NT, q_of, k_of, v_of, HPAD, mask_add[:, :],
                        (probs, sums, recip, least, pt), oT)

        def load(sp, b):
            sp.dma_start(ctxT[:, :, :], a["ctxT"][b]).then_inc(ctxT_in, 16)
            sp.dma_start(xb[:, :, :], a["x"][b]).then_inc(x_in, 16)
            sp.dma_start(mask_i[:, :], a["mask0"][b].partition_broadcast(P)).then_inc(mask_in, 16)

        def store(sp, b):
            sp.wait_ge(x1n_ready, 1)
            sp.dma_start(x_d[b], x1[:, :, :]).then_inc(rows_out, 16)
            sp.dma_start(rows_d[0:TOK, :].rearrange("(b t p) d -> b p t d", b=B, t=NT)[b],
                         x1n[:, :, :]).then_inc(rows_out, 16)
            sp.wait_ge(rows_out, 32)

        def attend_tensor(pe, background={}):
            def prep(i, dst, pairs):
                if i >= 4:
                    pe.wait_ge(prep_kept, i - 3)
                for n, (l, r) in enumerate(pairs):
                    last = nc.tensor.matmul(dst, l, r, start=n == 0, stop=n == len(pairs) - 1)
                last.then_inc(prep_ready, 1)

            pe.wait_ge(ctxT_in, 16)
            for i in range(DC):
                prep(i, ps[:, 2 + i % 4, :], [(wk[:, c, i * P:(i + 1) * P], ctxT[:, c, :]) for c in range(DC)])
            for t in range(NT):
                i = DC + t
                prep(i, ps[:, 2 + i % 4, :], [(ctxT[:, c, t * P:(t + 1) * P], wv[:, c, :]) for c in range(DC)])
            pe.wait_ge(xn_ready, 1)
            for c in range(DC):
                for t in range(NT):
                    last = nc.tensor.transpose(ps[:, c, t * P:(t + 1) * P], xn[:, t, c * P:(c + 1) * P], ident)
                last.then_inc(turned, 1)
            for j in range(DC):
                i = DC + NT + j
                if j == 0:
                    pe.wait_ge(xnT_ready, DC)
                prep(i, ps[:, 2 + i % 4, :], [(wq[:, c, j * P:(j + 1) * P], xnT[:, c, :]) for c in range(DC)])
            pe.wait_ge(prep_kept, NPREP + 1)
            att[0](pe, background)
            pe.wait_ge(att[3], QUADS)
            for t in range(NT):
                for g in range(QUADS):
                    last = nc.tensor.matmul(ps[:, t, 0:D], oT[:, g, t * P:(t + 1) * P], wo[:, g, :],
                                            start=g == 0, stop=g == QUADS - 1)
                last.then_inc(out_ready, 1)
        def attend_scalar(act, background={}):
            for c in range(DC):
                act.wait_ge(turned, c + 1)
                nc.scalar.activation(xnT[:, c, :], ps[:, c, :], ACT.Copy).then_inc(xnT_ready, 1)
            att[2](act, background)

        def attend_vector(v, background={}):
            v.wait_ge(x_in, 16)
            layernorm(nc, link, xb, xn, stats).then_inc(xn_ready, 1)
            v.wait_ge(mask_in, 16)
            link(nc.vector.tensor_scalar(mask_f[:, :], mask_i[:, :], 0.0, None, ALU.not_equal))
            nc.vector.tensor_scalar(mask_add[:, :], mask_f[:, :], -NEG1E9, NEG1E9, mult, add).then_inc(mask_ready, 1)
            for i in range(DC):
                v.wait_ge(prep_ready, i + 1)
                nc.vector.scalar_tensor_tensor(out=kT[:, i, :], in0=ps[:, 2 + i % 4, :], scalar=bqk[:, 1, i:i + 1],
                                               in1=mask_f[:, :], op0=add, op1=mult).then_inc(prep_kept, 1)

            def by_heads(first, heads):
                for h in range(first, first + heads):
                    last = nc.vector.tensor_scalar(kH[:, h, :], kT[:, h // 8, :], block16[:, h % 8:h % 8 + 1], None, mult)
                return last

            for t in range(NT):
                i = DC + t
                v.wait_ge(prep_ready, i + 1)
                nc.vector.tensor_tensor(vh[:, t, :], ps[:, 2 + i % 4, :], bv[:, :], add).then_inc(prep_kept, 1)
                if t:
                    v.wait_ge(prep_kept, DC)
                    by_heads(H0 // 4 * (t - 1), H0 // 4)
            for j in range(DC):
                i = DC + NT + j
                v.wait_ge(prep_ready, i + 1)
                nc.vector.tensor_scalar(qT[:, j, :], ps[:, 2 + i % 4, :], bqk[:, 0, j:j + 1], -DK0 ** -0.5,
                                        add, mult).then_inc(prep_kept, 1)
                if j == 0:
                    by_heads(H0 // 4 * 3, H0 // 4).then_inc(prep_kept, 1)
            v.wait_ge(mask_ready, 1)
            att[1](v, background)
            if background:
                v.wait_ge(rows_out, 32)
            for t in range(NT):
                v.wait_ge(out_ready, t + 1)
                link(nc.vector.tensor_tensor(tmp[:, t % 2, :], ps[:, t, 0:D], bo0, add))
                last = nc.vector.scalar_tensor_tensor(out=x1[:, t, :], in0=tmp[:, t % 2, :], scalar=gates[:, 0:1],
                                                      in1=xb[:, t, :], op0=mult, op1=add)
            last.then_inc(x1_ready, 1)
            v.wait_ge(x1_ready, 1)

        def keep_x1nT(c):
            return lambda v: nc.vector.tensor_copy(x1nT[:, c, :], ps[:, 7, :])

        def by_tile():
            return ps[:, 7, 0:NT * E].rearrange("p (t e) -> p t e", t=NT)

        def logits_job():
            def product(pe):
                for t in range(NT):
                    for c in range(DC):
                        last = nc.tensor.matmul(ps[:, 7, t * E:(t + 1) * E], x1nT[:, c, t * P:(t + 1) * P],
                                                wgate[:, c, :], start=c == 0, stop=c == DC - 1)
                return last

            def copy(v):
                for t in range(NT):
                    last = nc.vector.max(m8[:, t, :], by_tile()[:, t, :])
                link(last)
                return nc.vector.tensor_copy(lg[:, :, :], by_tile())

            return product, copy

        def choose():
            nc.vector.tensor_scalar(negm[:, :], m8[:, :, 0], -1.0, None, mult).then_inc(chosen, 1)
            nc.vector.wait_ge(chosen, 1)
            for t in range(NT):
                last = nc.vector.match_replace(rep[:, t, :], m8[:, t, :], lg[:, t, :], -FMAX)
            link(last)
            yield last
            link(nc.vector.tensor_tensor(sel[:, :, :], rep[:, :, :], lg[:, :, :], ALU.not_equal))
            yield last
            for t in range(NT):
                last = nc.vector.tensor_tensor(before[:, t + 1, :], before[:, t, :], sel[:, t, :], add)
                if t < NT - 1:
                    link(last)
            yield last

        def exponents(act):
            act.wait_ge(chosen, 1)
            for t in range(NT):
                nc.scalar.activation(ex[:, t, :], lg[:, t, :], ACT.Exp, bias=negm[:, t:t + 1])
                last = nc.scalar.activation(e8[:, t, :], m8[:, t, :], ACT.Exp, bias=negm[:, t:t + 1],
                                            accum_out=s8[:, t:t + 1])
            last.then_inc(exps, 1)

        def position_job():
            def product(pe):
                pe.wait_ge(before_ready, 1)
                for t in range(NT):
                    nc.tensor.matmul(ps[:, 7, t * E:(t + 1) * E], upper, sel[:, t, :], start=True, stop=False)
                    last = nc.tensor.matmul(ps[:, 7, t * E:(t + 1) * E], ones, before[:, t, :], start=False, stop=True)
                return last

            def copy(v):
                nc.vector.scalar_tensor_tensor(out=valid[:, :, :], in0=by_tile(), scalar=float(CAP), in1=sel[:, :, :],
                                               op0=ALU.is_lt, op1=mult)
                for t in range(NT):
                    last = nc.vector.scalar_tensor_tensor(out=key[:, t, :], in0=by_tile()[:, t, :], scalar=float(PAIRS),
                                                          in1=keyrow, op0=mult, op1=add)
                return last

            return product, copy

        def place(b):
            nc.vector.tensor_copy(before[:, 0, :], before[:, NT, :])
            nc.vector.wait_ge(exps, 1)
            link(nc.vector.reciprocal(r8[:, :], s8[:, :]))
            for t in range(NT):
                last = nc.vector.scalar_tensor_tensor(out=ex[:, t, :], in0=ex[:, t, :], scalar=r8[:, t:t + 1],
                                                      in1=sel[:, t, :], op0=mult, op1=mult)
            link(last)
            yield last
            nc.vector.tensor_tensor(ex[:, :, :], ex[:, :, :], valid[:, :, :], mult)
            link(nc.vector.tensor_tensor(key[:, :, :], key[:, :, :], valid[:, :, :], mult))
            yield last
            for t in range(NT):
                last = nc.vector.max(k8[:, t, :], key[:, t, :])
            link(last)
            yield last
            for t in range(NT):
                for k in range(TOPK):
                    last = nc.vector.scalar_tensor_tensor(out=junk[t][:, k, :], in0=key[:, t, :], scalar=k8[:, t, k:k + 1],
                                                          in1=ex[:, t, :], op0=ALU.is_equal, op1=mult,
                                                          accum_out=w8[:, t, k:k + 1])
                    if k == TOPK // 2 - 1:
                        yield last
                if t < NT - 1:
                    yield last
            link(last)
            nc.vector.tensor_copy(weight8[:, bass.ds(b * NT, NT), :], w8[:, :, :])
            nc.vector.tensor_scalar(slot8[:, bass.ds(b * NT, NT), :], k8[:, :, :], -1.0, 0.0, add, ALU.max)
            link(nc.vector.tensor_scalar(off8[:, :, :], k8[:, :, :], 0.0, float(2 * SLOTS), ALU.is_equal, mult))
            yield last
            link(nc.vector.scalar_tensor_tensor(out=place8[:, :, :], in0=k8[:, :, :], scalar=-1.0, in1=off8[:, :, :],
                                                op0=add, op1=add))
            link(nc.vector.tensor_copy(token_i[:, :], token_f[:, :]))
            yield nc.vector.tensor_scalar(token_f[:, :], token_f[:, :], float(S), None, add)

        def routing(b):
            return on_vector(layernorm_steps(nc, link, x1, x1n, stats), 7, x1n_ready) + \
                [turn_job(nc, ps, ident, x1n, c, x1n_ready, keep_x1nT(c)) for c in range(DC)] + \
                [logits_job()] + on_vector(choose(), 3, before_ready) + \
                [position_job()] + on_vector(place(b), 12, placed)

        def restart():
            link.n = 0

        restart()
        with zeroed(since), nc.Block() as block:
            @block.sync
            def _(sp):
                load(sp, 0)

            @block.tensor
            def _(pe):
                attend_tensor(pe)

            @block.scalar
            def _(act):
                attend_scalar(act)

            @block.vector
            def _(v):
                attend_vector(v)

        route_steps = list(range(1, 8)) + [10, 12, 15] + [18, 19, 20] + [24] + list(range(28, 40))
        exponents_step = 23
        with nc.Fori(1, B) as b, zeroed(since), nc.Block() as block:
            restart()
            route = spread(route_steps, routing(b - 1))

            @block.sync
            def _(sp):
                load(sp, b)
                store(sp, b - 1)

            @block.tensor
            def _(pe):
                attend_tensor(pe, route)

            @block.scalar
            def _(act):
                attend_scalar(act, {exponents_step: exponents})

            @block.vector
            def _(v):
                attend_vector(v, route)

            @block.gpsimd
            def _(pool):
                pool.wait_ge(placed, 1)
                scatter()
                pool.wait_ge(scattered, b * (NT * TOPK * 16))

        restart()
        with zeroed(since), nc.Block() as block:
            alone = run_jobs(routing(B - 1), route_ready, route_kept)

            @block.sync
            def _(sp):
                store(sp, B - 1)

            @block.tensor
            def _(pe):
                alone[0](pe)

            @block.scalar
            def _(act):
                exponents(act)

            @block.vector
            def _(v):
                alone[1](v)


def experts(nc, a, sem, G):
    ps, ident, taken, rows_d, taken_d, y_d = (G[k] for k in ("ps", "ident", "taken", "rows_d", "taken_d", "y_d"))
    ones, wq3, scale3, shared1 = (G[k] for k in ("ones", "wq3", "scale3", "shared1"))
    scattered, scatter = G["scattered"], G["scatter"]
    RING = 4
    N = PAIRS // RING
    with ExitStack() as ctx:
        def keep(name, shape, dt=F32, count=RING):
            return [ctx.enter_context(nc.sbuf_tensor(f"{name}_{i}", shape, dt)) for i in range(count)]

        wgu = keep("wgu", [P, DC, 2, 2 * INTER], count=2 * RING)
        wd = keep("wd", [IH, 2, 2, D], count=2 * RING)
        column = keep("column", [P, 1], U32)
        xg = keep("xg", [P, D])
        xgT = keep("xgT", [P, DC, P])
        h = keep("h", [P, INTER])
        hT = keep("hT", [IH, 2, P])
        y = keep("y", [P, D])

        w3 = ctx.enter_context(nc.sbuf_tensor("w3", [P, 2, D], F32))
        w3_d = ctx.enter_context(nc.sbuf_tensor("w3_d", [P, 2, P], F32))
        w3_s = ctx.enter_context(nc.sbuf_tensor("w3_s", [P, 4], F32))
        shared_in = sem("shared_in")
        w3_order, w3_ready, w3_turned, w3_kept = (sem(n) for n in ("w3_order", "w3_ready", "w3_turned", "w3_kept"))
        taken_in = sem("taken_in")
        wgu_in, wd_in = ([sem(f"{n}_in_{i}") for i in range(2 * RING)] for n in ("wgu", "wd"))
        column_ready = [sem(f"column_ready_{i}") for i in range(RING)]
        rows_in = [sem(f"xg_in_{i}") for i in range(RING)]
        turned = [sem(f"xg_turned_{i}") for i in range(RING)]
        xgT_ready = [sem(f"xgT_ready_{i}") for i in range(RING)]
        gu_ready = [sem(f"gu_ready_{i}") for i in range(RING)]
        silu_ready = [sem(f"silu_ready_{i}") for i in range(RING)]
        h_ready = [sem(f"h_ready_{i}") for i in range(RING)]
        h_turned = [sem(f"h_turned_{i}") for i in range(RING)]
        hT_ready = [sem(f"hT_ready_{i}") for i in range(RING)]
        y_ready = [sem(f"ye_ready_{i}") for i in range(RING)]
        y_kept = [sem(f"ye_kept_{i}") for i in range(RING)]
        y_out = [sem(f"ye_out_{i}") for i in range(RING)]

        with nc.Block() as block:
            @block.sync
            def _(sp):
                def load(i, pair):
                    sp.dma_start(wgu[i][:, :, :, :], a["L0_wgu"][pair]).then_inc(wgu_in[i], 16)
                    sp.dma_start(wd[i][:, :, :, :], a["L0_wd"][pair]).then_inc(wd_in[i], 16)

                y_rows = y_d.rearrange("(p r n) h -> r n p h", p=P, r=N)
                sp.dma_start(w3[:, :, :], a["L3_w"]).then_inc(shared_in, 16)
                for i in range(RING):
                    load(i, i)
                for dst, n in shared1:
                    whole = tuple(slice(None) for _ in dst.shape)
                    sp.dma_start(dst[whole], a[n]).then_inc(shared_in, 16)
                for i in range(RING, 2 * RING):
                    load(i, i)
                sp.wait_ge(scattered, B * NT * TOPK * 16)
                sp.dma_start(taken[:, :], taken_d.rearrange("(p n) o -> p (n o)", p=P)).then_inc(taken_in, 16)
                with sp.Fori(1, N // 2) as q:
                    for half in range(2):
                        for i in range(RING):
                            done, w = q * 2 + half - 1, half * RING + i
                            sp.wait_ge(gu_ready[i], done)
                            sp.dma_start(wgu[w][:, :, :, :], a["L0_wgu"][q * 2 * RING + w]).then_inc(wgu_in[w], 16)
                            sp.wait_ge(y_ready[i], done)
                            sp.dma_start(wd[w][:, :, :, :], a["L0_wd"][q * 2 * RING + w]).then_inc(wd_in[w], 16)
                            sp.wait_ge(y_kept[i], done)
                            sp.dma_start(y_rows[done - 1, i], y[i][:, :]).then_inc(y_out[i], 16)
                for done in (N - 1, N):
                    for i in range(RING):
                        sp.wait_ge(y_kept[i], done)
                        sp.dma_start(y_rows[done - 1, i], y[i][:, :]).then_inc(y_out[i], 16)
                sp.wait_ge(shared_in, 16 * (1 + len(shared1)))
                for i in range(RING):
                    sp.wait_ge(y_out[i], 16 * N)

            @block.gpsimd
            def _(pool):
                scatter()
                pool.wait_ge(taken_in, 16)

                def gather(done, i, at):
                    nc.gpsimd.tensor_copy(column[i][:, :], taken[:, bass.ds(at, 1)]).then_inc(column_ready[i], 1)
                    pool.wait_ge(taken_in, 16)
                    pool.wait_ge(column_ready[i], done)
                    nc.gpsimd.indirect_dma_start(xg[i][:, :], None, rows_d[:, :], bass.IndirectOffsetOnAxis(column[i][:, :], 0),
                                                 bounds_check=TOK + P - 1, oob_is_err=False).then_inc(rows_in[i], 16)

                for i in range(RING):
                    gather(1, i, i)
                with pool.Fori(2, N + 1) as done:
                    for i in range(RING):
                        at = pool.snap((done - 1) * RING + i)
                        pool.wait_ge(turned[i], done - 1)
                        gather(done, i, at)

            @block.tensor
            def _(pe):
                def turn(r, i):
                    pe.wait_ge(rows_in[i], 16 * r + 16)
                    for c in range(DC):
                        last = nc.tensor.transpose(ps[:, i % 2, c * P:(c + 1) * P], xg[i][:, c * P:(c + 1) * P], ident)
                    last.then_inc(turned[i], 1)

                def up(r, i, q, half):
                    w = half * RING + i
                    pe.wait_ge(wgu_in[w], 16 * q + 16)
                    pe.wait_ge(xgT_ready[i], r + 1)
                    for c in range(DC):
                        for e in range(2):
                            last = nc.tensor.matmul(ps[e * CAP:(e + 1) * CAP, 2 + i % 2, 0:2 * INTER],
                                                    xgT[i][:, c, e * CAP:(e + 1) * CAP], wgu[w][:, c, e, :],
                                                    start=c == 0, stop=c == DC - 1)
                    last.then_inc(gu_ready[i], 1)

                def turn_hidden(r, i):
                    pe.wait_ge(h_ready[i], r + 1)
                    for j in range(2):
                        last = nc.tensor.transpose(ps[0:IH, 6 + i % 2, j * P:(j + 1) * P], h[i][:, j * IH:(j + 1) * IH], ident)
                    last.then_inc(h_turned[i], 1)

                def down(r, i, q, half, first=False):
                    w = half * RING + i
                    pe.wait_ge(wd_in[w], 16 * q + 16)
                    pe.wait_ge(hT_ready[i], r + 1)
                    if i >= 2:
                        pe.wait_ge(y_kept[i - 2], r + 1)
                    elif not first:
                        pe.wait_ge(y_kept[i + 2], r)
                    for j in range(2):
                        for e in range(2):
                            last = nc.tensor.matmul(ps[e * CAP:(e + 1) * CAP, 4 + i % 2, 0:D], hT[i][:, j, e * CAP:(e + 1) * CAP],
                                                    wd[w][:, j, e, :], start=j == 0, stop=j == 1)
                    last.then_inc(y_ready[i], 1)

                def step(q, half, first=False, second=False, final=False):
                    r = q * 2 + half
                    for i in range(RING):
                        if i < RING - 1:
                            turn(r, i + 1)
                        elif not final:
                            turn(r + 1, 0)
                        up(r, i, q, half)
                        if i >= 1:
                            turn_hidden(r, i - 1)
                        elif not first:
                            turn_hidden(r - 1, RING - 1)
                        if i >= 2:
                            down(r, i - 2, q, half, first)
                        elif not first:
                            down(r - 1, i + RING - 2, q - 1 + half, 1 - half, second)

                pe.wait_ge(w3_ready, 1)
                for c in range(DC):
                    for o in range(2):
                        nc.tensor.transpose(ps[:, 6, c * D + o * P:c * D + (o + 1) * P], w3[:, o, c * P:(c + 1) * P], ident)
                for o in range(2):
                    last = nc.tensor.matmul(ps[:, 7, o * P:(o + 1) * P], ones, w3_d[:, o, :], start=True, stop=True)
                last.then_inc(w3_turned, 1)
                pe.wait_ge(w3_kept, 2)
                turn(0, 0)
                step(0, 0, first=True)
                step(0, 1, second=True)
                with pe.Fori(1, N // 2 - 1) as q:
                    step(q, 0)
                    step(q, 1)
                step(N // 2 - 1, 0)
                step(N // 2 - 1, 1, final=True)
                turn_hidden(N - 1, RING - 1)
                for i in (RING - 2, RING - 1):
                    down(N - 1, i, N // 2 - 1, 1)

            @block.scalar
            def _(act):
                def keep_turned(r, i):
                    act.wait_ge(turned[i], r + 1)
                    nc.scalar.activation(xgT[i][:, :, :], ps[:, i % 2, 0:D].rearrange("p (c s) -> p c s", c=DC),
                                         ACT.Copy).then_inc(xgT_ready[i], 1)

                def keep_hidden(r, i):
                    act.wait_ge(h_turned[i], r + 1)
                    nc.scalar.activation(hT[i][:, :, :], ps[0:IH, 6 + i % 2, 0:2 * P].rearrange("p (j s) -> p j s", j=2),
                                         ACT.Copy).then_inc(hT_ready[i], 1)

                def step(r, first=False, final=False):
                    for i in range(RING):
                        if i < RING - 1:
                            keep_turned(r, i + 1)
                        elif not final:
                            keep_turned(r + 1, 0)
                        act.wait_ge(gu_ready[i], r + 1)
                        nc.scalar.activation(h[i][:, :], ps[:, 2 + i % 2, 0:INTER], ACT.Silu).then_inc(silu_ready[i], 1)
                        if i >= 1:
                            keep_hidden(r, i - 1)
                        elif not first:
                            keep_hidden(r - 1, RING - 1)

                keep_turned(0, 0)
                step(0, first=True)
                with act.Fori(1, N - 1) as r:
                    step(r)
                step(N - 1, final=True)
                keep_hidden(N - 1, RING - 1)

            @block.vector
            def _(v):
                def hidden(r, i):
                    v.wait_ge(silu_ready[i], r + 1)
                    nc.vector.tensor_tensor(h[i][:, :], h[i][:, :], ps[:, 2 + i % 2, INTER:2 * INTER], mult).then_inc(h_ready[i], 1)

                def rows(r, i, first=False):
                    v.wait_ge(y_ready[i], r + 1)
                    if not first:
                        v.wait_ge(y_out[i], 16 * r)
                    nc.vector.tensor_copy(y[i][:, :], ps[:, 4 + i % 2, 0:D]).then_inc(y_kept[i], 1)

                def step(r, first=False, second=False):
                    for i in range(RING):
                        hidden(r, i)
                        if i >= 2:
                            rows(r, i - 2, first)
                        elif not first:
                            rows(r - 1, i + RING - 2, second)

                link = Chain(v, w3_order)
                v.wait_ge(shared_in, 16 * (1 + len(shared1)))
                for last in quantise(nc, link, w3[:, :, :], 2, w3_s[:, 0:2], w3_s[:, 2:4]):
                    pass
                link(last)
                for o in range(2):
                    last = nc.vector.tensor_scalar(w3_d[:, o, :], ident, w3_s[:, 2 + o:3 + o], None, mult)
                last.then_inc(w3_ready, 1)
                v.wait_ge(w3_turned, 1)
                nc.vector.tensor_copy(wq3[:, :, :], ps[:, 6, :].rearrange("p (c o) -> p c o", c=DC)).then_inc(w3_kept, 1)
                nc.vector.tensor_copy(scale3[:, :], ps[:, 7, 0:D]).then_inc(w3_kept, 1)

                step(0, first=True)
                step(1, second=True)
                with v.Fori(2, N) as r:
                    step(r)
                for i in (RING - 2, RING - 1):
                    rows(N - 1, i)


def layer1_weights(nc, scope):
    def keep(name, shape):
        return scope.enter_context(nc.sbuf_tensor(name, shape, F32))

    return [(keep("gw1", [P, 6, 36]), "L1_gw"),
            (keep("gb1", [36, 1]), "L1_gb"),
            (keep("minus1", [H1, H1, P]), "minus1"),
            (keep("wr1", [P, DC, P]), "L1_wr"),
            (keep("w11", [P, DC, F1]), "L1_w1"),
            (keep("b11", [P, FC1]), "L1_b1"),
            (keep("w21", [P, FC1, D]), "L1_w2"),
            (keep("earlier", [P, 7 * P]), "earlier")]


def side_by_side(*parts):
    places = [next(p) for p in parts]
    while any(p is not None for p in places):
        n = min((p, n) for n, p in enumerate(places) if p is not None)[1]
        places[n] = next(parts[n], None)


def layer1(nc, a, allocate, every, zeroed, G):
    ps, ident, gates, slot8, weight8 = (G[k] for k in ("ps", "ident", "gates", "slot8", "weight8"))
    x_d, y_d, outw1, b21 = (G[k] for k in ("x_d", "y_d", "outw1", "b21"))
    PAIR = 2
    LAG, LAG_MIX = 0.05, 8
    PRODUCT, KEEP_HEAD = 1, 3
    SUMS = (4, 4.1, 11, 12, 20, 24.3, 44, 45)
    TURN, GATES, MLSTM, NORM, MIX = 5, 5.4, 8, 25, 33
    with ExitStack() as ctx:
        def sem(name):
            return allocate(name, ctx)

        def keep(name, shape, dt=F32):
            return ctx.enter_context(nc.sbuf_tensor(name, shape, dt))

        def both(name, shape, dt=F32):
            return [keep(f"{name}_{u}", shape, dt) for u in range(PAIR)]

        def sems(name):
            return [sem(f"{name}_{u}") for u in range(PAIR)]

        gw1, gb1, minus1, wr1, w11, b11, w21, earlier = (t for t, _ in G["shared1"])
        xbs = [G["xb"], keep("xb_1", [P, NT, D])]
        xns = [G["xn"], keep("xn_1", [P, NT, D])]
        xnTs = [G["xnT"], keep("xnT_1", [P, DC, S])]
        ctxTs = [G["ctxT"], keep("ctxT_1", [P, DC, S])]
        tmps = [G["tmp"], keep("tmp_1", [P, 2, D])]
        statss = [G["stats"], tuple(keep(f"{n}_1", shape) for n, shape in (
            ("s6", [P, 16, 6]), ("mv", [P, 16, 2]), ("rstd", [P, 16]), ("var", [P, 16]), ("half", [P, 16])))]
        ctxbs = both("ctxb1", [P, NT, D])
        idx8s, w8s = both("idx8", [P, NT * TOPK], U32), both("w8b", [P, NT, TOPK])
        qHs = both("qH1", [P, H1, S])
        works = both("work1", [P, 8 * S])
        yg = both("yg1", [P, TOPK, D])
        yaccs = both("yacc1", [P, NT, D])
        eTs = both("eT1", [P, 4, S])
        vaugs = both("vaug1", [P, NT, H1, 66])
        rowss = both("rows1", [36, 4 * S + 4])
        stacks = both("stack1", [36, S])
        gTs, ens = both("gT1", [P, NT, 36]), both("en1", [P, NT, H1])
        hbs = both("hb1", [P, NT, H1, DH1])
        hns = [e[:, 0:2, :].rearrange("p a (b h d) -> p (a b) h d", b=2, h=H1) for e in eTs]
        smalls = both("small1", [P, 32])

        TILES = PAIR * NT
        y_in = [allocate(f"y_in_{i}") for i in range(2)]
        since = len(every)
        idx_ready, summed, sum_order = sem("B_idx_ready"), sem("B_summed"), sem("B_sum_order")
        names = ("x_in", "ctx_in", "order", "xn_ready", "turned", "xnT_ready",
                 "gates_ready", "gsb_ready", "f_ready", "abs_ready", "softplus", "stack_ready", "stackT_ready", "gT_ready",
                 "en_ready", "gb_ready", "d_ready", "dmask_ready", "qk_ready", "c_ready", "h_ready", "n_ready", "h_kept",
                 "score_ready", "col_ready", "sig_ready", "hid_ready", "hid_kept", "out_ready", "out_kept", "x_ready", "x_out")
        Ls = [{n: sem(f"B{u}_{n}") for n in names} for u in range(PAIR)]

        def take_indices(first_batch):
            for u in range(PAIR):
                nc.gpsimd.tensor_copy(idx8s[u][:, :], slot8[:, bass.ds((first_batch + u) * NT, NT), :].rearrange("p t k -> p (t k)"))\
                    .then_inc(idx_ready, 1)
            nc.gpsimd.wait_ge(idx_ready, PAIR)

        def gather(j, ks=range(TOPK)):
            t, u = divmod(j, PAIR)
            if j >= 2 and ks[0] == 0:
                nc.gpsimd.wait_ge(summed, j - 1)
            for k in ks:
                nc.gpsimd.indirect_dma_start(yg[j % 2][:, k, :], None, y_d[:, :],
                                             bass.IndirectOffsetOnAxis(idx8s[u][:, t * TOPK + k:t * TOPK + k + 1], 0),
                                             bounds_check=SLOTS - 1, oob_is_err=False).then_inc(y_in[j % 2], 16)

        def take_weights(link, first_batch):
            for u in range(PAIR):
                last = nc.vector.tensor_copy(w8s[u][:, :, :], weight8[:, bass.ds((first_batch + u) * NT, NT), :])
            link(last)

        def add_up(link, j, passes):
            t, u = divmod(j, PAIR)
            o = yaccs[u][:, t, :]
            nc.vector.wait_ge(y_in[j % 2], passes * (TILES // 2 * TOPK * 16) + (j // 2 + 1) * TOPK * 16)
            link(nc.vector.tensor_scalar(o, yg[j % 2][:, 0, :], w8s[u][:, t, 0:1], None, mult))
            for k in range(1, TOPK):
                last = nc.vector.scalar_tensor_tensor(out=o, in0=yg[j % 2][:, k, :], scalar=w8s[u][:, t, k:k + 1], in1=o,
                                                      op0=mult, op1=add)
                if k < TOPK - 1:
                    link(last)
            last.then_inc(summed, 1)

        with zeroed(since), nc.Block() as block:
            @block.gpsimd
            def _(pool):
                take_indices(0)
                for j in range(TILES):
                    gather(j)

            @block.vector
            def _(v):
                link = Chain(v, sum_order)
                for u in range(PAIR):
                    for h in range(H1):
                        o = 64 * (1 - h % 2)
                        nc.vector.memset(qHs[u][o:o + 64, h, :], 0.0)
                    nc.vector.memset(stacks[u][:, :], 0.0)
                    nc.vector.memset(vaugs[u][:, :, :, 64:65], 1.0)
                take_weights(link, 0)
                for j in range(TILES):
                    add_up(link, j, 0)

        with nc.Fori(0, B // PAIR) as pair, zeroed(since), nc.Block() as block:
            @block.sync
            def _(sp):
                for u in range(PAIR):
                    b, L = pair * PAIR + u, Ls[u]
                    sp.dma_start(xbs[u][:, :, :], x_d[b]).then_inc(L["x_in"], 16)
                    sp.dma_start(ctxbs[u][:, :, :], a["ctx"][b]).then_inc(L["ctx_in"], 16)
                    sp.dma_start(ctxTs[u][:, :, :], a["ctxT"][b]).then_inc(L["ctx_in"], 16)
                for u in range(PAIR):
                    sp.wait_ge(Ls[u]["x_ready"], 1)
                    sp.dma_start(x_d[pair * PAIR + u], xbs[u][:, :, :]).then_inc(Ls[u]["x_out"], 16)
                for u in range(PAIR):
                    sp.wait_ge(Ls[u]["x_out"], 16)

            @block.gpsimd
            def _(pool):
                def part(u):
                    for n in range(H1 * NT):
                        yield u * (LAG + 0.05) + MLSTM + n + 0.3
                        pool.wait_ge(Ls[u]["d_ready"], n + 1)
                        d = eTs[u][:, n % 4, n % NT * P:(n % NT + 1) * P]
                        nc.gpsimd.affine_select(out=d, in_=d, pattern=[[1, P]], compare_op=ALU.is_ge, fill=0.0, base=0,
                                                channel_multiplier=-1).then_inc(Ls[u]["dmask_ready"], 1)

                def next_rows():
                    yield 0
                    take_indices(pair * PAIR + PAIR)
                    for j in range(TILES // 2):
                        gather(j)
                    for n in range(H1 * NT):
                        yield MLSTM + n + 4.4
                        j, k = divmod(n * 2, TOPK)
                        gather(TILES // 2 + j, range(k, k + 2))

                side_by_side(part(0), part(1), next_rows())

            @block.tensor
            def _(pe):
                def part(u):
                    late, after = u * LAG, u * LAG_MIX
                    L, xn, xnT, ctxT, qH, vaug = Ls[u], xns[u], xnTs[u], ctxTs[u], qHs[u], vaugs[u]
                    bank = [ps[:, 4 * u + i, :] for i in range(4)]
                    cT = works[u][:, :].rearrange("p (i c s) -> p i c s", i=2, c=NT)
                    wide = works[u][:, :].rearrange("p (f s) -> p f s", f=FC1)
                    G_r = rowss[u][0:H1, 3 * S + 2:4 * S + 2]

                    def turn(k):
                        pe.wait_ge(L["xn_ready"], k + 1)
                        for c in range(DC):
                            for t in range(NT):
                                last = nc.tensor.transpose(bank[c][:, t * P:(t + 1) * P], xn[:, t, c * P:(c + 1) * P], ident)
                            last.then_inc(L["turned"], 1)

                    yield late
                    pe.wait_ge(L["ctx_in"], 32)
                    for n, c in enumerate(range(2 * DC)):
                        nc.tensor.matmul(bank[2][0:36, :], gw1[:, 2 + c, :], ctxT[:, c % DC, :], start=n == 0, stop=False)
                    yield late + TURN
                    turn(0)
                    yield late + GATES
                    pe.wait_ge(L["xnT_ready"], 4)
                    for h in range(H1):
                        last = nc.tensor.matmul(bank[2][0:36, :], gw1[:, h // 2, :], qH[:, h, :], start=False, stop=h == H1 - 1)
                    last.then_inc(L["gates_ready"], 1)
                    yield late + GATES + 1.6
                    pe.wait_ge(L["stack_ready"], 1)
                    for t in range(NT):
                        last = nc.tensor.transpose(bank[3][:, t * 36:(t + 1) * 36], stacks[u][:, t * P:(t + 1) * P], ident[0:36, 0:36])
                    last.then_inc(L["stackT_ready"], 1)
                    yield late + u * 0.05 + MLSTM
                    pe.wait_ge(L["gT_ready"], 1)

                    def product(h):
                        pe.wait_ge(L["c_ready"], NT * (h + 1))
                        if h:
                            pe.wait_ge(L["h_kept"], h)
                        for st in range(NT):
                            for tc in range(st + 1):
                                last = nc.tensor.matmul(bank[2][:, st * 65:(st + 1) * 65], cT[:, h % 2, tc, st * P:(st + 1) * P],
                                                        vaug[:, tc, h, 0:65], start=tc == 0, stop=tc == st)
                        last.then_inc(L["h_ready"], 1)

                    for h in range(H1):
                        yield late + u * 0.05 + MLSTM + NT * h
                        if h:
                            pe.wait_ge(L["d_ready"], NT * h)
                        nc.tensor.matmul(bank[3], minus1[:, h, :], G_r, start=True, stop=True).then_inc(L["gb_ready"], 1)
                        for tc in range(NT):
                            n = h * NT + tc
                            yield late + u * 0.05 + MLSTM + n + 0.1
                            if n >= 2:
                                pe.wait_ge(L["c_ready"], n - 1)
                            nc.tensor.matmul(bank[n % 2][:, tc * P:S], ctxT[:, h // 2, tc * P:(tc + 1) * P], qH[:, h, tc * P:S],
                                             start=True, stop=True).then_inc(L["qk_ready"], 1)
                            if h and tc == PRODUCT:
                                yield late + u * 0.05 + MLSTM + n + 0.15
                                product(h - 1)
                    yield late + u * 0.05 + MLSTM + H1 * NT + 0.2
                    product(H1 - 1)

                    yield after + MIX
                    turn(1)
                    yield after + MIX + 0.4
                    pe.wait_ge(L["h_kept"], H1)
                    pe.wait_ge(L["xnT_ready"], 6)
                    for c in range(DC):
                        last = nc.tensor.matmul(bank[2], wr1[:, c, :], xnT[:, c, :], start=c == 0, stop=c == DC - 1)
                    last.then_inc(L["score_ready"], 1)
                    for f in range(FC1):
                        yield after + MIX + 1 + f / 2
                        if f >= 2:
                            pe.wait_ge(L["hid_kept"], f - 1)
                        for c in range(DC):
                            last = nc.tensor.matmul(bank[f % 2], w11[:, c, f * P:(f + 1) * P], xnT[:, c, :],
                                                    start=c == 0, stop=c == DC - 1)
                        last.then_inc(L["hid_ready"], 1)
                    yield after + MIX + 5
                    pe.wait_ge(L["hid_kept"], FC1)
                    pe.wait_ge(L["col_ready"], 1)
                    for t in range(NT):
                        if t >= 2:
                            yield after + MIX + 5 + t
                            pe.wait_ge(L["out_kept"], t - 1)
                        for f in range(FC1):
                            last = nc.tensor.matmul(bank[2 + t % 2][:, 0:D], wide[:, f, t * P:(t + 1) * P], w21[:, f, :],
                                                    start=f == 0, stop=f == FC1 - 1)
                        last.then_inc(L["out_ready"], 1)

                side_by_side(part(0), part(1))

            @block.scalar
            def _(act):
                def part(u):
                    late, after = u * LAG, u * LAG_MIX
                    L, xnT, qH, eT, hb = Ls[u], xnTs[u], qHs[u], eTs[u], hbs[u]
                    bank = [ps[:, 4 * u + i, :] for i in range(4)]
                    wide = works[u][:, :].rearrange("p (f s) -> p f s", f=FC1)
                    gsb, f_r, a_r = rowss[u][0:36, 0:S], rowss[u][0:H1, S:2 * S], rowss[u][0:H1, 2 * S:3 * S]
                    gT = gTs[u]
                    yield late + TURN + 0.2
                    for c in range(DC):
                        act.wait_ge(L["turned"], c + 1)
                        for s in range(2):
                            r = slice(64 * s, 64 * s + 64)
                            nc.scalar.activation(qH[r, 2 * c + s, :], bank[c][r, :], ACT.Copy).then_inc(L["xnT_ready"], 1)
                    yield late + GATES + 0.4
                    act.wait_ge(L["gsb_ready"], 1)
                    nc.scalar.activation(f_r, gsb[32:36, :], ACT.Copy).then_inc(L["f_ready"], 1)
                    yield late + GATES + 0.8
                    act.wait_ge(L["abs_ready"], 1)
                    nc.scalar.activation(a_r, a_r, ACT.Exp, scale=-1.0).then_inc(L["softplus"], 1)
                    yield late + GATES + 1
                    act.wait_ge(L["softplus"], 1)
                    nc.scalar.activation(a_r, a_r, ACT.Ln, bias=1.0).then_inc(L["softplus"], 1)
                    yield late + GATES + 2
                    act.wait_ge(L["gT_ready"], 1)
                    nc.scalar.activation(ens[u][:, :, :], gT[:, :, 32:36], ACT.Exp, scale=-1.0).then_inc(L["en_ready"], 1)

                    def keep_head(h):
                        act.wait_ge(L["n_ready"], h + 1)
                        n4 = smalls[u][:, 4 * (h % 2):4 * (h % 2) + 4]
                        for t in range(NT):
                            last = nc.scalar.activation(hb[:, t, h, :], bank[2][:, t * 65:t * 65 + 64], ACT.Copy, scale=n4[:, t:t + 1])
                        last.then_inc(L["h_kept"], 1)

                    for n in range(H1 * NT):
                        h, tc = divmod(n, NT)
                        yield late + u * 0.05 + MLSTM + n + 0.2
                        act.wait_ge(L["gb_ready"], h + 1)
                        if n >= 4:
                            act.wait_ge(L["c_ready"], n - 3)
                        nc.scalar.activation(eT[:, n % 4, tc * P:S], bank[3][:, tc * P:S], ACT.Exp, bias=gT[:, tc, h:h + 1])\
                            .then_inc(L["d_ready"], 1)
                        if h and tc == KEEP_HEAD:
                            yield late + u * 0.05 + MLSTM + n + 0.7
                            keep_head(h - 1)
                    yield late + u * 0.05 + MLSTM + H1 * NT + 0.6
                    keep_head(H1 - 1)
                    yield after + MIX + 0.2
                    for c in range(DC):
                        act.wait_ge(L["turned"], DC + c + 1)
                        nc.scalar.activation(xnT[:, c, :], bank[c], ACT.Copy).then_inc(L["xnT_ready"], 1)
                    yield after + MIX + 0.8
                    act.wait_ge(L["col_ready"], 1)
                    nc.scalar.activation(smalls[u][:, 20:24], smalls[u][:, 8:12], ACT.Exp, scale=-1.0).then_inc(L["sig_ready"], 1)
                    for f in range(FC1):
                        yield after + MIX + 1.2 + f / 2
                        act.wait_ge(L["hid_ready"], f + 1)
                        nc.scalar.activation(wide[:, f, :], bank[f % 2], ACT.Gelu_apprx_tanh, bias=b11[:, f:f + 1])\
                            .then_inc(L["hid_kept"], 1)

                side_by_side(part(0), part(1))

            @block.vector
            def _(v):
                def part(u):
                    late, after = u * LAG, u * LAG_MIX
                    L, xb, xn, tmp, stats = Ls[u], xbs[u], xns[u], tmps[u], statss[u]
                    eT, vaug, hb, hn, en, gT, small = eTs[u], vaugs[u], hbs[u], hns[u], ens[u], gTs[u], smalls[u]
                    bank = [ps[:, 4 * u + i, :] for i in range(4)]
                    cT = works[u][:, :].rearrange("p (i c s) -> p i c s", i=2, c=NT)
                    rows, stack = rowss[u], stacks[u]
                    gsb, f_r, a_r = rows[0:36, 0:S], rows[0:H1, S:2 * S], rows[0:H1, 2 * S:3 * S]
                    G_r = rows[0:H1, 3 * S + 2:4 * S + 2]
                    cs_r = eT[0:H1, 0:2, :].rearrange("p a b -> p (a b)")[:, 0:S + 1]
                    link = Chain(v, L["order"])

                    yield 0
                    nc.vector.memset(cs_r[:, 0:1], 0.0)
                    nc.vector.memset(G_r, 1.0)
                    v.wait_ge(L["x_in"], 16)
                    for t in range(NT):
                        last = nc.vector.scalar_tensor_tensor(out=xb[:, t, :], in0=yaccs[u][:, t, :], scalar=gates[:, 4:5], in1=xb[:, t, :],
                                                              op0=mult, op1=add)
                    link(last)
                    for n, last in enumerate(layernorm_steps(nc, link, xb, xn, stats)):
                        yield late + 0.1 + n / 4 + u * 0
                    last.then_inc(L["xn_ready"], 1)

                    v.wait_ge(L["ctx_in"], 32)
                    nc.vector.tensor_copy(vaug[:, :, :, 0:64], ctxbs[u][:, :, :].rearrange("p c (h d) -> p c h d", h=H1))
                    yield late + GATES + 0.2
                    v.wait_ge(L["gates_ready"], 1)
                    nc.vector.tensor_scalar(gsb, bank[2][0:36, :], gb1[:, 0:1], None, add).then_inc(L["gsb_ready"], 1)
                    yield late + GATES + 0.6
                    v.wait_ge(L["f_ready"], 1)
                    nc.vector.scalar_tensor_tensor(out=a_r, in0=f_r, scalar=-1.0, in1=f_r, op0=mult, op1=ALU.max).then_inc(L["abs_ready"], 1)
                    yield late + GATES + 1.4
                    v.wait_ge(L["softplus"], 2)
                    link(nc.vector.scalar_tensor_tensor(out=f_r, in0=f_r, scalar=0.0, in1=a_r,
                                                        op0=ALU.min, op1=subtract))
                    link(nc.vector.tensor_tensor_scan(cs_r[:, 1:S + 1], G_r, f_r, 0.0, mult, add))
                    link(nc.vector.tensor_tensor(stack[0:H1, :], gsb[0:H1, :], cs_r[:, 0:S], subtract))
                    link(nc.vector.tensor_tensor_scan(G_r, stack[0:H1, :], stack[0:H1, :], -FMAX, ALU.max, ALU.max))
                    nc.vector.tensor_tensor(stack[32:36, :], cs_r[:, 1:S + 1], G_r, add).then_inc(L["stack_ready"], 1)
                    yield late + GATES + 1.8
                    v.wait_ge(L["stackT_ready"], 1)
                    nc.vector.tensor_copy(gT[:, :, :], bank[3][:, 0:NT * 36].rearrange("p (t k) -> p t k", t=NT)).then_inc(L["gT_ready"], 1)

                    def normaliser(h):
                        o = bank[2][:, 0:NT * 65].rearrange("p (t d) -> p t d", t=NT)
                        n4 = small[:, 4 * (h % 2):4 * (h % 2) + 4]
                        v.wait_ge(L["h_ready"], h + 1)
                        v.wait_ge(L["en_ready"], 1)
                        link(nc.vector.tensor_tensor(n4, o[:, :, 64], en[:, :, h], ALU.max))
                        link(nc.vector.scalar_tensor_tensor(out=n4, in0=o[:, :, 64], scalar=-1.0, in1=n4, op0=mult, op1=ALU.max))
                        link(nc.vector.tensor_scalar(n4, n4, 1e-8, None, add))
                        nc.vector.reciprocal(n4, n4).then_inc(L["n_ready"], 1)

                    for n in range(H1 * NT):
                        h, tc = divmod(n, NT)
                        yield late + u * 0.05 + MLSTM + n + 0.5
                        v.wait_ge(L["qk_ready"], n + 1)
                        v.wait_ge(L["dmask_ready"], n + 1)
                        if h >= 2:
                            v.wait_ge(L["h_ready"], h - 1)
                        nc.vector.scalar_tensor_tensor(out=cT[:, h % 2, tc, tc * P:S], in0=bank[n % 2][:, tc * P:S], scalar=DH1 ** -0.5,
                                                       in1=eT[:, n % 4, tc * P:S], op0=mult, op1=mult).then_inc(L["c_ready"], 1)
                        if tc == KEEP_HEAD and h:
                            yield late + u * 0.05 + MLSTM + n + 0.6
                            normaliser(h - 1)
                    yield late + u * 0.05 + MLSTM + H1 * NT + 0.4
                    normaliser(H1 - 1)
                    yield after + NORM
                    v.wait_ge(L["h_kept"], H1)
                    groups = [h.rearrange("p t h d -> p (t h) d") for h in (hb, hn)]
                    for n, last in enumerate(layernorm_steps(nc, link, *groups, stats, NT * H1)):
                        yield after + NORM + n / 4
                    link(last)
                    link(nc.vector.tensor_scalar(tmp[:, 1, :], outw1, 1.0, gates[:, 1:2], add, mult))
                    hrow = hn.rearrange("p t h d -> p t (h d)")
                    for t in range(NT):
                        last = nc.vector.tensor_tensor(hrow[:, t, :], hrow[:, t, :], tmp[:, 1, :], mult)
                    link(last)
                    link(nc.vector.tensor_tensor(xb[:, :, :], xb[:, :, :], hrow, add))
                    for n, last in enumerate(layernorm_steps(nc, link, xb, xn, stats)):
                        yield after + (NORM + MIX) / 2 + 0.25 * n
                    last.then_inc(L["xn_ready"], 1)

                    srow, one_row, sjunk = eT[:, 0, :], eT[:, 1, :], eT[:, 2, :]
                    col, c1, c2, sig = small[:, 8:12], small[:, 12:16], small[:, 16:20], small[:, 20:24]
                    yield after + MIX + 0.6
                    link(nc.vector.memset(one_row, 1.0))
                    v.wait_ge(L["score_ready"], 1)
                    link(nc.vector.tensor_copy(srow, bank[2]))
                    for t in range(NT):
                        last = nc.vector.tensor_tensor_reduce(out=sjunk[:, t * P:(t + 1) * P], in0=srow[:, t * P:(t + 1) * P], in1=ident, scale=1.0,
                                                              scalar=0.0, op0=mult, op1=add, accum_out=col[:, t:t + 1])
                    last.then_inc(L["col_ready"], 1)
                    v.wait_ge(L["col_ready"], 1)
                    for t in range(NT):
                        yield after + MIX + 1 + t
                        link(nc.vector.scalar_tensor_tensor(out=sjunk, in0=srow, scalar=col[:, t:t + 1], in1=one_row,
                                                            op0=ALU.is_gt, op1=mult, accum_out=c1[:, t:t + 1]))
                        last = nc.vector.scalar_tensor_tensor(out=sjunk, in0=srow, scalar=col[:, t:t + 1],
                                                              in1=earlier[:, 3 * P - t * P:3 * P - t * P + S], op0=ALU.is_equal,
                                                              op1=mult, accum_out=c2[:, t:t + 1])
                        link(last)
                    yield after + MIX + 5
                    link(nc.vector.tensor_tensor(c1, c1, c2, add))
                    v.wait_ge(L["sig_ready"], 1)
                    link(nc.vector.tensor_scalar(sig, sig, 1.0, None, add))
                    link(nc.vector.reciprocal(sig, sig))
                    link(nc.vector.scalar_tensor_tensor(out=sig, in0=c1, scalar=float(KEEP), in1=sig, op0=ALU.is_lt, op1=mult))
                    for t in range(NT):
                        yield after + MIX + 5.5 + t
                        v.wait_ge(L["out_ready"], t + 1)
                        o = tmp[:, t % 2, :]
                        nc.vector.tensor_tensor(o, bank[2 + t % 2][:, 0:D], b21, add).then_inc(L["out_kept"], 1)
                        v.wait_ge(L["out_kept"], t + 1)
                        link(nc.vector.scalar_tensor_tensor(out=o, in0=o, scalar=sig[:, t:t + 1], in1=xn[:, t, :], op0=mult, op1=add))
                        last = nc.vector.scalar_tensor_tensor(out=xb[:, t, :], in0=o, scalar=gates[:, 5:6], in1=xb[:, t, :],
                                                              op0=mult, op1=add)
                    last.then_inc(L["x_ready"], 1)

                def next_sums():
                    link = Chain(v, sum_order)
                    yield 1
                    take_weights(link, pair * PAIR + PAIR)
                    for j in range(TILES):
                        yield SUMS[j]
                        add_up(link, j, pair + 1)

                side_by_side(part(0), part(1), next_sums())


def layers2to3(nc, a, sem, every, zeroed, G, out):
    ps, ident, gates = (G[k] for k in ("ps", "ident", "gates"))
    xb, xn, xnT, ctxT, stats, tmp = (G[k] for k in ("xb", "xn", "xnT", "ctxT", "stats", "tmp"))
    least, sums, recip, x_d = (G[k] for k in ("least", "sums", "recip", "x_d"))
    bo2, bias3, wq3, scale3 = (G[k] for k in ("bo2", "bias3", "wq3", "scale3"))
    with ExitStack() as ctx:
        def keep(name, shape, dt=F32):
            return ctx.enter_context(nc.sbuf_tensor(name, shape, dt))

        ln2 = keep("ln2", [P, 4, DC])
        ln3 = keep("ln3", [P, 4, DC])
        wp1 = keep("wp1", [P, DC, NAV])
        bp1 = keep("bp1", [P, 1])
        wp2 = keep("wp2", [P, E2])
        bp2 = keep("bp2", [1, E2])
        wo2f = keep("wo2f", [P, DC, D])
        arena = keep("arena", [P, 40 * 256])
        wq2 = keep("wq2", [P, DC, INNER])
        wk2 = keep("wk2", [P, DC, P])
        wv2 = keep("wv2", [P, DC, DH2])
        xb2 = keep("xb2", [P, NT, D])
        xnT2 = keep("xnT2", [P, DC, S])
        cnT = keep("cnT", [P, DC, S])
        ctxb = keep("ctxb", [P, NT, D])
        qT = [keep(f"qT_{i}", [P, S]) for i in range(2)]
        kH = [[keep(f"kH_{i}{s}", [P, KEYS3]) for s in range(2)] for i in range(2)]
        vh = [keep(f"vh_{i}", [P, KEYS3 // P, P]) for i in range(2)]
        work = keep("work", [P, 2 * 8 * S])
        wide = keep("wide", [P, 8, S])
        pbuf = keep("pbuf", [P, 4, KEYS3])
        small = keep("small", [P, 64])
        we1 = work[:, 0:DC * FE2].rearrange("p (c f) -> p c f", c=DC)
        we2 = work[:, DC * FE2:DC * FE2 + FEC * D].rearrange("p (c f) -> p c f", c=FEC)
        be1 = keep("be1", [P, FEC])
        be2 = keep("be2", [P, DC])

        def cut(start, *shape):
            n = int(np.prod(shape))
            names = "bcd"[:len(shape)]
            v = arena[:, start:start + n]
            return v.rearrange(f"p (b c) -> p b c", b=shape[0]), start + n

        wo2, at = cut(0, HP, D)
        wff1, at = cut(at, DC, 2 * FF2)
        wff2, at = cut(at, FFC, D)
        assert at <= 40 * 256
        wqx, at = cut(0, DC, INNER)
        wkx, at = cut(at, DC, INNER)
        wvx, at = cut(at, DC, INNER)
        wox, at = cut(at, HP, D)
        keysT, at = cut(at, DC, KEYS3)
        assert at <= 40 * 256
        mask_u8 = keep("mask_u8", [P, S], mybir.dt.uint8)
        mask3 = keep("mask3", [P, KEYS3])
        xqT = keep("xqT", [P, DC, S], BF16)
        pick = keep("pick", [1, 8], U32)

        since = len(every)
        x_in, ctx_in, mask_in, arena_in, arena3_in, out_done = (
            sem(n + "_C") for n in ("x_in", "ctx_in", "mask_in", "arena_in", "arena3_in", "out_done"))
        order = sem("dve_orderC")
        const_in = sem("constC_in")
        loads = [(ln2[:, :, :], "L2_ln"), (wk2[:, :, :], "L2_wk"), (wv2[:, :, :], "L2_wv"), (wq2[:, :, :], "L2_wq"),
                 (ln3[:, :, :], "L3_ln"), (wp1[:, :, :], "L2_wp1"), (bp1[:, :], "L2_bp1"),
                 (wp2[:, :], "L2_wp2"), (bp2[:, :], "L2_bp2"), (wo2f[:, :, :], "L2_wof")]
        link = Chain(nc.vector, order)

        def pe_turn(src, turned):
            for c in range(DC):
                for t in range(NT):
                    last = nc.tensor.transpose(ps[:, c, t * P:(t + 1) * P], src[:, t, c * P:(c + 1) * P], ident)
                last.then_inc(turned, 1)

        N2 = {n: sem("N2_" + n) for n in ("xn_ready", "cn_ready", "ready", "kept")}

        def q_job(w, xT, g):
            def product(pe):
                for c in range(DC):
                    last = nc.tensor.matmul(ps[:, 7, :], w[:, c, g * P:(g + 1) * P], xT[:, c, :], start=c == 0, stop=c == DC - 1)
                return last

            return product, lambda v: nc.vector.tensor_scalar(qT[g % 2][:, :], ps[:, 7, :], -DH2 ** -0.5, None, mult)

        def k_job():
            def product(pe):
                for c in range(DC):
                    last = nc.tensor.matmul(ps[:, 7, :], wk2[:, c, :], cnT[:, c, :], start=c == 0, stop=c == DC - 1)
                return last

            def copy(v):
                for s in range(2):
                    r = slice(64 * s, 64 * s + 64)
                    last = nc.vector.tensor_copy(kH[0][s][r, 0:S], ps[r, 7, :])
                return last

            return product, copy

        def v_job():
            def product(pe):
                for t in range(NT):
                    for c in range(DC):
                        last = nc.tensor.matmul(ps[:, 7, t * DH2:(t + 1) * DH2], cnT[:, c, t * P:(t + 1) * P], wv2[:, c, :],
                                                start=c == 0, stop=c == DC - 1)
                return last

            return product, lambda v: nc.vector.tensor_copy(
                vh[0][:, 0:NT, 0:DH2], ps[:, 7, 0:NT * DH2].rearrange("p (t d) -> p t d", t=NT))

        def norm_jobs():
            def begin(v):
                v.wait_ge(x_in, 16)
                v.wait_ge(ctx_in, 16)

            def keep_x(c):
                return lambda v: nc.vector.tensor_scalar(xnT2[:, c, :], ps[:, 7, :], ln2[:, 0, c:c + 1], ln2[:, 1, c:c + 1], mult, add)

            def keep_ctx(c):
                def run(v):
                    nc.vector.tensor_copy(ctxT[:, c, :], ps[:, 7, :])
                    return nc.vector.tensor_scalar(cnT[:, c, :], ps[:, 7, :], ln2[:, 2, c:c + 1], ln2[:, 3, c:c + 1], mult, add)
                return run

            return [(None, begin)] + \
                on_vector(layernorm_steps(nc, link, xb2, xn, stats, twice=True), 11, N2["xn_ready"]) + \
                on_vector(layernorm_steps(nc, link, ctxb, ctxb, stats), 7, N2["cn_ready"]) + \
                [turn_job(nc, ps, ident, xn, c, N2["xn_ready"], keep_x(c)) for c in range(DC)] + \
                [turn_job(nc, ps, ident, ctxb, c, N2["cn_ready"], keep_ctx(c)) for c in range(DC)] + \
                [q_job(wq2, xnT2, 0), k_job(), v_job()]

        A = {n: sem("A2_" + n) for n in ("gate_ready", "silu_ready", "hT_ready", "out_ready")}
        hT2 = work[:, 0:FFC * S].rearrange("p (f s) -> p f s", f=FFC)

        att2 = attention(nc, sem, "a2", ps, ident, 2, HP, NT,
                         lambda g, s, qt: qT[g % 2][:, qt * P:(qt + 1) * P],
                         lambda g, s, kb: kH[0][s][:, 0:S],
                         lambda g, s, kc: vh[0][:, kc, 0:DH2], DH2, None,
                         ([pbuf[:, i // 2, (i % 2) * S:(i % 2 + 1) * S] for i in range(8)], sums, recip, least,
                          [work[:, i * 2 * NT * S:(i + 1) * 2 * NT * S].rearrange("p (s c q) -> p s c q", s=2, c=NT)
                           for i in range(2)]), wide,
                         jobs=lambda g: [q_job(wq2, xnT2, g)])

        R = {n: sem("R2_" + n) for n in ("xn_ready", "turned", "xnT_ready", "z_ready", "z_kept", "logit_ready", "picked", "we_in", "hid_ready", "hid_kept",
                                         "mid_ready", "mid_kept", "out_ready")}
        z, lrow, l8 = small[:, 32:33], small[0:1, 40:48], small[0:1, 48:56]
        LAST_FIRST = [NT - 1] + list(range(NT - 1))

        def r2_turn(n, tiles):
            nc.tensor.wait_ge(R["xn_ready"], n)
            for c in range(DC):
                for t in tiles:
                    last = nc.tensor.transpose(ps[:, c, t * P:(t + 1) * P], xn[:, t, c * P:(c + 1) * P], ident)
                last.then_inc(R["turned"], 1)

        def l2_tensor(pe, background={}):
            att2[0](pe, background)
            pe.wait_ge(arena_in, 48)
            for f in range(FFC):
                if f >= 2:
                    pe.wait_ge(A["hT_ready"], f - 1)
                for c in range(DC):
                    nc.tensor.matmul(ps[:, f % 2, :], wff1[:, c, FF2 + f * P:FF2 + (f + 1) * P], xnT2[:, c, :],
                                     start=c == 0, stop=c == DC - 1)
                for c in range(DC):
                    last = nc.tensor.matmul(ps[:, 2 + f % 2, :], wff1[:, c, f * P:(f + 1) * P], xnT2[:, c, :],
                                            start=c == 0, stop=c == DC - 1)
                last.then_inc(A["gate_ready"], 1)
            pe.wait_ge(att2[3], HP)
            pe.wait_ge(A["hT_ready"], FFC)
            for t in LAST_FIRST:
                for g in range(HP):
                    nc.tensor.matmul(ps[:, 4 + t, 0:D], wide[:, g, t * P:(t + 1) * P], wo2[:, g, :], start=g == 0, stop=False)
                for f in range(FFC):
                    last = nc.tensor.matmul(ps[:, 4 + t, 0:D], hT2[:, f, t * P:(t + 1) * P], wff2[:, f, :],
                                            start=False, stop=f == FFC - 1)
                last.then_inc(A["out_ready"], 1)
                if t == 0:
                    r2_turn(1, [NT - 1])
                if t == 1:
                    pe.wait_ge(R["xnT_ready"], DC)
                    for c in range(DC):
                        last = nc.tensor.matmul(ps[:, 2, 0:1], wp1[:, c, :], xnT[:, c, S - 1:S], start=c == 0, stop=c == DC - 1)
                    last.then_inc(R["z_ready"], 1)
            pe.wait_ge(R["z_kept"], 1)
            nc.tensor.matmul(ps[0:1, 3, 0:E2], z, wp2[:, :], start=True, stop=True).then_inc(R["logit_ready"], 1)

        def l2_scalar(act):
            att2[2](act)
            for f in range(FFC):
                act.wait_ge(A["gate_ready"], f + 1)
                if f >= 2:
                    act.wait_ge(A["hT_ready"], f - 1)
                nc.scalar.activation(pbuf[:, f % 2, 0:S], ps[:, f % 2, :], ACT.Silu).then_inc(A["silu_ready"], 1)

        def l2_vector(v, background={}):
            att2[1](v, background)
            for f in range(FFC):
                v.wait_ge(A["silu_ready"], f + 1)
                nc.vector.tensor_tensor(hT2[:, f, :], pbuf[:, f % 2, 0:S], ps[:, 2 + f % 2, :], mult).then_inc(A["hT_ready"], 1)
            if background:
                v.wait_ge(out_done, 16)
            for n, t in enumerate(LAST_FIRST):
                v.wait_ge(A["out_ready"], n + 1)
                link(nc.vector.scalar_tensor_tensor(out=xb[:, t, :], in0=ps[:, 4 + t, 0:D], scalar=gates[:, 2:3],
                                                    in1=xb2[:, t, :], op0=mult, op1=add))
                if n == 0:
                    layernorm(nc, link, xb[:, NT - 1:NT, :], xn[:, NT - 1:NT, :], stats, 1).then_inc(R["xn_ready"], 1)
            v.wait_ge(R["logit_ready"], 1)
            link(nc.vector.tensor_tensor(lrow, ps[0:1, 3, 0:E2], bp2[:, :], add))
            link(nc.vector.max(l8, lrow))
            nc.vector.max_index(pick[:, :], l8, lrow).then_inc(R["picked"], 1)

        def r2_tensor(pe):
            r2_turn(2, range(NT - 1))
            pe.wait_ge(R["xnT_ready"], 2 * DC)
            pe.wait_ge(R["we_in"], 64)
            for f in range(FEC):
                for c in range(DC):
                    last = nc.tensor.matmul(ps[:, 4 + f, :], we1[:, c, f * P:(f + 1) * P], xnT[:, c, :],
                                            start=c == 0, stop=c == DC - 1)
                last.then_inc(R["hid_ready"], 1)
            for h in range(DC):
                for f in range(FEC):
                    if h == 0:
                        pe.wait_ge(R["hid_kept"], f + 1)
                    last = nc.tensor.matmul(ps[:, h, :], we2[:, f, h * P:(h + 1) * P], wide[:, f, :],
                                            start=f == 0, stop=f == FEC - 1)
                last.then_inc(R["mid_ready"], 1)
            pe.wait_ge(R["mid_kept"], DC)
            for t in range(NT):
                for h in range(DC):
                    last = nc.tensor.matmul(ps[:, 2 + t, 0:D], wide[:, FEC + h, t * P:(t + 1) * P], wo2f[:, h, :],
                                            start=h == 0, stop=h == DC - 1)
                last.then_inc(R["out_ready"], 1)

        def r2_scalar(act):
            def keep_turned(n, columns):
                for c in range(DC):
                    act.wait_ge(R["turned"], n * DC + c + 1)
                    nc.scalar.activation(xnT[:, c, columns], ps[:, c, columns], ACT.Copy).then_inc(R["xnT_ready"], 1)

            keep_turned(0, slice(S - P, S))
            act.wait_ge(R["z_ready"], 1)
            nc.scalar.activation(z, ps[:, 2, 0:1], ACT.Gelu, bias=bp1[:, 0:1]).then_inc(R["z_kept"], 1)
            keep_turned(1, slice(0, S - P))
            act.wait_ge(R["we_in"], 64)
            for f in range(FEC):
                act.wait_ge(R["hid_ready"], f + 1)
                nc.scalar.activation(wide[:, f, :], ps[:, 4 + f, :], ACT.Gelu, bias=be1[:, f:f + 1]).then_inc(R["hid_kept"], 1)

        def r2_vector(v):
            layernorm(nc, link, xb[:, 0:NT - 1, :], xn[:, 0:NT - 1, :], stats, NT - 1).then_inc(R["xn_ready"], 1)
            v.wait_ge(R["we_in"], 64)
            for h in range(DC):
                v.wait_ge(R["mid_ready"], h + 1)
                nc.vector.tensor_scalar(wide[:, FEC + h, :], ps[:, h, :], be2[:, h:h + 1], None, add).then_inc(R["mid_kept"], 1)
            for t in range(NT):
                v.wait_ge(R["out_ready"], t + 1)
                o = tmp[:, t % 2, :]
                link(nc.vector.tensor_tensor(o, ps[:, 2 + t, 0:D], bo2, add))
                link(nc.vector.scalar_tensor_tensor(out=o, in0=o, scalar=0.3, in1=xn[:, t, :], op0=mult, op1=add))
                last = nc.vector.scalar_tensor_tensor(out=xb[:, t, :], in0=o, scalar=gates[:, 6:7], in1=xb[:, t, :],
                                                      op0=mult, op1=add)
            link(last)

        M = {n: sem("A3_" + n) for n in ("mask_ready", "xn_ready", "turned", "keys_ready", "first_ready", "first_kept", "out_ready", "x_ready")}
        latT = keysT[:, :, S:KEYS3]

        def q_product(g, bank):
            for c in range(DC):
                last = nc.tensor.matmul(ps[:, bank, :], wqx[:, c, g * P:(g + 1) * P], latT[:, c, :], start=c == 0, stop=c == DC - 1)
            return last

        def key_product(g, kb, bank):
            for c in range(DC):
                last = nc.tensor.matmul(ps[:, bank, :], wkx[:, c, g * P:(g + 1) * P], keysT[:, c, kb * BANK:(kb + 1) * BANK],
                                        start=c == 0, stop=c == DC - 1)
            return last

        def value_product(g, kb, bank):
            for i in range(4):
                tok = slice((4 * kb + i) * P, (4 * kb + i + 1) * P)
                for c in range(DC):
                    last = nc.tensor.matmul(ps[:, bank, i * P:(i + 1) * P], keysT[:, c, tok], wvx[:, c, g * P:(g + 1) * P],
                                            start=c == 0, stop=c == DC - 1)
            return last

        def by_token(bank):
            return ps[:, bank, :].rearrange("p (i d) -> p i d", i=4)

        def jobs3(g):
            def keys(kb):
                def copy(v):
                    for s in range(2):
                        r = slice(64 * s, 64 * s + 64)
                        last = nc.vector.tensor_copy(kH[g % 2][s][r, kb * BANK:(kb + 1) * BANK], ps[r, 7, :])
                    return last

                return lambda pe: key_product(g, kb, 7), copy

            def vals(kb):
                return (lambda pe: value_product(g, kb, 7),
                        lambda v: nc.vector.tensor_copy(vh[g % 2][:, 4 * kb:4 * kb + 4, :], by_token(7)))

            return [q_job(wqx, latT, g), keys(0), keys(1), vals(0), vals(1)]

        firsts = [(2, lambda bank: key_product(0, 0, bank), "keys", 0), (3, lambda bank: value_product(0, 0, bank), "values", 0),
                  (4, lambda bank: q_product(0, bank), "queries", 0), (5, lambda bank: key_product(0, 1, bank), "keys", 1),
                  (6, lambda bank: value_product(0, 1, bank), "values", 1)]

        def keep_first(bank, product, kind, kb):
            if kind == "keys":
                for s in range(2):
                    r = slice(64 * s, 64 * s + 64)
                    last = nc.scalar.activation(kH[0][s][r, kb * BANK:(kb + 1) * BANK], ps[r, bank, :], ACT.Copy)
                return last
            if kind == "values":
                return nc.scalar.activation(vh[0][:, 4 * kb:4 * kb + 4, :], by_token(bank), ACT.Copy)
            return nc.scalar.activation(qT[0][:, :], ps[:, bank, :], ACT.Copy, scale=-DH2 ** -0.5)

        att3 = attention(nc, sem, "a3", ps, ident, 2, HP, KEYS3 // P,
                         lambda g, s, qt: qT[g % 2][:, qt * P:(qt + 1) * P],
                         lambda g, s, kb: kH[g % 2][s][:, kb * BANK:(kb + 1) * BANK],
                         lambda g, s, kc: vh[g % 2][:, kc, s * DH2:(s + 1) * DH2], DH2, mask3[:, :],
                         ([pbuf[:, i, :] for i in range(4)], sums, recip, least,
                          [work[:, :].rearrange("p (s c q) -> p s c q", s=2, c=KEYS3 // P)]), wide,
                         jobs=jobs3)

        def l3_tensor(pe, background={}):
            def project(first):
                first[1](first[0]).then_inc(M["first_ready"], 1)

            pe.wait_ge(M["keys_ready"], DC)
            for first in firsts[:2]:
                project(first)
            pe.wait_ge(M["xn_ready"], 1)
            pe_turn(xn, M["turned"])
            pe.wait_ge(M["keys_ready"], 2 * DC)
            for first in firsts[2:]:
                project(first)
            pe.wait_ge(M["first_kept"], len(firsts))
            att3[0](pe, background)
            pe.wait_ge(att3[3], HP)
            for t in range(NT):
                for g in range(HP):
                    last = nc.tensor.matmul(ps[:, t, 0:D], wide[:, g, t * P:(t + 1) * P], wox[:, g, :], start=g == 0, stop=g == HP - 1)
                last.then_inc(M["out_ready"], 1)

        def l3_scalar(act):
            for c in range(DC):
                nc.scalar.activation(keysT[:, c, 0:S], ctxT[:, c, :], ACT.Identity, bias=ln3[:, 1, c:c + 1],
                                     scale=ln3[:, 0, c:c + 1]).then_inc(M["keys_ready"], 1)
            for n, first in enumerate(firsts):
                if n == 2:
                    for c in range(DC):
                        act.wait_ge(M["turned"], c + 1)
                        nc.scalar.activation(latT[:, c, :], ps[:, c, :], ACT.Identity, bias=ln3[:, 3, c:c + 1],
                                             scale=ln3[:, 2, c:c + 1]).then_inc(M["keys_ready"], 1)
                act.wait_ge(M["first_ready"], n + 1)
                keep_first(*first).then_inc(M["first_kept"], 1)
            att3[2](act)

        def l3_vector(v, background={}):
            layernorm(nc, link, xb, xn, stats, twice=True).then_inc(M["xn_ready"], 1)
            nc.vector.tensor_scalar(mask3[:, 0:S], mask_u8[:, :], 0.0, FMAX, ALU.is_equal, mult).then_inc(M["mask_ready"], 1)
            nc.vector.memset(mask3[:, S:KEYS3], 0.0).then_inc(M["mask_ready"], 1)
            v.wait_ge(M["mask_ready"], 2)
            v.wait_ge(M["turned"], DC)
            att3[1](v, background)
            for t in range(NT):
                v.wait_ge(M["out_ready"], t + 1)
                last = nc.vector.scalar_tensor_tensor(out=xb[:, t, :], in0=ps[:, t, 0:D], scalar=gates[:, 3:4],
                                                      in1=xb[:, t, :], op0=mult, op1=add)
            last.then_inc(M["x_ready"], 1)
            v.wait_ge(M["x_ready"], 1)

        Q = {n: sem("Q3_" + n) for n in ("xn_ready", "xq_ready", "x_ready", "ready", "kept")}
        amax, xscale = small[:, 0:4], small[:, 4:8]

        def quantise_rows():
            nc.vector.wait_ge(Q["xn_ready"], 1)
            yield from quantise(nc, link, xn[:, :, :], NT, amax, xscale)

        def linear_jobs():
            def keep_x(c):
                return lambda v: nc.vector.tensor_copy(xqT[:, c, :], ps[:, 7, :])

            def linear(half):
                def product(pe):
                    for t in (2 * half, 2 * half + 1):
                        for c in range(DC):
                            last = nc.tensor.matmul(ps[:, 7, t % 2 * D:(t % 2 + 1) * D], xqT[:, c, t * P:(t + 1) * P], wq3[:, c, :],
                                                    start=c == 0, stop=c == DC - 1)
                    return last

                def scaled(v):
                    for t in (2 * half, 2 * half + 1):
                        last = nc.vector.scalar_tensor_tensor(out=tmp[:, t % 2, :], in0=ps[:, 7, t % 2 * D:(t % 2 + 1) * D],
                                                              scalar=xscale[:, t:t + 1], in1=scale3[:, :], op0=mult, op1=mult)
                        if t % 2 == 0:
                            link(last)
                    return last

                def residual(v):
                    for t in (2 * half, 2 * half + 1):
                        link(nc.vector.tensor_tensor(tmp[:, t % 2, :], tmp[:, t % 2, :], bias3, add))
                    for t in (2 * half, 2 * half + 1):
                        last = nc.vector.scalar_tensor_tensor(out=xb[:, t, :], in0=tmp[:, t % 2, :], scalar=gates[:, 7:8],
                                                              in1=xb[:, t, :], op0=mult, op1=add)
                    last.then_inc(Q["x_ready"], 1)
                    v.wait_ge(Q["x_ready"], half + 1)

                return [(product, scaled), (None, residual)]

            return on_vector(layernorm_steps(nc, link, xb, xn, stats), 7, Q["xn_ready"]) + \
                on_vector(quantise_rows(), 6, Q["xq_ready"]) + \
                [turn_job(nc, ps, ident, xn, c, Q["xq_ready"], keep_x(c)) for c in range(DC)] + linear(0) + linear(1)

        def load_l2(sp):
            for dst, n in ((wo2, "L2_wo"), (wff1, "L2_wff1"), (wff2, "L2_wff2")):
                sp.dma_start(dst, a[n]).then_inc(arena_in, 16)

        def load_next(sp, b):
            sp.dma_start(xb2[:, :, :], x_d[b]).then_inc(x_in, 16)
            sp.dma_start(ctxb[:, :, :], a["ctx"][b]).then_inc(ctx_in, 16)

        def load_l3(sp, b):
            sp.wait_ge(R["picked"], 1)
            e = sp.value_load(pick[0:1, 0:1], min_val=0, max_val=E2 - 1)
            for dst, n in ((we1, "L2_we1"), (be1[:, :], "L2_be1"), (we2, "L2_we2"), (be2[:, :], "L2_be2")):
                sp.dma_start(dst, a[n][e]).then_inc(R["we_in"], 16)
            sp.dma_start(mask_u8[:, :], a["mask3"][b].partition_broadcast(P)).then_inc(mask_in, 16)
            for dst, n in ((wqx, "L3_wq"), (wkx, "L3_wk"), (wvx, "L3_wv"), (wox, "L3_wo")):
                sp.dma_start(dst, a[n]).then_inc(arena3_in, 16)
            sp.wait_ge(mask_in, 16)
            sp.wait_ge(arena3_in, 64)

        def store(sp, b):
            sp.wait_ge(Q["x_ready"], 2)
            sp.dma_start(out[b], xb[:, :, :]).then_inc(out_done, 16)
            sp.wait_ge(out_done, 16)

        link.n = 0
        jobs = norm_jobs()
        x_norm, ctx_norm, x_turns, ctx_turns, projections = (jobs[i:j] for i, j in ((1, 12), (12, 19), (19, 21), (21, 23), (23, 26)))
        alone = run_jobs(jobs[0:1] + ctx_norm + [(None, lambda v: v.wait_ge(const_in, 16 * len(loads)))] +
                         ctx_turns[0:1] + x_norm[0:4] + ctx_turns[1:2] + x_norm[4:7] + projections[1:2] + x_norm[7:10] +
                         projections[2:3] + x_norm[10:11] + x_turns + projections[0:1], N2["ready"], N2["kept"])
        with zeroed(since), nc.Block() as block:
            @block.sync
            def _(sp):
                load_next(sp, 0)
                for dst, n in loads:
                    sp.dma_start(dst, a[n]).then_inc(const_in, 16)
                load_l2(sp)
                load_l3(sp, 0)

            @block.tensor
            def _(pe):
                alone[0](pe)
                pe.wait_ge(N2["kept"], 2 * DC + 3)
                l2_tensor(pe)
                r2_tensor(pe)

            @block.scalar
            def _(act):
                l2_scalar(act)
                r2_scalar(act)

            @block.vector
            def _(v):
                for i in range(2):
                    nc.vector.memset(kH[i][0][64:P, :], 0.0)
                    link(nc.vector.memset(kH[i][1][0:64, :], 0.0))
                alone[1](v)
                l2_vector(v)
                r2_vector(v)

        link.n = 0
        norm_steps = [n for n in range(0, 7 * 8) if n % 8 >= 5][-19:] + [56, 57, 58, 59, 60, 61, 62]
        linear_steps = range(3, 60, 3)

        norms = spread(norm_steps, norm_jobs())
        linear = spread(linear_steps, linear_jobs())
        with nc.Fori(0, B - 1) as b, zeroed(since), nc.Block() as block:
            @block.sync
            def _(sp):
                load_next(sp, b + 1)
                sp.wait_ge(M["out_ready"], NT)
                load_l2(sp)
                store(sp, b)
                load_l3(sp, b + 1)

            @block.tensor
            def _(pe):
                l3_tensor(pe, norms)
                pe.wait_ge(att3[4], att3[5](norms)[2])
                pe.wait_ge(M["x_ready"], 1)
                l2_tensor(pe, linear)
                r2_tensor(pe)

            @block.scalar
            def _(act):
                l3_scalar(act)
                l2_scalar(act)
                r2_scalar(act)

            @block.vector
            def _(v):
                l3_vector(v, norms)
                l2_vector(v, linear)
                r2_vector(v)

        link.n = 0
        rest = run_jobs(linear_jobs(), Q["ready"], Q["kept"])
        with nc.Block() as block:
            @block.sync
            def _(sp):
                store(sp, B - 1)

            @block.tensor
            def _(pe):
                l3_tensor(pe)
                rest[0](pe)

            @block.scalar
            def _(act):
                l3_scalar(act)

            @block.vector
            def _(v):
                l3_vector(v)
                rest[1](v)


def kernel(**inputs):
    import numpy as _np
    import concourse.bacc as _bacc
    from concourse import mybir as _mybir
    from concourse.bass_utils import run_bass_kernel_spmd as _run

    i = {k: _np.asarray(v) for k, v in inputs.items()}

    def rows(w):
        return w.reshape(-1, P, w.shape[1]).transpose(1, 0, 2)

    def cols(v):
        return v.reshape(-1, P).T

    def tiles(x):
        return x.reshape(B, NT, P, D).transpose(0, 2, 1, 3)

    def heads_padded(w):
        z = _np.zeros((H0, HPAD) + w.shape[1:], w.dtype)
        z[:, :DK0] = w.reshape((H0, DK0) + w.shape[1:])
        return z.reshape((H0 * HPAD,) + w.shape[1:])

    consts = _np.zeros((P, 4, P), _np.float32)
    consts[:, 0] = _np.eye(P)
    consts[:, 1] = _np.triu(_np.ones((P, P)), 1)
    consts[:, 2] = 1
    e = _np.arange(E)
    consts[:, 3, :E] = (e % 2) * CAP * PAIRS + e // 2 + 1
    minus1 = _np.zeros((H1, H1, P), _np.float32)
    for h in range(H1):
        minus1[h, h] = -1
    gw1 = _np.zeros((3 * D, 36), _np.float32)
    gw1[:, 0:H1] = i["L1_xattn_igate_w"].T
    gw1[:, 32:36] = i["L1_xattn_fgate_w"].T
    gb1 = _np.zeros((36, 1), _np.float32)
    gb1[0:H1, 0] = i["L1_xattn_igate_b"]
    gb1[32:36, 0] = i["L1_xattn_fgate_b"]
    w_gate, w_up = (i["L0_ffn_" + n].reshape(PAIRS, 2, INTER, DC, P).transpose(0, 4, 3, 1, 2) for n in ("w_gate", "w_up"))
    wkv2, wkv3 = i["L2_xattn_Wkv"], i["L3_xattn_Wkv"]
    arrays = {
        "consts": consts,
        "gates": _np.concatenate([i["g_xattn"], i["g_ffn"]]),
        "vec": _np.stack([i["L0_xattn_bo"], i["L1_xattn_out_w"], i["L1_ffn_b2"], i["L2_ffn_bo"], i["L3_ffn_bias"]]),
        "block16": _np.repeat(_np.eye(P // DK0, dtype=_np.float32), DK0, axis=0),
        "token": _np.arange(S, dtype=_np.float32).reshape(NT, P).T,
        "minus1": minus1,
        "earlier": (_np.arange(7 * P)[None] < 3 * P + _np.arange(P)[:, None]).astype(_np.float32),
        "x": tiles(i["x"]),
        "ctx": tiles(i["ctx_1024"]),
        "ctxT": i["ctx_1024"].transpose(0, 2, 1).reshape(B, DC, P, S).transpose(0, 2, 1, 3),
        "mask0": i["mask_BxS2_if1"],
        "mask3": i["mask_BxS2_bk0"],
        "L0_wq": rows(i["L0_xattn_Wq"].T),
        "L0_wk": rows(i["L0_xattn_Wk"].T),
        "L0_wv": rows(heads_padded(i["L0_xattn_Wv"]).T),
        "L0_wo": rows(heads_padded(i["L0_xattn_Wo"].T)),
        "L0_bqk": _np.stack([cols(i["L0_xattn_bq"]), cols(i["L0_xattn_bk"])], axis=1),
        "L0_bv": heads_padded(i["L0_xattn_bv"]),
        "L0_gate": rows(i["L0_ffn_gate_w"].T),
        "L0_wgu": _np.concatenate([w_gate, w_up], axis=4),
        "L0_wd": i["L0_ffn_w_down"].reshape(PAIRS, 2, D, 2, IH).transpose(0, 4, 3, 1, 2),
        "L1_gw": rows(gw1),
        "L1_gb": gb1,
        "L1_wr": _np.repeat(cols(i["L1_ffn_w_router"])[:, :, None], P, axis=2),
        "L1_w1": rows(i["L1_ffn_W1"]),
        "L1_b1": cols(i["L1_ffn_b1"]),
        "L1_w2": rows(i["L1_ffn_W2"]),
        "L2_ln": _np.stack([cols(i["L2_xattn_" + n]) for n in ("ln_g", "ln_b", "cln_g", "cln_b")], axis=1),
        "L2_wq": rows(i["L2_xattn_Wq"]),
        "L2_wk": rows(_np.concatenate([wkv2[:, :DH2], wkv2[:, :DH2]], axis=1)),
        "L2_wv": rows(wkv2[:, DH2:]),
        "L2_wo": rows(i["L2_xattn_Wo"]),
        "L2_wff1": rows(i["L2_xattn_Wff1"]),
        "L2_wff2": rows(i["L2_xattn_Wff2"]),
        "L2_wp1": rows(i["L2_ffn_Wp1"]),
        "L2_bp1": cols(i["L2_ffn_bp1"]),
        "L2_wp2": i["L2_ffn_Wp2"],
        "L2_bp2": i["L2_ffn_bp2"][None],
        "L2_we1": i["L2_ffn_W1"].reshape(E2, DC, P, FE2).transpose(0, 2, 1, 3),
        "L2_be1": i["L2_ffn_b1"].reshape(E2, FEC, P).transpose(0, 2, 1),
        "L2_we2": i["L2_ffn_W2"].reshape(E2, FEC, P, D).transpose(0, 2, 1, 3),
        "L2_be2": i["L2_ffn_b2"].reshape(E2, DC, P).transpose(0, 2, 1),
        "L2_wof": rows(i["L2_ffn_Wo"]),
        "L3_ln": _np.stack([cols(i["L3_xattn_" + n]) for n in ("g1", "b1", "g2", "b2")], axis=1),
        "L3_wq": rows(i["L3_xattn_Wq"]),
        "L3_wk": rows(wkv3[:, :INNER]),
        "L3_wv": rows(wkv3[:, INNER:]),
        "L3_wo": rows(i["L3_xattn_Wout"]),
        "L3_w": i["L3_ffn_weight"].reshape(DC, P, D).transpose(1, 0, 2),
    }
    nc = _bacc.Bacc("TRN2", target_bir_lowering=False, num_devices=1)
    feed, aps = {}, {}
    for name, arr in arrays.items():
        arr = _np.ascontiguousarray(arr)
        feed[f"in_{name}"] = arr
        aps[name] = nc.dram_tensor(f"in_{name}", arr.shape, _mybir.dt.from_np(arr.dtype), kind="ExternalInput").ap()
    out = nc.dram_tensor("out_0", (B, P, NT, D), F32, kind="ExternalOutput").ap()
    program(nc, aps, out)
    r = _run(nc, [feed], core_ids=[0])
    return r.results[0]["out_0"].reshape(B, P, NT, D).transpose(0, 2, 1, 3).reshape(B, S, D)
```
